# Optimizing a Trainium2 kernel written in Bass

```python
import numpy as np
import jax
import jax.numpy as jnp

def _softmax(x, axis=-1):
    return jax.nn.softmax(x, axis=axis)

def _gelu(x):
    return jax.nn.gelu(x, approximate=True)

def _silu(x):
    return jax.nn.silu(x)

def _sigmoid(x):
    return jax.nn.sigmoid(x)

def _layernorm(x, axis=-1, eps=1e-05):
    m = jnp.mean(x, axis=axis, keepdims=True)
    v = jnp.var(x, axis=axis, keepdims=True)
    return (x - m) / jnp.sqrt(v + eps)

def _scatter_add(tgt, idx, src, axis=0):
    return tgt.at[idx].add(src)

def _segment_sum(src, seg, n):
    return jax.ops.segment_sum(src, seg, n)
kernel_name = 'mk_prb_d1_jaxref_r4_d6b382'

def setup_inputs(seed: int=0):
    np.random.seed(seed)
    _w = jnp.asarray

    def _L0_attn_setup():
        import jax, jax.numpy as jnp
        from jax import lax
        import numpy as np
        D_MODEL = 256
        E = 2 * D_MODEL
        N = 16
        D_CONV = 4
        DT_RANK = D_MODEL // 16
        B_SZ, L = (4, 512)

        def _mamba_params(key, scale=0.02):
            ks = jax.random.split(key, 7)
            return dict(in_w=jax.random.normal(ks[0], (D_MODEL, 2 * E), jnp.float32) * scale, conv_w=jax.random.normal(ks[1], (E, D_CONV), jnp.float32) * scale, conv_b=jnp.zeros((E,), jnp.float32), xproj_w=jax.random.normal(ks[2], (E, DT_RANK + 2 * N), jnp.float32) * scale, dt_w=jax.random.normal(ks[3], (DT_RANK, E), jnp.float32) * scale, dt_b=jax.random.normal(ks[4], (E,), jnp.float32) * 0.01, A_log=jnp.log(jnp.broadcast_to(jnp.arange(1, N + 1, dtype=jnp.float32), (E, N))), Dp=jnp.ones((E,), jnp.float32), out_w=jax.random.normal(ks[5], (E, D_MODEL), jnp.float32) * scale)

        def _mamba(x, in_w, conv_w, conv_b, xproj_w, dt_w, dt_b, A_log, Dp, out_w):
            xz = x @ in_w
            xi, z = jnp.split(xz, 2, axis=-1)
            xc = jnp.transpose(xi, (0, 2, 1))
            xc = lax.conv_general_dilated(xc, conv_w[:, None, :], (1,), [(D_CONV - 1, 0)], feature_group_count=E)
            xi = jax.nn.silu(jnp.transpose(xc + conv_b[None, :, None], (0, 2, 1)))
            proj = xi @ xproj_w
            dt, Bm, Cm = jnp.split(proj, [DT_RANK, DT_RANK + N], axis=-1)
            delta = jax.nn.softplus(dt @ dt_w + dt_b)
            A = -jnp.exp(A_log)

            def step(h, inp):
                d_t, b_t, c_t, u_t = inp
                h = jnp.exp(d_t[..., None] * A) * h + (d_t * u_t)[..., None] * b_t[:, None, :]
                y = jnp.einsum('ben,bn->be', h, c_t)
                return (h, y)
            h0 = jnp.zeros((x.shape[0], E, N), x.dtype)
            xs = (jnp.moveaxis(delta, 1, 0), jnp.moveaxis(Bm, 1, 0), jnp.moveaxis(Cm, 1, 0), jnp.moveaxis(xi, 1, 0))
            _, ys = lax.scan(step, h0, xs)
            y = jnp.moveaxis(ys, 0, 1) + xi * Dp
            y = y * jax.nn.silu(z)
            return y @ out_w
        key = jax.random.key(seed)
        kx, kf, kb = jax.random.split(key, 3)
        inp = {'x': jax.random.normal(kx, (B_SZ, L, D_MODEL), jnp.float32)}
        for pref, k in (('fwd_', kf), ('bwd_', kb)):
            for name, v in _mamba_params(k).items():
                inp[pref + name] = v
        return inp
    _L0_attn_in = _L0_attn_setup()

    def _L0_ffn_setup():
        import math
        import jax, jax.numpy as jnp
        import numpy as np
        D_MODEL = 256
        D_FF = 1024
        E = 8
        K = 2
        CAP_FACTOR = 1.25
        CLAMP = 10000.0
        LN_EPS = 1e-05
        B, S = (2, 512)
        key = jax.random.key(seed)
        ks = jax.random.split(key, 6)
        b12 = math.sqrt(6.0 / (D_MODEL + 2 * D_FF))
        b3 = math.sqrt(6.0 / (D_FF + D_MODEL))
        br = 0.02 * math.sqrt(3.0)
        return {'x': jax.random.normal(ks[0], (B, S, D_MODEL), dtype=jnp.float32), 'ln_gamma': jnp.ones((D_MODEL,), jnp.float32), 'ln_beta': jnp.zeros((D_MODEL,), jnp.float32), 'router_w': jax.random.uniform(ks[1], (E, D_MODEL), jnp.float32, -br, br), 'w12': jax.random.uniform(ks[2], (E, 2 * D_FF, D_MODEL), jnp.float32, -b12, b12), 'w3': jax.random.uniform(ks[3], (E, D_MODEL, D_FF), jnp.float32, -b3, b3)}
    _L0_ffn_in = _L0_ffn_setup()
    _d = {'L0_attn_x': _L0_attn_in['x'], 'L0_attn_fwd_in_w': _L0_attn_in['fwd_in_w'], 'L0_attn_fwd_conv_w': _L0_attn_in['fwd_conv_w'], 'L0_attn_fwd_conv_b': _L0_attn_in['fwd_conv_b'], 'L0_attn_fwd_xproj_w': _L0_attn_in['fwd_xproj_w'], 'L0_attn_fwd_dt_w': _L0_attn_in['fwd_dt_w'], 'L0_attn_fwd_dt_b': _L0_attn_in['fwd_dt_b'], 'L0_attn_fwd_A_log': _L0_attn_in['fwd_A_log'], 'L0_attn_fwd_Dp': _L0_attn_in['fwd_Dp'], 'L0_attn_fwd_out_w': _L0_attn_in['fwd_out_w'], 'L0_attn_bwd_in_w': _L0_attn_in['bwd_in_w'], 'L0_attn_bwd_conv_w': _L0_attn_in['bwd_conv_w'], 'L0_attn_bwd_conv_b': _L0_attn_in['bwd_conv_b'], 'L0_attn_bwd_xproj_w': _L0_attn_in['bwd_xproj_w'], 'L0_attn_bwd_dt_w': _L0_attn_in['bwd_dt_w'], 'L0_attn_bwd_dt_b': _L0_attn_in['bwd_dt_b'], 'L0_attn_bwd_A_log': _L0_attn_in['bwd_A_log'], 'L0_attn_bwd_Dp': _L0_attn_in['bwd_Dp'], 'L0_attn_bwd_out_w': _L0_attn_in['bwd_out_w'], 'L0_ffn_ln_gamma': _L0_ffn_in['ln_gamma'], 'L0_ffn_ln_beta': _L0_ffn_in['ln_beta'], 'L0_ffn_router_w': _L0_ffn_in['router_w'], 'L0_ffn_w12': _L0_ffn_in['w12'], 'L0_ffn_w3': _L0_ffn_in['w3']}
    _x0 = _d['L0_attn_x']
    _d['L0_attn_x'] = jax.random.normal(jax.random.fold_in(jax.random.key(seed), 1), (4, 1024, 256), dtype=_x0.dtype)
    del _x0
    return _d

def reference(L0_attn_x, L0_attn_fwd_in_w, L0_attn_fwd_conv_w, L0_attn_fwd_conv_b, L0_attn_fwd_xproj_w, L0_attn_fwd_dt_w, L0_attn_fwd_dt_b, L0_attn_fwd_A_log, L0_attn_fwd_Dp, L0_attn_fwd_out_w, L0_attn_bwd_in_w, L0_attn_bwd_conv_w, L0_attn_bwd_conv_b, L0_attn_bwd_xproj_w, L0_attn_bwd_dt_w, L0_attn_bwd_dt_b, L0_attn_bwd_A_log, L0_attn_bwd_Dp, L0_attn_bwd_out_w, L0_ffn_ln_gamma, L0_ffn_ln_beta, L0_ffn_router_w, L0_ffn_w12, L0_ffn_w3):

    def _L0_attn_ref(x, fwd_in_w, fwd_conv_w, fwd_conv_b, fwd_xproj_w, fwd_dt_w, fwd_dt_b, fwd_A_log, fwd_Dp, fwd_out_w, bwd_in_w, bwd_conv_w, bwd_conv_b, bwd_xproj_w, bwd_dt_w, bwd_dt_b, bwd_A_log, bwd_Dp, bwd_out_w):
        import jax, jax.numpy as jnp
        from jax import lax
        import numpy as np
        D_MODEL = 256
        E = 2 * D_MODEL
        N = 16
        D_CONV = 4
        DT_RANK = D_MODEL // 16
        B_SZ, L = (4, 512)

        def _mamba_params(key, scale=0.02):
            ks = jax.random.split(key, 7)
            return dict(in_w=jax.random.normal(ks[0], (D_MODEL, 2 * E), jnp.float32) * scale, conv_w=jax.random.normal(ks[1], (E, D_CONV), jnp.float32) * scale, conv_b=jnp.zeros((E,), jnp.float32), xproj_w=jax.random.normal(ks[2], (E, DT_RANK + 2 * N), jnp.float32) * scale, dt_w=jax.random.normal(ks[3], (DT_RANK, E), jnp.float32) * scale, dt_b=jax.random.normal(ks[4], (E,), jnp.float32) * 0.01, A_log=jnp.log(jnp.broadcast_to(jnp.arange(1, N + 1, dtype=jnp.float32), (E, N))), Dp=jnp.ones((E,), jnp.float32), out_w=jax.random.normal(ks[5], (E, D_MODEL), jnp.float32) * scale)

        def _mamba(x, in_w, conv_w, conv_b, xproj_w, dt_w, dt_b, A_log, Dp, out_w):
            xz = x @ in_w
            xi, z = jnp.split(xz, 2, axis=-1)
            xc = jnp.transpose(xi, (0, 2, 1))
            xc = lax.conv_general_dilated(xc, conv_w[:, None, :], (1,), [(D_CONV - 1, 0)], feature_group_count=E)
            xi = jax.nn.silu(jnp.transpose(xc + conv_b[None, :, None], (0, 2, 1)))
            proj = xi @ xproj_w
            dt, Bm, Cm = jnp.split(proj, [DT_RANK, DT_RANK + N], axis=-1)
            delta = jax.nn.softplus(dt @ dt_w + dt_b)
            A = -jnp.exp(A_log)

            def step(h, inp):
                d_t, b_t, c_t, u_t = inp
                h = jnp.exp(d_t[..., None] * A) * h + (d_t * u_t)[..., None] * b_t[:, None, :]
                y = jnp.einsum('ben,bn->be', h, c_t)
                return (h, y)
            h0 = jnp.zeros((x.shape[0], E, N), x.dtype)
            xs = (jnp.moveaxis(delta, 1, 0), jnp.moveaxis(Bm, 1, 0), jnp.moveaxis(Cm, 1, 0), jnp.moveaxis(xi, 1, 0))
            _, ys = lax.scan(step, h0, xs)
            y = jnp.moveaxis(ys, 0, 1) + xi * Dp
            y = y * jax.nn.silu(z)
            return y @ out_w
        h_fwd = _mamba(x, fwd_in_w, fwd_conv_w, fwd_conv_b, fwd_xproj_w, fwd_dt_w, fwd_dt_b, fwd_A_log, fwd_Dp, fwd_out_w)
        x_rev = jnp.flip(x, axis=1)
        h_bwd_rev = _mamba(x_rev, bwd_in_w, bwd_conv_w, bwd_conv_b, bwd_xproj_w, bwd_dt_w, bwd_dt_b, bwd_A_log, bwd_Dp, bwd_out_w)
        return h_fwd + jnp.flip(h_bwd_rev, axis=1)

    def _L0_ffn_ref(x, ln_gamma, ln_beta, router_w, w12, w3):
        import math
        import jax, jax.numpy as jnp
        import numpy as np
        D_MODEL = 256
        D_FF = 1024
        E = 8
        K = 2
        CAP_FACTOR = 1.25
        CLAMP = 10000.0
        LN_EPS = 1e-05
        B, S = (2, 512)
        Bq, Sq, D = x.shape
        T = Bq * Sq
        mu = jnp.mean(x, axis=-1, keepdims=True)
        var = jnp.mean(jnp.square(x - mu), axis=-1, keepdims=True)
        xn = (x - mu) * jax.lax.rsqrt(var + LN_EPS) * ln_gamma + ln_beta
        xf = xn.reshape(T, D)
        logits = jnp.clip(xf @ router_w.T, -CLAMP, CLAMP)
        top_v, top_i = jax.lax.top_k(logits, K)
        m = jnp.max(top_v, axis=-1, keepdims=True)
        ev = jnp.exp(top_v - m)
        top_p = ev / (jnp.sum(ev, axis=-1, keepdims=True) + 1e-12)
        Stot = T * K
        experts = top_i.reshape(-1)
        weights = top_p.reshape(-1)
        tokens = jnp.repeat(jnp.arange(T), K)
        oh = (experts[:, None] == jnp.arange(E)[None, :]).astype(jnp.int32)
        pos = jnp.take_along_axis(jnp.cumsum(oh, axis=0) - 1, experts[:, None], axis=1)[:, 0]
        C = max(1, math.ceil(T * K * CAP_FACTOR / E))
        kept = pos < C
        slot = jnp.where(kept, experts * C + pos, E * C)
        buf = jnp.zeros((E * C + 1, D), x.dtype).at[slot].set(xf[tokens])
        xb = buf[:E * C].reshape(E, C, D)
        gu = jnp.einsum('ecd,efd->ecf', xb, w12)
        g, u = jnp.split(gu, 2, axis=-1)
        h = jax.nn.silu(g) * u
        yb = jnp.einsum('ecf,edf->ecd', h, w3).reshape(E * C, D)
        ys = yb[jnp.minimum(slot, E * C - 1)] * (weights * kept.astype(weights.dtype))[:, None]
        out = jnp.zeros((T, D), x.dtype).at[tokens].add(ys)
        return out.reshape(Bq, Sq, D)
    x = L0_attn_x
    xn = _layernorm(x, axis=-1)
    x = x + _L0_attn_ref(xn, L0_attn_fwd_in_w, L0_attn_fwd_conv_w, L0_attn_fwd_conv_b, L0_attn_fwd_xproj_w, L0_attn_fwd_dt_w, L0_attn_fwd_dt_b, L0_attn_fwd_A_log, L0_attn_fwd_Dp, L0_attn_fwd_out_w, L0_attn_bwd_in_w, L0_attn_bwd_conv_w, L0_attn_bwd_conv_b, L0_attn_bwd_xproj_w, L0_attn_bwd_dt_w, L0_attn_bwd_dt_b, L0_attn_bwd_A_log, L0_attn_bwd_Dp, L0_attn_bwd_out_w) + _L0_ffn_ref(xn, L0_ffn_ln_gamma, L0_ffn_ln_beta, L0_ffn_router_w, L0_ffn_w12, L0_ffn_w3)
    return x

_drawn_inputs = setup_inputs


def setup_inputs(seed=0):
    import zlib

    import numpy as np

    out = dict(_drawn_inputs(seed))
    spreads = {'L0_attn_fwd_conv_b': (0.0, 0.8),
     'L0_attn_fwd_Dp': (1.0, 0.6),
     'L0_attn_bwd_conv_b': (0.0, 0.8),
     'L0_attn_bwd_Dp': (1.0, 0.6),
     'L0_ffn_ln_gamma': (1.0, 0.6),
     'L0_ffn_ln_beta': (0.0, 0.8)}
    factors = {'L0_attn_fwd_in_w': 8.0,
     'L0_attn_fwd_conv_w': 8.0,
     'L0_attn_fwd_xproj_w': 8.0,
     'L0_attn_fwd_dt_w': 8.0,
     'L0_attn_fwd_dt_b': 8.0,
     'L0_attn_fwd_A_log': 8.0,
     'L0_attn_fwd_out_w': 8.0,
     'L0_attn_bwd_in_w': 8.0,
     'L0_attn_bwd_conv_w': 8.0,
     'L0_attn_bwd_xproj_w': 8.0,
     'L0_attn_bwd_dt_w': 8.0,
     'L0_attn_bwd_dt_b': 28.607,
     'L0_attn_bwd_A_log': 8.0,
     'L0_attn_bwd_out_w': 8.0,
     'L0_ffn_router_w': 8.0,
     'L0_ffn_w12': 8.0,
     'L0_ffn_w3': 8.0}
    for name, (base, spread) in spreads.items():
        noise = np.random.default_rng([zlib.crc32(name.encode()), seed]).standard_normal(out[name].shape)
        drawn = base * np.exp(spread * noise) if base else spread * noise
        out[name] = jnp.asarray(drawn.astype(out[name].dtype))
    for name, factor in factors.items():
        out[name] = (out[name] * factor).astype(out[name].dtype)
    return out
```

```python
from contextlib import ExitStack

import numpy as np

import concourse.bass as bass
from concourse import mybir

F32 = mybir.dt.float32
I32 = mybir.dt.int32
U32 = mybir.dt.uint32
ALU = mybir.AluOpType
ACT = mybir.ActivationFunctionType
AX_X = mybir.AxisListType.X

P = 128
BATCH, L, D = 4, 1024, 256
E = 512
ET = E // P
KD = D // P
NS = 16
RANK = 16
TAPS = 4
HALO = TAPS - 1
H = 512
TT = H // P
TILES = BATCH * L // P
UNITS = 4
DIR = (0, 0, 1, 1)
HALF = (0, 1, 1, 0)
EX, CAP, FF = 8, 1280, 1024
FB = FF // P
CH = 160
CR = CH // 2
ITERS = BATCH * UNITS * TT
SLOTS = EX * CAP
NPI = NS // TT
CLAMP = 10000.0
EPS = 1e-5
BROW = 32
GT = 4

SCAN0 = 2
STT0 = 4
HT0 = 4


def mixed_block(nc, x, ln_g, ln_b, routerT, w12T, w3T, mamba, const, out):
    ctx = ExitStack()
    with ctx:
        def sb(name, shape, dt=F32):
            return ctx.enter_context(nc.sbuf_tensor(name, shape, dt))

        def sem(name):
            return ctx.enter_context(nc.semaphore(name))

        def dram(name, shape):
            return nc.dram_tensor(name, shape, F32).ap()

        xnT_d = dram("xnT_d", (TILES, P, KD, P))
        xb_d = dram("xb_d", (SLOTS, D))
        yb_d = dram("yb_d", (SLOTS, D))
        bT_d = dram("bT_d", (2, NS, H))
        yd_d = dram("yd_d", (2, TILES, P, D))

        def bank(name):
            return ctx.enter_context(nc.psum_tensor(name, [P, 512], F32))

        ps_a = [bank("ps_a0"), bank("ps_a1")]
        ps_hT = [bank("ps_hT0"), bank("ps_hT1")]
        ps_m = [bank("ps_m0"), bank("ps_m1")]
        ps_p = bank("ps_p")
        ps_e = bank("ps_e")

        cst = sb("cst", [P, 2 * P + EX])
        ident = cst[:, 0:P]
        below = cst[:, P:2 * P]
        iota8 = cst[:, 2 * P:2 * P + EX]
        in_w = [sb(f"in_w{d}", [P, KD, 2 * E]) for d in range(2)]
        xp_w = [sb(f"xp_w{d}", [P, ET, BROW + 2 * NS]) for d in range(2)]
        dt_w = [sb(f"dt_w{d}", [RANK + 1, E]) for d in range(2)]
        cv_w = [sb(f"cv_w{d}", [P, ET, TAPS]) for d in range(2)]
        cv_b = [sb(f"cv_b{d}", [P, ET]) for d in range(2)]
        dp = [sb(f"dp{d}", [P, ET]) for d in range(2)]
        diag = [sb(f"diag{d}", [P, ET, P]) for d in range(2)]
        negA = [sb(f"negA{d}", [P, NS, ET]) for d in range(2)]
        out_w = [sb(f"out_w{d}", [P, ET, D]) for d in range(2)]
        wmoe = [sb(f"wmoe{i}", [P, KD * 2 * FF + FB * D]) for i in range(2)]
        w12 = [w[:, 0:KD * 2 * FF].rearrange("p (k f) -> p k f", k=KD) for w in wmoe]
        w3 = [w[:, KD * 2 * FF:].rearrange("p (j n) -> p j n", j=FB) for w in wmoe]
        gate_w = sb("gate_w", [P, 2, TILES])
        slot_sc = sb("slot_sc", [P, 2, TILES], I32)
        slot_ga = sb("slot_ga", [P, 2, TILES], I32)

        dT = [sb(f"dT{i}", [P, ET, H]) for i in range(2)]
        duT = [sb(f"duT{i}", [P, ET, H]) for i in range(2)]
        hy = sb("hy", [P, 2 * ET * H + 2 * TT * E])
        h = [hy[:, i * ET * H:(i + 1) * ET * H].rearrange("p (e t) -> p e t", e=ET) for i in range(2)]
        y = [hy[:, (2 + i) * ET * H:(3 + i) * ET * H].rearrange("p (t e) -> p t e", t=TT)
             for i in range(2)]
        xf_all = hy[:, :].rearrange("p (t d) -> p t d", t=TILES)
        bm = [sb(f"bm{i}", [P, 2, H]) for i in range(2)]
        bbc = sb("bbc", [P, 2, NPI, H])
        c_t = [sb(f"c_t{i}", [P, TT, NS]) for i in range(2)]
        state = sb("state", [P, NS, ET])

        xnP = sb("xnP", [P, KD, P])
        xi = sb("xi", [P, ET, P + HALO])
        cv = sb("cv", [P, ET, P])
        th = sb("th", [P, ET, P])
        u2 = sb("u2", [P, ET, P])
        dtb = sb("dtb", [BROW + NS, P])
        dtT, bs = dtb[0:BROW, :], dtb
        sp = sb("sp", [P, ET, P])

        xnE = sb("xnE", [P, KD, P])
        sz = sb("sz", [P, E])
        yg = sb("yg", [P, E])
        ygT = sb("ygT", [P, E])
        o_sbuf = sb("o_sbuf", [P, D])

        xbr = sb("xbr", [CR, 2, D])
        xbT = sb("xbT", [P, KD, CH])
        tg = sb("tg", [P, 2 * CH])
        tu = tg
        gs = sb("gs", [P, 2 * CH])
        hm = sb("hm", [P, FB, CH])
        ybT = sb("ybT", [P, KD, CH])
        ybr = sb("ybr", [CR, 2 * D])

        taken = {}

        def view(owner, n):
            at = taken.get(owner.name, 0)
            taken[owner.name] = at + n
            flat = owner[:, :, :].rearrange("p a b -> p (a b)") if len(owner.shape) == 3 else owner[:, :]
            assert at + n <= flat.shape[1]
            return flat[:, at:at + n]

        def tiles_of(ap, n):
            return ap.rearrange("p (t s) -> p t s", t=n)

        xg = [tiles_of(view(dT[1], GT * D), GT) for _ in range(2)]
        xfg = [tiles_of(view(duT[1], GT * D), GT) for _ in range(2)]
        spare = wmoe[1]
        lnT = [view(spare, 2 * D) for _ in range(2)]
        gam, bet = view(spare, D), view(spare, D)
        st6 = tiles_of(view(spare, 6 * GT), GT)
        mv = tiles_of(view(spare, 2 * GT), GT)
        ve, sd, rs, nt = [view(spare, GT) for _ in range(4)]
        lg, both, tot, pos = [tiles_of(view(spare, TILES * EX), TILES) for _ in range(4)]
        m8, i8, prod = [tiles_of(view(spare, TILES * EX), TILES) for _ in range(3)]
        oh = [tiles_of(view(spare, TILES * EX), TILES) for _ in range(2)]
        ones = view(spare, P)
        rt = tiles_of(view(spare, KD * EX), KD)
        ixf, slf, kp = [tiles_of(view(spare, 2 * TILES), 2) for _ in range(3)]
        ev = tiles_of(view(spare, 2 * TILES), 2)
        rsum = view(spare, TILES)
        fin = [[view(wmoe[0], D) for _ in range(3)] for _ in range(2)]
        fga = [[view(wmoe[0], D) for _ in range(2)] for _ in range(2)]
        fo = [view(wmoe[0], D) for _ in range(2)]

        s_const, s_w = sem("s_const"), sem("s_w")
        s_zero, s_zfill, s_neg, s_diag, s_mem = sem("s_zero"), sem("s_zfill"), sem("s_neg"), sem("s_diag"), sem("s_mem")
        s_x = [sem("s_x0"), sem("s_x1")]
        s_var, s_sd, s_step, s_xf, s_xfc = sem("s_var"), sem("s_sd"), sem("s_step"), sem("s_xf"), sem("s_xfc")
        s_lnT, s_lnTs, s_lg = sem("s_lnT"), sem("s_lnTs"), sem("s_lg")
        s_xst = [sem("s_xst0"), sem("s_xst1")]
        s_scaled, s_cum, s_dif, s_exp, s_slot, s_scat = (sem("s_scaled"), sem("s_cum"), sem("s_dif"), sem("s_exp"),
                                                        sem("s_slot"), sem("s_scat"))
        s_places = sem("s_places")
        a_ready, scan_done, b_ready = sem("a_ready"), sem("scan_done"), sem("b_ready")
        ht_ready, stt_done, saved, bbc_in = sem("ht_ready"), sem("stt_done"), sem("saved"), sem("bbc_in")
        xnp_in, xi_mm, xi_sb, tap, halo = sem("xnp_in"), sem("xi_mm"), sem("xi_sb"), sem("tap"), sem("halo")
        halo0, th_done, u2_done, proj_mm = sem("halo0"), sem("th_done"), sem("u2_done"), sem("proj_mm")
        proj_sb, bT_out, v_mm, sp_step = sem("proj_sb"), sem("bT_out"), sem("v_mm"), sem("sp_step")
        d_done, du_done, yi_mm, yi_done = sem("d_done"), sem("du_done"), sem("yi_mm"), sem("yi_done")
        xne_in, z_mm, tz_done, sz_done = sem("xne_in"), sem("z_mm"), sem("tz_done"), sem("sz_done")
        yg_done, ygT_mm, ygT_sb, o_mm, o_sb, o_out = (sem("yg_done"), sem("ygT_mm"), sem("ygT_sb"), sem("o_mm"),
                                                      sem("o_sb"), sem("o_out"))
        w_in = [sem("w_in0"), sem("w_in1")]
        xb_in, xbT_mm, xbT_sb, g_mm, u_mm = sem("xb_in"), sem("xbT_mm"), sem("xbT_sb"), sem("g_mm"), sem("u_mm")
        tg_done, gs_done, tu_done, hm_done = sem("tg_done"), sem("gs_done"), sem("tu_done"), sem("hm_done")
        ybT_mm, ybT_sb, ybr_mm, ybr_sb, yb_out = (sem("ybT_mm"), sem("ybT_sb"), sem("ybr_mm"), sem("ybr_sb"),
                                                  sem("yb_out"))
        f_in = [sem("f_in0"), sem("f_in1")]
        f_ga = [sem("f_ga0"), sem("f_ga1")]
        f_dve = sem("f_dve")
        f_out = [sem("f_out0"), sem("f_out1")]
        gates = {"sp": sem("gate_sp"), "pool": sem("gate_pool"), "act": sem("gate_act"),
                 "dve": sem("gate_dve"), "pe": sem("gate_pe")}

        def holder(eng, name):
            def held(s, value):
                eng.wait_ge(s, value)
                eng.sem_inc(gates[name], 1)
            return held

        def run(eng, unit):
            def batch(b, first, last):
                for uu in range(UNITS):
                    unit(b, uu, not (first and uu == 0), not (last and uu == UNITS - 1))
            batch(0, True, False)
            with eng.Fori(1, BATCH - 1) as b:
                batch(b, False, False)
            batch(BATCH - 1, False, True)

        def repeat(eng, b, uu, iteration, end=TT):
            if isinstance(b, int) and b == 0 and uu < 2:
                for q in range(end):
                    iteration(q)
            else:
                with eng.Fori(0, end) as q:
                    iteration(q)

        def first_g(b, uu):
            return b * (UNITS * TT) + uu * TT

        def order(d, q):
            return q if d == 0 else (TT - 1) - q

        def token_tile(b, uu, tt):
            return (b + uu // UNITS) * (L // P) + (HALF[uu % UNITS] * TT) + tt

        def pro_tt(uu, q):
            return order(DIR[uu % UNITS], q)

        def epi_tt(uu, q):
            return order(DIR[(uu + 2) % UNITS], q)

        block = ctx.enter_context(nc.Block())

        @block.sync
        def _(eng):
            held = holder(eng, "sp")
            eng.dma_start(cst[:, :], const).then_inc(s_const, 16)
            eng.dma_start(gam, ln_g.partition_broadcast(P)).then_inc(s_const, 16)
            eng.dma_start(bet, ln_b.partition_broadcast(P)).then_inc(s_const, 16)
            eng.dma_start(rt, routerT.rearrange("(k p) e -> p k e", p=P)).then_inc(s_const, 16)

            def load_x(group, i):
                eng.dma_start(xg[i], x[bass.ds(group * GT, GT)].rearrange("t p d -> p t d")).then_inc(s_x[i], 16)

            load_x(0, 0)
            load_x(1, 1)
            for d in range(2):
                m = mamba[d]
                eng.dma_start(in_w[d][:], m["in_w"].rearrange("(k p) n -> p k n", p=P)).then_inc(s_w, 16)
                eng.dma_start(xp_w[d][:], m["xproj"].rearrange("(k p) n -> p k n", p=P)).then_inc(s_w, 16)
                eng.dma_start(dt_w[d][:], m["dt_w"]).then_inc(s_w, 16)
                eng.dma_start(cv_w[d][:], m["conv_w"]).then_inc(s_w, 16)
                eng.dma_start(cv_b[d][:], m["conv_b"]).then_inc(s_w, 16)
                eng.dma_start(dp[d][:], m["Dp"]).then_inc(s_w, 16)
                eng.dma_start(negA[d][:], m["A_log"]).then_inc(s_w, 16)
                eng.dma_start(out_w[d][:], m["out_w"].rearrange("(k p) n -> p k n", p=P)).then_inc(s_w, 16)
            eng.wait_ge(s_zero, 1)
            zrows = xb_d.rearrange("(c p r) d -> c p (r d)", p=P, r=8)
            for c in range(SLOTS // (P * 8)):
                eng.dma_start(zrows[c], dT[0][:].rearrange("p e t -> p (e t)")).then_inc(s_zfill, 16)

            def load_expert_part(e, i, part):
                f = 2 * FF // FB
                eng.dma_start(w12[i][:, :, bass.ds(part * f, f)],
                              w12T[bass.ds(e, 1), :, bass.ds(part * f, f)].rearrange("a (k p) f -> p (a k) f", p=P))\
                   .then_inc(w_in[i], 16)
                eng.dma_start(w3[i][:, bass.ds(part, 1), :],
                              w3T[bass.ds(e, 1), bass.ds(part * P, P), :].rearrange("a p n -> p a n"))\
                   .then_inc(w_in[i], 16)

            for part in range(FB):
                load_expert_part(0, 0, part)

            def first_pair(k2, last):
                for i in range(2):
                    for t in range(GT):
                        k = k2 * (2 * GT) + (i * GT + t)
                        held(s_lnTs, k + 1)
                        eng.dma_start(xnT_d[bass.ds(k, 1)].rearrange("a p k t -> p (a k t)"),
                                      lnT[t % 2][:, 0:D]).then_inc(s_xst[t % 2], 16)
                    if not last:
                        load_x(k2 * 2 + (i + 2), i)

            with eng.Fori(0, TILES // (2 * GT) - 1) as k2:
                first_pair(k2, False)
            first_pair(TILES // (2 * GT) - 1, True)
            for i in range(2):
                eng.wait_ge(s_xst[i], 16 * (TILES // 2))

            def load_pro(b, uu, q, ps):
                held(xi_mm, ps)
                eng.dma_start(xnP[:], xnT_d[bass.ds(token_tile(b, uu, pro_tt(uu, q)), 1)]
                              .rearrange("a p k t -> p (a k) t")).then_inc(xnp_in, 16)

            def load_epi(b, uu, q, es):
                held(z_mm, es)
                eng.dma_start(xnE[:], xnT_d[bass.ds(token_tile(b, uu, epi_tt(uu, q)), 1)]
                              .rearrange("a p k t -> p (a k) t")).then_inc(xne_in, 16)

            def store_b(uu, q, ps):
                held(proj_sb, ps * 3 + 3)
                eng.dma_start(bT_d[uu % 2][:, bass.ds(pro_tt(uu, q) * P, P)], bs[BROW:BROW + NS, :])\
                   .then_inc(bT_out, 16)

            def load_bbc(uu, q, slices):
                held(bT_out, slices * 16)
                rows = bT_d[uu % 2][bass.ds(q * NPI, NPI), :].rearrange("(a n) t -> a (n t)", a=1)
                eng.dma_start(bbc[:, bass.ds(q % 2, 1)].rearrange("p a n t -> p (a n t)"),
                              rows.broadcast_to([P, NPI * H])).then_inc(bbc_in, 16)

            def load_slots(g, previous):
                held(xbT_mm, previous)
                eng.dma_start(xbr[:], xb_d[bass.ds(g * CH, CH)].rearrange("(j p) d -> p j d", p=CR))\
                   .then_inc(xb_in, 16)

            def store_epi(b, uu, q, es):
                held(o_sb, es + 1)
                eng.dma_start(yd_d[DIR[uu % UNITS]][bass.ds(token_tile(b, uu, epi_tt(uu, q)), 1)]
                              .rearrange("a p d -> p (a d)"), o_sbuf[:]).then_inc(o_out, 16)

            load_pro(0, 0, 0, 0)
            for q in range(TT):
                load_pro(0, (q + 1) // TT, (q + 1) % TT, q + 1)
                store_b(0, q, q)
            load_bbc(0, 0, TT)
            eng.wait_ge(s_scat, 32 * TILES)
            load_slots(0, 0)

            def unit(b, uu, epi, pro):
                g0 = first_g(b, uu)
                last_batch = isinstance(b, int) and b == BATCH - 1

                def iteration(q, g, end):
                    if not end:
                        held(b_ready, g * (2 * NPI))
                        held(bbc_in, g * 16 + 16)
                        load_bbc(uu, q + 1, g0 + TT)
                    if not (end and not pro):
                        load_slots(g + 1, g + 1)
                    if not (last_batch and uu >= 2):
                        held(ybT_mm, first_g(b, uu - uu % 2))
                        load_expert_part(b * 2 + (uu // 2 + 1), 1 - uu // 2, (uu % 2) * TT + q)
                    if pro and not (end and last_batch and uu == UNITS - 2):
                        load_pro(b, uu + 1 + end, 0 if end else q + 1, g + (TT + 1))
                    if epi or end:
                        load_epi(b, uu - 1 + end, 0 if end else q + 1, g - (TT - 1))
                    if pro:
                        store_b(uu + 1, q, g + TT)
                        if end:
                            held(b_ready, g * (2 * NPI))
                            held(bbc_in, g * 16 + 16)
                            load_bbc(uu + 1, 0, g0 + 2 * TT)
                    if epi:
                        store_epi(b, uu - 1, q, g - TT)
                    held(ybr_sb, g + 1)
                    eng.dma_start(yb_d[bass.ds(g * CH, CH)].rearrange("(j p) d -> p j d", p=CR),
                                  ybr[:].rearrange("p (j d) -> p j d", j=2)).then_inc(yb_out, 16)

                repeat(eng, b, uu, lambda q: iteration(q, g0 + q, False), TT - 1)
                iteration(TT - 1, g0 + (TT - 1), True)

            run(eng, unit)

            for q in range(TT):
                es = ITERS - TT + q
                if q + 1 < TT:
                    load_epi(BATCH - 1, UNITS - 1, q + 1, es + 1)
                store_epi(BATCH - 1, UNITS - 1, q, es)

            eng.wait_ge(o_out, 16 * ITERS)
            eng.wait_ge(yb_out, 16 * ITERS)

            def last_pair(k2, first):
                for i in range(2):
                    t = k2 * 2 + i
                    if not first:
                        held(f_dve, t * 4 - 4)
                    eng.dma_start(fin[i][0], x[bass.ds(t, 1)].rearrange("a p d -> p (a d)")).then_inc(f_in[i], 16)
                    for d in range(2):
                        eng.dma_start(fin[i][1 + d], yd_d[d][bass.ds(t, 1)].rearrange("a p d -> p (a d)"))\
                           .then_inc(f_in[i], 16)

            last_pair(0, True)
            with eng.Fori(1, TILES // 2) as k2:
                last_pair(k2, False)
            for i in range(2):
                eng.wait_ge(f_out[i], 16 * (TILES // 2))

        @block.gpsimd
        def _(eng):
            held = holder(eng, "pool")
            eng.memset(dT[0][:], 0.0).then_inc(s_zero, 1)
            eng.memset(ones, 1.0).then_inc(s_mem, 1)
            eng.memset(dtT, 1.0).then_inc(s_mem, 1)

            eng.wait_ge(s_slot, 1)
            eng.wait_ge(s_xfc, TILES // GT)
            eng.wait_ge(s_zfill, 16 * (SLOTS // (P * 8)))
            for t in range(TILES):
                for k in range(2):
                    eng.indirect_dma_start(xb_d, bass.IndirectOffsetOnAxis(ap=slot_sc[:, k, t:t + 1], axis=0),
                                           xf_all[:, t, :], None, bounds_check=SLOTS - 1, oob_is_err=False)\
                       .then_inc(s_scat, 16)
            eng.wait_ge(s_w, 16 * 16)

            def zero_halo(d):
                eng.memset(xi[:, :, 0:HALO] if d == 0 else xi[:, :, P:P + HALO], 0.0).then_inc(halo0, 1)

            def move_halo(d, ps):
                held(tap, ps * TAPS + TAPS)
                tail, head = xi[:, :, P:P + HALO], xi[:, :, 0:HALO]
                src, dst = (tail, head) if d == 0 else (head, tail)
                eng.tensor_copy(dst, src).then_inc(halo, 1)

            def make_du(uu, q, ps):
                held(d_done, ps + 1)
                held(u2_done, ps + 1)
                tt = pro_tt(uu, q)
                part = bass.ds(tt * P, P)
                eng.tensor_tensor(duT[uu % 2][:, :, part], dT[uu % 2][:, :, part], u2[:], ALU.mult)\
                   .then_inc(du_done, 1)

            def gate_y(uu, q, es):
                held(sz_done, es + 1)
                held(ygT_mm, es)
                tt = epi_tt(uu, q)
                eng.tensor_tensor(yg[:], y[uu % 2][:, bass.ds(tt, 1), :].rearrange("p a e -> p (a e)"), sz[:],
                                  ALU.mult).then_inc(yg_done, 1)

            def times_gate(g, i):
                held(tu_done, g * 4 + (i + 1))
                held(gs_done, g * 4 + (i + 1))
                if i == 0:
                    held(ybT_mm, g)
                eng.tensor_tensor(hm[:, 2 * i:2 * i + 2, :].rearrange("p f c -> p (f c)"), tu[:], gs[:],
                                  ALU.mult).then_inc(hm_done, 1)

            zero_halo(0)
            for ps in range(TT):
                move_halo(0, ps)
                make_du(0, ps, ps)

            def unit(b, uu, epi, pro):
                par = uu % 2
                pd = DIR[(uu + 1) % UNITS]
                last_col = H - 1 if DIR[uu] == 0 else 0
                if pro and uu % 2 == 1:
                    held(tap, first_g(b, uu) * TAPS + TT * TAPS)
                    held(halo, first_g(b, uu) + TT)
                    zero_halo(pd)
                held(du_done, first_g(b, uu) + TT)

                def save(n, src, col, g4):
                    held(scan_done, g4)
                    eng.tensor_copy(state[:, bass.ds(n, 1), :],
                                    h[src][:, :, col:col + 1].rearrange("p e a -> p a e")).then_inc(saved, 1)

                def iteration(q):
                    g = first_g(b, uu) + q
                    held(bbc_in, g * 16 + 16)
                    if epi:
                        held(stt_done, first_g(b, uu) * NS + STT0)
                    for j in range(2 * NPI):
                        n, half = j // 2, j % 2
                        held(scan_done, g * 16 + 2 * j)
                        eng.tensor_tensor(bm[j % 2][:], duT[par][:, 2 * half:2 * half + 2, :],
                                          bbc[:, bass.ds(q % 2, 1), n, :].broadcast_to([P, 2, H]),
                                          ALU.mult).then_inc(b_ready, 1)
                        if j == 0:
                            save((q * NPI + (NS - 1)) % NS, 1, last_col, g * 16 + SCAN0)
                        if j in (3, 5, 7):
                            m = (j - 3) // 2
                            save(q * NPI + m, m % 2, last_col, g * 16 + (4 * m + 4 + SCAN0))
                        if j in (2, 3, 4, 5):
                            times_gate(g, j - 2)
                        if pro:
                            ps = g + TT
                            if j == 2:
                                move_halo(pd, ps)
                            if j == 7:
                                make_du((uu + 1) % UNITS, q, ps)
                        if epi and j == 4:
                            gate_y((uu - 1) % UNITS, q, g - TT)

                repeat(eng, b, uu, iteration)

            run(eng, unit)

            eng.wait_ge(stt_done, ITERS * NS + STT0)
            for q in range(TT):
                gate_y(UNITS - 1, q, ITERS - TT + q)

            eng.wait_ge(yb_out, 16 * ITERS)
            for t in range(TILES):
                if t >= 2:
                    eng.wait_ge(f_dve, 4 * (t - 1))
                for k in range(2):
                    eng.indirect_dma_start(fga[t % 2][k], None, yb_d,
                                           bass.IndirectOffsetOnAxis(ap=slot_ga[:, k, t:t + 1], axis=0))\
                       .then_inc(f_ga[t % 2], 16)
            for i in range(2):
                eng.wait_ge(f_ga[i], 32 * (TILES // 2))

        @block.scalar
        def _(eng):
            held = holder(eng, "act")

            def first_pair(k2, first):
                for i in range(2):
                    grp = k2 * 2 + i
                    for r in range(2):
                        held(s_var, grp * 2 + (r + 1))
                        eng.activation(sd, ve, ACT.Sqrt).then_inc(s_sd, 1)
                    held(s_xf, grp + 1)
                    eng.activation(xf_all[:, bass.ds(grp * GT, GT), :], xfg[i], ACT.Copy).then_inc(s_xfc, 1)
                    for t in range(GT):
                        k = grp * GT + t
                        held(s_lnT, k + 1)
                        if not (first and i == 0 and t < 2):
                            held(s_xst[t % 2], grp * (8 * GT) + (t // 2) * 16)
                            held(s_lg, k - 1)
                        eng.activation(lnT[t % 2], ps_hT[t % 2][:, :], ACT.Copy).then_inc(s_lnTs, 1)

            first_pair(0, True)
            with eng.Fori(1, TILES // (2 * GT)) as k2:
                first_pair(k2, False)

            eng.wait_ge(s_dif, 1)
            eng.activation(ev[:, 0, :], ev[:, 1, :], ACT.Exp).then_inc(s_exp, 1)
            eng.wait_ge(s_w, 16 * 16)
            for d in range(2):
                eng.activation(negA[d][:], negA[d][:], ACT.Exp).then_inc(s_neg, 1)
            eng.wait_ge(s_neg, 2)
            for d in range(2):
                eng.activation(negA[d][:], negA[d][:], ACT.Copy, scale=-1.0).then_inc(s_neg, 1)
            eng.wait_ge(s_neg, 4)
            eng.wait_ge(s_scat, 32 * TILES)
            eng.wait_ge(s_zfill, 16 * (SLOTS // (P * 8)))

            def xi_out(d, ps):
                held(xi_mm, ps + 1)
                held(halo, ps)
                lo = HALO if d == 0 else 0
                eng.activation(xi[:, :, lo:lo + P], ps_p[:, :].rearrange("p (e t) -> p e t", e=ET), ACT.Copy)\
                   .then_inc(xi_sb, 1)

            def tanh_conv(ps):
                held(tap, ps * TAPS + TAPS)
                held(u2_done, ps)
                eng.activation(th[:], cv[:], ACT.Tanh, scale=0.5).then_inc(th_done, 1)

            def proj_out(uu, q, ps):
                held(proj_mm, ps + 1)
                held(v_mm, ps)
                eng.activation(dtT[0:RANK, :], ps_p[0:RANK, 0:P], ACT.Copy, scale=0.5).then_inc(proj_sb, 1)
                held(bT_out, ps * 16)
                eng.activation(bs[BROW:BROW + NS, :], ps_p[BROW:BROW + NS, 0:P], ACT.Copy, scale=0.25)\
                   .then_inc(proj_sb, 1)
                eng.activation(c_t[uu % 2][:, bass.ds(pro_tt(uu, q), 1), :].rearrange("p a n -> p (a n)"),
                               ps_p[:, P:P + NS], ACT.Copy, scale=0.5).then_inc(proj_sb, 1)

            def softplus_out(ps):
                flat = ps_p[:, :].rearrange("p (e t) -> p e t", e=ET)
                held(v_mm, ps + 1)
                held(d_done, ps)
                eng.activation(sp[:], flat, ACT.Abs).then_inc(sp_step, 1)
                held(sp_step, ps * 3 + 1)
                eng.activation(sp[:], sp[:], ACT.Exp, scale=-1.0).then_inc(sp_step, 1)
                held(sp_step, ps * 3 + 2)
                eng.activation(sp[:], sp[:], ACT.Ln, bias=1.0).then_inc(sp_step, 1)

            def y_init(uu, q, ps, es):
                held(yi_mm, ps + 1)
                if es is not None:
                    held(yg_done, es + 1)
                eng.activation(y[uu % 2][:, bass.ds(pro_tt(uu, q), 1), :].rearrange("p a e -> p (a e)"),
                               ps_p[:, :], ACT.Copy).then_inc(yi_done, 1)

            def tanh_z(es):
                held(z_mm, es + 1)
                held(yg_done, es)
                eng.activation(sz[:], ps_e[:, :], ACT.Tanh, scale=0.5).then_inc(tz_done, 1)

            def ygT_out(es):
                held(ygT_mm, es + 1)
                held(o_mm, es)
                eng.activation(ygT[:], ps_e[:, :], ACT.Copy, scale=0.5).then_inc(ygT_sb, 1)

            def o_out_sb(es):
                held(o_mm, es + 1)
                held(o_out, es * 16)
                eng.activation(o_sbuf[:], ps_e[:, 0:D], ACT.Copy).then_inc(o_sb, 1)

            def xbT_out(g):
                held(xbT_mm, g + 1)
                held(u_mm, g * 4)
                eng.activation(xbT[:], ps_m[1][:, 0:KD * CH].rearrange("p (k c) -> p k c", k=KD), ACT.Copy)\
                   .then_inc(xbT_sb, 1)

            def tanh_g(g, i):
                held(g_mm, g * 4 + (i + 1))
                held(hm_done, g * 4 + i)
                eng.activation(tg[:], ps_m[0][:, 0:2 * CH], ACT.Tanh, scale=0.5).then_inc(tg_done, 1)
                eng.activation(gs[:], ps_m[0][:, 0:2 * CH], ACT.Copy, scale=0.5).then_inc(gs_done, 1)

            def ybT_out(g):
                held(ybT_mm, g + 1)
                held(ybr_mm, g)
                eng.activation(ybT[:], ps_m[0][:, 0:KD * CH].rearrange("p (k c) -> p k c", k=KD), ACT.Copy)\
                   .then_inc(ybT_sb, 1)

            def ybr_out(g):
                held(ybr_mm, g + 1)
                held(yb_out, g * 16)
                eng.activation(ybr[:], ps_m[1][0:CR, :], ACT.Copy).then_inc(ybr_sb, 1)

            for ps in range(TT):
                xi_out(0, ps)
                tanh_conv(ps)
                proj_out(0, ps, ps)
                softplus_out(ps)
                y_init(0, ps, ps, None)

            def unit(b, uu, epi, pro):
                par, d = uu % 2, DIR[uu]
                nu, g0 = (uu + 1) % UNITS, first_g(b, uu)
                held(d_done, g0 + TT)
                def iteration(q):
                    g = g0 + q
                    ps, es = g + TT, (g - TT if epi else None)
                    for s in range(NPI * ET):
                        n, e = s // ET, s % ET
                        held(scan_done, g * 16 + (s + 1))
                        eng.activation(ps_a[s % 2][:, :], dT[par][:, e, :], ACT.Exp,
                                       scale=negA[d][:, bass.ds(q * NPI + n, 1), e]).then_inc(a_ready, 1)
                        if s == 0:
                            xbT_out(g)
                        if s == 1 and pro:
                            xi_out(DIR[nu], ps)
                        if s in (2, 4, 6, 8):
                            tanh_g(g, s // 2 - 1)
                        if s == 3 and epi:
                            tanh_z(es)
                        if s == 4 and pro:
                            tanh_conv(ps)
                        if s == 10 and pro:
                            held(stt_done, g0 * NS + STT0)
                            proj_out(nu, q, ps)
                        if s == 10 and epi:
                            ygT_out(es)
                        if s == 12 and pro:
                            softplus_out(ps)
                        if s == 13:
                            ybT_out(g)
                        if s == 14 and epi:
                            o_out_sb(es)
                        if s == 15 and pro:
                            y_init(nu, q, ps, es)
                    ybr_out(g)

                repeat(eng, b, uu, iteration)

            run(eng, unit)

            for q in range(TT):
                es = ITERS - TT + q
                tanh_z(es)
                ygT_out(es)
                o_out_sb(es)

            with eng.Fori(0, TILES // 2) as k2:
                for i in range(2):
                    t = k2 * 2 + i
                    held(f_dve, t * 4 + 4)
                    eng.dma_start(out[bass.ds(t, 1)].rearrange("a p d -> p (a d)"), fo[i]).then_inc(f_out[i], 16)

        @block.tensor
        def _(eng):
            held = holder(eng, "pe")
            eng.wait_ge(s_const, 16 * 4)

            def first_pair(k2, first):
                for i in range(2):
                    grp = k2 * 2 + i
                    eng.wait_ge(s_xf, grp + 1)
                    for t in range(GT):
                        k = grp * GT + t
                        if not (first and i == 0 and t < 2):
                            eng.wait_ge(s_lnTs, k - 1)
                        for j, src in enumerate((xg[i], xfg[i])):
                            for c in range(KD):
                                o = (j * KD + c) * P
                                ins = eng.transpose(ps_hT[t % 2][:, o:o + P], src[:, t, c * P:(c + 1) * P], ident)
                        ins.then_inc(s_lnT, 1)
                        if not (first and i == 0 and t == 0):
                            logits(grp * GT + (t - 1), (t + 1) % 2)

            def logits(k, par):
                eng.wait_ge(s_lnTs, k + 1)
                for c in range(KD):
                    ins = eng.matmul(ps_m[0][:, bass.ds(k * EX, EX)], lnT[par][:, D + c * P:D + (c + 1) * P],
                                     rt[:, c, :], start=(c == 0), stop=(c == KD - 1))
                ins.then_inc(s_lg, 1)

            first_pair(0, True)
            with eng.Fori(1, TILES // (2 * GT)) as k2:
                first_pair(k2, False)
            logits(TILES - 1, 1)

            eng.wait_ge(s_places, 1)
            eng.wait_ge(s_mem, 2)
            flat = both.rearrange("p t e -> p (t e)")
            eng.matmul(ps_m[1][:, 0:TILES * EX], below, flat, start=True, stop=True)
            eng.matmul(ps_p[:, 0:TILES * EX], ones, flat, start=True, stop=True).then_inc(s_cum, 1)
            eng.wait_ge(s_w, 16 * 16)
            eng.wait_ge(s_diag, 1)

            def xi_in(d, ps):
                eng.wait_ge(xnp_in, ps * 16 + 16)
                eng.wait_ge(yi_done, ps)
                for e in range(ET):
                    for k in range(KD):
                        ins = eng.matmul(ps_p[:, e * P:(e + 1) * P], in_w[d][:, k, e * P:(e + 1) * P],
                                         xnP[:, k, :], start=(k == 0), stop=(k == KD - 1))
                ins.then_inc(xi_mm, 1)

            def proj(d, ps):
                eng.wait_ge(u2_done, ps + 1)
                eng.wait_ge(xi_sb, ps + 1)
                for e in range(ET):
                    eng.matmul(ps_p[0:BROW + NS, 0:P], xp_w[d][:, e, 0:BROW + NS], u2[:, e, :],
                               start=(e == 0), stop=(e == ET - 1))
                for e in range(ET):
                    ins = eng.matmul(ps_p[:, P:P + NS], u2[:, e, :], xp_w[d][:, e, BROW + NS:],
                                     start=(e == 0), stop=(e == ET - 1))
                ins.then_inc(proj_mm, 1)

            def v_in(d, ps):
                eng.wait_ge(proj_sb, ps * 3 + 3)
                for e in range(ET):
                    ins = eng.matmul(ps_p[:, e * P:(e + 1) * P], dt_w[d][:, e * P:(e + 1) * P],
                                     dtT[0:RANK + 1, :], start=True, stop=True)
                ins.then_inc(v_mm, 1)

            def y_start(d, ps):
                eng.wait_ge(d_done, ps + 1)
                for e in range(ET):
                    ins = eng.matmul(ps_p[:, e * P:(e + 1) * P], u2[:, e, :], diag[d][:, e, :],
                                     start=True, stop=True)
                ins.then_inc(yi_mm, 1)

            def z_in(d, es):
                eng.wait_ge(xne_in, es * 16 + 16)
                eng.wait_ge(o_sb, es)
                for k in range(KD):
                    ins = eng.matmul(ps_e[:, :], xnE[:, k, :], in_w[d][:, k, E:2 * E],
                                     start=(k == 0), stop=(k == KD - 1))
                ins.then_inc(z_mm, 1)

            def yg_turn(es):
                eng.wait_ge(sz_done, es + 1)
                eng.wait_ge(yg_done, es + 1)
                for e in range(ET):
                    ins = eng.transpose(ps_e[:, e * P:(e + 1) * P], yg[:, e * P:(e + 1) * P], ident)
                ins.then_inc(ygT_mm, 1)

            def out_proj(d, es):
                eng.wait_ge(ygT_sb, es + 1)
                for e in range(ET):
                    ins = eng.matmul(ps_e[:, 0:D], ygT[:, e * P:(e + 1) * P], out_w[d][:, e, :],
                                     start=(e == 0), stop=(e == ET - 1))
                ins.then_inc(o_mm, 1)

            def slots_turn(g):
                eng.wait_ge(xb_in, g * 16 + 16)
                eng.wait_ge(ybr_sb, g)
                for k in range(KD):
                    for j in range(2):
                        o = k * CH + j * CR
                        ins = eng.transpose(ps_m[1][:, o:o + CR], xbr[:, j, k * P:(k + 1) * P], ident[0:CR, 0:CR])
                ins.then_inc(xbT_mm, 1)

            def gate_or_up(w, g, i, up):
                eng.wait_ge(xbT_sb, g + 1)
                if not up:
                    eng.wait_ge(gs_done, g * 4 + i)
                    if i == 0:
                        eng.wait_ge(ybT_sb, g)
                else:
                    eng.wait_ge(tu_done, g * 4 + i)
                for f in range(2):
                    c0 = up * FF + (2 * i + f) * P
                    for k in range(KD):
                        ins = eng.matmul(ps_m[up][:, f * CH:(f + 1) * CH], w12[w][:, k, c0:c0 + P],
                                         xbT[:, k, :], start=(k == 0), stop=(k == KD - 1))
                ins.then_inc(u_mm if up else g_mm, 1)

            def down(w, g, k):
                if k == 0:
                    eng.wait_ge(hm_done, g * 4 + 4)
                for f in range(FB):
                    ins = eng.matmul(ps_m[0][:, k * CH:(k + 1) * CH], w3[w][:, f, k * P:(k + 1) * P],
                                     hm[:, f, :], start=(f == 0), stop=(f == FB - 1))
                if k == KD - 1:
                    ins.then_inc(ybT_mm, 1)

            def rows_turn(g):
                eng.wait_ge(ybT_sb, g + 1)
                for j in range(2):
                    for k in range(KD):
                        o = j * D + k * P
                        ins = eng.transpose(ps_m[1][0:CR, o:o + P], ybT[:, k, j * CR:(j + 1) * CR], ident)
                ins.then_inc(ybr_mm, 1)

            for ps in range(TT):
                xi_in(0, ps)
                proj(0, ps)
                v_in(0, ps)
                y_start(0, ps)

            eng.sem_inc(ht_ready, HT0)

            def turn_states(g, n, tt):
                if tt == 0:
                    eng.wait_ge(scan_done, g * 16 + (4 * n + 4 + SCAN0))
                eng.wait_ge(stt_done, g * 16 + (4 * n + tt + STT0 - 1))
                for e in range(ET):
                    ins = eng.transpose(ps_hT[tt % 2][:, e * P:(e + 1) * P], h[n % 2][:, e, tt * P:(tt + 1) * P], ident)
                ins.then_inc(ht_ready, 1)

            def unit(b, uu, epi, pro):
                pd, ed, w = DIR[(uu + 1) % UNITS], DIR[(uu - 1) % UNITS], uu // 2
                if uu % 2 == 0:
                    held(w_in[w], b * (32 * FB) + 32 * FB)
                def iteration(q):
                    g = first_g(b, uu) + q
                    ps, es = g + TT, g - TT if epi else None
                    for s in range((NPI + 1) * ET):
                        if s == 0:
                            slots_turn(g)
                            if pro:
                                xi_in(pd, ps)
                            if epi:
                                z_in(ed, es)
                        if s in (1, 3):
                            gate_or_up(w, g, s // 2, 0)
                            gate_or_up(w, g, s // 2, 1)
                        if s >= ET:
                            turn_states(g, (s - ET) // TT, (s - ET) % TT)
                        if s in (5, 6, 7, 8):
                            gate_or_up(w, g, (s - 5) // 2 + 2, (s - 5) % 2)
                        if s == 9:
                            if pro:
                                proj(pd, ps)
                            if epi:
                                yg_turn(es)
                        if s == 10:
                            down(w, g, 0)
                        if s == 11 and pro:
                            v_in(pd, ps)
                        if s == 12:
                            down(w, g, 1)
                        if s == 13 and epi:
                            out_proj(ed, es)
                        if s == 14 and pro:
                            y_start(pd, ps)
                        if s == 15:
                            rows_turn(g)

                repeat(eng, b, uu, iteration)

            run(eng, unit)

            for q in range(TT):
                es = ITERS - TT + q
                z_in(1, es)
                yg_turn(es)
                out_proj(1, es)

        @block.vector
        def _(eng):
            held = holder(eng, "dve")
            eng.wait_ge(s_const, 16 * 4)

            def stepper(base):
                count = [0]

                def step(ins):
                    ins.then_inc(s_step, 1)
                    count[0] += 1
                    eng.wait_ge(s_step, base + count[0])
                return step, count

            STEPS = 15

            def inverse_root(src, r, grp, step):
                for t in range(GT):
                    ins = eng.bn_stats(st6[:, t, :], src[:, t, :])
                step(ins)
                eng.sem_inc(gates["dve"], 1)
                for t in range(GT):
                    ins = eng.bn_aggr(mv[:, t, :], st6[:, t, :])
                step(ins)
                eng.tensor_scalar(ve, mv[:, :, 1], EPS, None, ALU.add).then_inc(s_var, 1)
                eng.wait_ge(s_sd, grp * 2 + (r + 1))
                step(eng.reciprocal(rs, sd))
                step(eng.tensor_tensor(nt, rs, rs, ALU.mult))
                step(eng.tensor_tensor(nt, nt, ve, ALU.mult))
                step(eng.tensor_scalar(nt, nt, -0.5, 1.5, ALU.mult, ALU.add))
                step(eng.tensor_tensor(rs, rs, nt, ALU.mult))

            def first_pair(k2, first):
                for i in range(2):
                    grp = k2 * 2 + i
                    step, count = stepper(grp * STEPS)
                    eng.wait_ge(s_x[i], k2 * 16 + 16)
                    inverse_root(xg[i], 0, grp, step)
                    for t in range(GT):
                        ins = eng.tensor_scalar(xg[i][:, t, :], xg[i][:, t, :], mv[:, t, 0:1], rs[:, t:t + 1],
                                                ALU.subtract, ALU.mult)
                    step(ins)
                    inverse_root(xg[i], 1, grp, step)
                    assert count[0] == STEPS
                    if not first:
                        eng.wait_ge(s_xfc, grp - 1)
                    for t in range(GT):
                        ins = eng.scalar_tensor_tensor(out=xfg[i][:, t, :], in0=xg[i][:, t, :],
                                                       scalar=mv[:, t, 0:1], in1=gam, op0=ALU.subtract,
                                                       op1=ALU.mult)
                    ins.then_inc(s_scaled, 1)
                    eng.wait_ge(s_scaled, grp + 1)
                    for t in range(GT):
                        ins = eng.scalar_tensor_tensor(out=xfg[i][:, t, :], in0=xfg[i][:, t, :],
                                                       scalar=rs[:, t:t + 1], in1=bet, op0=ALU.mult,
                                                       op1=ALU.add)
                    ins.then_inc(s_xf, 1)

            GROUPS = TILES // GT
            first_pair(0, True)
            with eng.Fori(1, GROUPS // 2) as k2:
                first_pair(k2, False)

            step, _ = stepper(GROUPS * STEPS)
            eng.wait_ge(s_lg, TILES)
            step(eng.tensor_scalar(lg.rearrange("p t e -> p (t e)"), ps_m[0][:, 0:TILES * EX], CLAMP, -CLAMP,
                                   ALU.min, ALU.max))
            for t in range(TILES):
                ins = eng.max(out=m8[:, t, :], in_=lg[:, t, :])
            step(ins)
            i8u = i8.bitcast(U32)
            for t in range(TILES):
                ins = eng.max_index(out=i8u[:, t, :], in_max=m8[:, t, :], in_values=lg[:, t, :])
            step(ins)
            for k in range(2):
                step(eng.tensor_copy(ixf[:, k, :], i8u[:, :, k]))
            iota = iota8.rearrange("p (a e) -> p a e", a=1).broadcast_to([P, TILES, EX])
            for k in range(2):
                one = ixf[:, k, :].rearrange("p (t a) -> p t a", a=1).broadcast_to([P, TILES, EX])
                step(eng.tensor_tensor(oh[k], iota, one, ALU.is_equal))
            eng.tensor_tensor(both, oh[0], oh[1], ALU.add).then_inc(s_places, 1)
            step(eng.tensor_tensor(ev[:, 1, :], m8[:, :, 1], m8[:, :, 0], ALU.subtract))
            eng.nop().then_inc(s_dif, 1)
            eng.wait_ge(s_cum, 1)
            step(eng.tensor_copy(tot.rearrange("p t e -> p (t e)"), ps_p[:, 0:TILES * EX]))
            for e in range(EX):
                ins = eng.tensor_tensor_scan(pos[:, :, e], ones[:, 0:TILES], tot[:, :, e], 0.0, ALU.mult, ALU.add)
            step(ins)
            step(eng.tensor_tensor(pos, pos, tot, ALU.subtract))
            step(eng.tensor_tensor(pos, pos, ps_m[1][:, 0:TILES * EX].rearrange("p (t e) -> p t e", t=TILES), ALU.add))
            for k in range(2):
                step(eng.tensor_tensor(prod, pos, oh[k], ALU.mult))
                step(eng.tensor_reduce(slf[:, k, :], prod, AX_X, ALU.add))
            step(eng.tensor_scalar(kp, slf, float(CAP), None, ALU.is_lt))
            step(eng.scalar_tensor_tensor(out=slf, in0=ixf, scalar=float(CAP), in1=slf, op0=ALU.mult, op1=ALU.add))
            step(eng.tensor_scalar(slot_ga[:], slf, float(SLOTS - 1), None, ALU.min))
            step(eng.tensor_scalar(ixf, kp, -2.0 * SLOTS, 2.0 * SLOTS, ALU.mult, ALU.add))
            eng.tensor_tensor(slot_sc[:], slf, ixf, ALU.add).then_inc(s_slot, 1)
            eng.wait_ge(s_exp, 1)
            step(eng.tensor_scalar(rsum, ev[:, 0, :], 1.0, 1e-12, ALU.add, ALU.add))
            step(eng.reciprocal(rsum, rsum))
            step(eng.tensor_tensor(ev[:, 1, :], ev[:, 0, :], rsum, ALU.mult))
            step(eng.tensor_tensor(gate_w[:, 0, :], rsum, kp[:, 0, :], ALU.mult))
            step(eng.tensor_tensor(gate_w[:, 1, :], ev[:, 1, :], kp[:, 1, :], ALU.mult))
            eng.wait_ge(s_w, 16 * 16)
            for d in range(2):
                for e in range(ET):
                    ins = eng.tensor_scalar(diag[d][:, e, :], ident, dp[d][:, e:e + 1], 0.5, ALU.mult, ALU.mult)
            ins.then_inc(s_diag, 1)

            def conv_tap(d, k, ps, starts):
                if k == 0:
                    eng.wait_ge(xi_sb, ps + 1)
                    eng.wait_ge(halo, ps)
                    eng.wait_ge(halo0, starts)
                    eng.wait_ge(u2_done, ps)
                else:
                    eng.wait_ge(tap, ps * TAPS + k)
                off = k if d == 0 else HALO - k
                for e in range(ET):
                    rest = cv_b[d][:, e:e + 1].broadcast_to([P, P]) if k == 0 else cv[:, e, :]
                    ins = eng.scalar_tensor_tensor(out=cv[:, e, :], in0=xi[:, e, off:off + P],
                                                   scalar=cv_w[d][:, e, k:k + 1], in1=rest,
                                                   op0=ALU.mult, op1=ALU.add)
                ins.then_inc(tap, 1)

            def make_u2(ps):
                eng.wait_ge(th_done, ps + 1)
                eng.wait_ge(yi_mm, ps)
                eng.wait_ge(du_done, ps)
                eng.scalar_tensor_tensor(out=u2[:], in0=th[:], scalar=1.0, in1=cv[:], op0=ALU.add,
                                         op1=ALU.mult).then_inc(u2_done, 1)

            def delta(uu, q, ps):
                held(sp_step, ps * 3 + 3)
                tt = pro_tt(uu, q)
                eng.scalar_tensor_tensor(out=dT[uu % 2][:, :, bass.ds(tt * P, P)],
                                         in0=ps_p[:, :].rearrange("p (e t) -> p e t", e=ET), scalar=0.0,
                                         in1=sp[:], op0=ALU.max, op1=ALU.add).then_inc(d_done, 1)

            def silu_z(es):
                eng.wait_ge(tz_done, es + 1)
                eng.scalar_tensor_tensor(out=sz[:], in0=sz[:], scalar=1.0, in1=ps_e[:, :], op0=ALU.add,
                                         op1=ALU.mult).then_inc(sz_done, 1)

            def times_up(g, i):
                eng.wait_ge(tg_done, g * 4 + (i + 1))
                eng.wait_ge(u_mm, g * 4 + (i + 1))
                eng.scalar_tensor_tensor(out=tu[:], in0=tg[:], scalar=1.0, in1=ps_m[1][:, 0:2 * CH],
                                         op0=ALU.add, op1=ALU.mult).then_inc(tu_done, 1)

            for ps in range(TT):
                for k in range(TAPS):
                    conv_tap(0, k, ps, 1)
                make_u2(ps)
                delta(0, ps, ps)
            eng.wait_ge(s_scat, 32 * TILES)
            eng.sem_inc(scan_done, SCAN0)
            eng.sem_inc(stt_done, STT0)

            def unit(b, uu, epi, pro):
                par, d, g0 = uu % 2, DIR[uu], first_g(b, uu)
                starts = b * 2 + ((uu + 1) // 2 + 1)
                held(yi_done, g0 + TT)
                held(proj_sb, g0 * 3 + 3 * TT)
                flip = slice(None) if d == 0 else slice(None, None, -1)
                def iteration(q):
                    g = g0 + q
                    ps, es = g + TT, g - TT if epi else None

                    def scan(n, e):
                        s = n * ET + e
                        eng.wait_ge(a_ready, g * 16 + (s + 1))
                        if s % 2 == 0:
                            eng.wait_ge(b_ready, g * 8 + (s // 2 + 1))
                        if e == 0:
                            eng.wait_ge(ht_ready, g * 16 + 4 * n)
                            eng.wait_ge(saved, g * 4 + n)
                        init = state[:, bass.ds(q * NPI + n, 1), e] if uu % 2 == 1 else 0.0
                        eng.tensor_tensor_scan(h[n % 2][:, e, flip], ps_a[s % 2][:, flip],
                                               bm[s // 2 % 2][:, e % 2, flip], init, ALU.mult, ALU.add)\
                           .then_inc(scan_done, 1)

                    def add_state(n, tt):
                        k = n * TT + tt
                        eng.wait_ge(ht_ready, g * 16 + (k + 1 + HT0))
                        eng.wait_ge(stt_done, g * 16 + (k + 1))
                        eng.scalar_tensor_tensor(out=y[par][:, tt, :], in0=ps_hT[tt % 2][:, :],
                                                 scalar=c_t[par][:, tt, bass.ds(q * NPI + n, 1)],
                                                 in1=y[par][:, tt, :], op0=ALU.mult, op1=ALU.add)\
                           .then_inc(stt_done, 1)

                    for s in range((NPI + 1) * ET):
                        if s < NPI * ET:
                            scan(s // ET, s % ET)
                        if s >= ET:
                            add_state((s - ET) // TT, (s - ET) % TT)
                        if s in (3, 5, 7, 9):
                            times_up(g, (s - 3) // 2)
                        if s in (2, 3) and pro:
                            conv_tap(DIR[(uu + 1) % UNITS], 2 * s - 4, ps, starts)
                            conv_tap(DIR[(uu + 1) % UNITS], 2 * s - 3, ps, starts)
                        if s == 4 and epi:
                            silu_z(es)
                        if s == 6 and pro:
                            make_u2(ps)
                        if s == 13 and pro:
                            delta((uu + 1) % UNITS, q, ps)

                repeat(eng, b, uu, iteration)

            run(eng, unit)

            for q in range(TT):
                silu_z(ITERS - TT + q)

            def last_pair(k2, first):
                for i in range(2):
                    t = k2 * 2 + i
                    eng.wait_ge(f_in[i], k2 * 48 + 48)
                    if not first:
                        eng.wait_ge(f_out[i], k2 * 16)
                    eng.tensor_tensor(fo[i], fin[i][1], fin[i][2], ALU.add).then_inc(f_dve, 1)
                    eng.wait_ge(f_dve, t * 4 + 1)
                    eng.tensor_tensor(fo[i], fo[i], fin[i][0], ALU.add).then_inc(f_dve, 1)
                    eng.wait_ge(f_ga[i], k2 * 32 + 32)
                    for k in range(2):
                        eng.wait_ge(f_dve, t * 4 + (k + 2))
                        eng.scalar_tensor_tensor(out=fo[i], in0=fga[i][k], scalar=gate_w[:, k, bass.ds(t, 1)],
                                                 in1=fo[i], op0=ALU.mult, op1=ALU.add).then_inc(f_dve, 1)

            last_pair(0, True)
            with eng.Fori(1, TILES // 2) as k2:
                last_pair(k2, False)


_MAMBA = ("in_w", "conv_w", "conv_b", "xproj", "dt_w", "A_log", "Dp", "out_w")


def _laid_out(inputs):
    def rows(a):
        return np.ascontiguousarray(a.reshape(ET, P, -1).transpose(1, 0, 2))

    pre = {k: np.asarray(v) for k, v in inputs.items()}
    got = {
        "x": pre["L0_attn_x"].reshape(TILES, P, D),
        "ln_g": pre["L0_ffn_ln_gamma"],
        "ln_b": pre["L0_ffn_ln_beta"],
        "routerT": pre["L0_ffn_router_w"].T,
        "w12T": pre["L0_ffn_w12"].transpose(0, 2, 1),
        "w3T": pre["L0_ffn_w3"].transpose(0, 2, 1),
        "const": np.concatenate([np.eye(P), np.triu(np.ones((P, P)), 1), np.tile(np.arange(EX), (P, 1))], 1)
                   .astype(np.float32),
    }
    for side, name in enumerate(("fwd", "bwd")):
        w = {k: pre[f"L0_attn_{name}_{k}"] for k in
             ("in_w", "conv_w", "conv_b", "xproj_w", "dt_w", "dt_b", "A_log", "Dp", "out_w")}
        pad = np.zeros((E, BROW - RANK), np.float32)
        parts = {
            "in_w": w["in_w"],
            "conv_w": rows(w["conv_w"]),
            "conv_b": rows(w["conv_b"])[:, :, 0],
            "xproj": np.concatenate([w["xproj_w"][:, :RANK], pad, w["xproj_w"][:, RANK:]], 1),
            "dt_w": np.concatenate([w["dt_w"], w["dt_b"][None, :]], 0),
            "A_log": rows(w["A_log"]).transpose(0, 2, 1),
            "Dp": rows(w["Dp"])[:, :, 0],
            "out_w": w["out_w"],
        }
        for k in _MAMBA:
            got[f"{k}{side}"] = parts[k]
    return {k: np.ascontiguousarray(v) for k, v in got.items()}


def kernel(**inputs):
    import concourse.bacc as _bacc
    from concourse.bass_utils import run_bass_kernel_spmd as _run

    nc = _bacc.Bacc("TRN2", target_bir_lowering=False, num_devices=1)
    arrays, aps = {}, {}
    for name, a in _laid_out(inputs).items():
        arrays[f"in_{name}"] = a
        aps[name] = nc.dram_tensor(f"in_{name}", a.shape, mybir.dt.from_np(a.dtype), kind="ExternalInput").ap()
    out = nc.dram_tensor("out_0", (TILES, P, D), F32, kind="ExternalOutput").ap()
    mamba = [{k: aps[f"{k}{d}"] for k in _MAMBA} for d in range(2)]
    mixed_block(nc, aps["x"], aps["ln_g"], aps["ln_b"], aps["routerT"], aps["w12T"], aps["w3T"], mamba,
                aps["const"], out)
    r = _run(nc, [arrays], core_ids=[0])
    return r.results[0]["out_0"].reshape(BATCH, L, D)
```

```python
from collections import namedtuple
from contextlib import ExitStack

import numpy as np

import concourse.bass as bass
from concourse import mybir

F32 = mybir.dt.float32
I32 = mybir.dt.int32
U32 = mybir.dt.uint32
ALU = mybir.AluOpType
ACT = mybir.ActivationFunctionType
AX_X = mybir.AxisListType.X

P = 128
BATCH, L, D = 4, 1024, 256
E = 512
ET = E // P
KD = D // P
NS = 16
RANK = 16
TAPS = 4
HALO = TAPS - 1
H = 512
TT = H // P
TILES = BATCH * L // P
UNITS = 4
DIR = (0, 0, 1, 1)
HALF = (0, 1, 1, 0)
EX, CAP, FF = 8, 1280, 1024
FB = FF // P
CH = 160
CR = CH // 2
ITERS = BATCH * UNITS * TT
SLOTS = EX * CAP
NPI = NS // TT
CLAMP = 10000.0
EPS = 1e-5
BROW = 32
GT = 4

SCAN0 = 2
STT0 = 4
HT0 = 4

STEPS = NPI * ET

Iteration = namedtuple("Iteration", "b uu q g epi pro")

PE_AT = dict(xi=-4, proj=7, v=10, y=15, z=6, turn=14, out=(16, 17), slots=0,
             gate=(8, 10, 12, 14), up=(9, 11, 13, 15), down=(18, 19, 20, 21), rows=23)
ACT_AT = dict(xi=0, tanh=8, proj=11, softplus=14, log=15, y=18, z=10, turn=18, out=21, slots=4,
              gate=(11, 13, 15, 17), down=25, rows=27)
DVE_AT = dict(taps=(1, 2, 3, 4), u2=6, delta=13, z=8, up=(10, 12, 14, 16))
POOL_AT = dict(halo=3, du=(7, 7), gated=5, hidden=(6, 7, 8, 9))


def mixed_block(nc, x, ln_g, ln_b, routerT, w12T, w3T, mamba, const, out):
    ctx = ExitStack()
    with ctx:
        def sb(name, shape, dt=F32):
            return ctx.enter_context(nc.sbuf_tensor(name, shape, dt))

        def sem(name):
            return ctx.enter_context(nc.semaphore(name))

        def dram(name, shape):
            return nc.dram_tensor(name, shape, F32).ap()

        xnT_d = dram("xnT_d", (TILES, P, KD, P))
        xb_d = dram("xb_d", (SLOTS, D))
        yb_d = dram("yb_d", (SLOTS, D))
        bT_d = dram("bT_d", (2, NS, H))
        yd_d = dram("yd_d", (2, TILES, P, D))

        def bank(name):
            return ctx.enter_context(nc.psum_tensor(name, [P, 512], F32))

        ps_a = bank("ps_a")
        ps_x = bank("ps_x")
        ps_hT = [bank("ps_hT0"), bank("ps_hT1")]
        ps_m = [bank("ps_m0"), bank("ps_m1")]
        ps_p = bank("ps_p")
        ps_e = bank("ps_e")

        cst = sb("cst", [P, P + EX])
        ident = cst[:, 0:P]
        iota8 = cst[:, P:P + EX]
        in_w = [sb(f"in_w{d}", [P, KD, 2 * E]) for d in range(2)]
        xp_w = [sb(f"xp_w{d}", [P, ET, BROW + 2 * NS]) for d in range(2)]
        dt_w = [sb(f"dt_w{d}", [RANK + 1, E]) for d in range(2)]
        cv_w = [sb(f"cv_w{d}", [P, ET, TAPS]) for d in range(2)]
        cv_b = [sb(f"cv_b{d}", [P, ET]) for d in range(2)]
        dp = [sb(f"dp{d}", [P, ET]) for d in range(2)]
        diag = [sb(f"diag{d}", [P, ET, P]) for d in range(2)]
        negA = [sb(f"negA{d}", [P, NS, ET]) for d in range(2)]
        out_w = [sb(f"out_w{d}", [P, ET, D]) for d in range(2)]
        wmoe = [sb(f"wmoe{i}", [P, KD * 2 * FF + FB * D]) for i in range(2)]
        w12 = [w[:, 0:KD * 2 * FF].rearrange("p (k f) -> p k f", k=KD) for w in wmoe]
        w3 = [w[:, KD * 2 * FF:].rearrange("p (j n) -> p j n", j=FB) for w in wmoe]
        gate_w = sb("gate_w", [P, 2, TILES])
        slot_sc = sb("slot_sc", [P, 2, TILES], I32)
        slot_ga = sb("slot_ga", [P, 2, TILES], I32)

        dT = [sb(f"dT{i}", [P, ET, H]) for i in range(2)]
        duT = [sb(f"duT{i}", [P, ET, H]) for i in range(2)]
        hy = sb("hy", [P, 2 * ET * H + 2 * TT * E])
        h = [hy[:, i * ET * H:(i + 1) * ET * H].rearrange("p (e t) -> p e t", e=ET) for i in range(2)]
        y = [hy[:, (2 + i) * ET * H:(3 + i) * ET * H].rearrange("p (t e) -> p t e", t=TT)
             for i in range(2)]
        xf_all = hy[:, 0:TILES * D].rearrange("p (t d) -> p t d", t=TILES)
        bm = [sb(f"bm{i}", [P, 2, H]) for i in range(2)]
        ex = [ps_a] + [sb(f"ex{i}", [P, H]) for i in (1, 2, 3)]
        bbc = sb("bbc", [P, 2, NPI, H])
        c_t = [sb(f"c_t{i}", [P, TT, NS]) for i in range(2)]
        state = sb("state", [P, NS, ET])

        xnP = sb("xnP", [P, KD, P])
        xi = sb("xi", [P, ET, P + HALO])
        cv = sb("cv", [P, ET, P])
        th = sb("th", [P, ET, P])
        u2 = cv
        dtb = sb("dtb", [BROW + NS, P])
        dtT, bs = dtb[0:BROW, :], dtb
        sp = th

        xnE = sb("xnE", [P, KD, P])
        sz = sb("sz", [P, E])
        yg = sz
        ygT = sb("ygT", [P, E])
        o_sbuf = ygT[:, 0:D]

        xbr = sb("xbr", [CR, 2, D])
        xbT = sb("xbT", [P, KD, CH])
        tg = [sb(f"tg{i}", [P, 2 * CH]) for i in range(2)]
        tu = tg
        gs = [sb(f"gs{i}", [P, 2 * CH]) for i in range(2)]
        hm = sb("hm", [P, FB, CH])
        ybT = sb("ybT", [P, KD, CH])
        ybr = sb("ybr", [CR, 2 * D])

        taken = {}

        def view(owner, n):
            at = taken.get(owner.name, 0)
            taken[owner.name] = at + n
            flat = owner[:, :, :].rearrange("p a b -> p (a b)") if len(owner.shape) == 3 else owner[:, :]
            assert at + n <= flat.shape[1]
            return flat[:, at:at + n]

        def tiles_of(ap, n):
            return ap.rearrange("p (t s) -> p t s", t=n)

        xg = [tiles_of(view(dT[1], GT * D), GT) for _ in range(2)]
        xfg = [tiles_of(view(duT[1], GT * D), GT) for _ in range(2)]
        spare = wmoe[1]
        lnT = [view(spare, 2 * D) for _ in range(2)]
        gam, bet = view(spare, D), view(spare, D)
        st6 = tiles_of(view(spare, 6 * GT), GT)
        mv = tiles_of(view(spare, 2 * GT), GT)
        ve, sd, rs, nt = [view(spare, GT) for _ in range(4)]
        lg, both, tot, pos = [tiles_of(view(spare, TILES * EX), TILES) for _ in range(4)]
        m8, i8, prod = [tiles_of(view(spare, TILES * EX), TILES) for _ in range(3)]
        oh = [tiles_of(view(spare, TILES * EX), TILES) for _ in range(2)]
        ones, below = view(spare, P), view(spare, P)
        rt = tiles_of(view(spare, KD * EX), KD)
        ixf, slf, kp = [tiles_of(view(spare, 2 * TILES), 2) for _ in range(3)]
        ev = tiles_of(view(spare, 2 * TILES), 2)
        rsum = view(spare, TILES)
        fin = [[view(wmoe[0], D) for _ in range(3)] for _ in range(2)]
        fga = [[view(wmoe[0], D) for _ in range(2)] for _ in range(2)]
        fo = [view(wmoe[0], D) for _ in range(2)]

        s_const, s_w = sem("s_const"), sem("s_w")
        s_zero, s_zfill, s_neg, s_diag, s_mem = sem("s_zero"), sem("s_zfill"), sem("s_neg"), sem("s_diag"), sem("s_mem")
        s_x = [sem("s_x0"), sem("s_x1")]
        s_var, s_sd, s_step, s_xf, s_xfc = sem("s_var"), sem("s_sd"), sem("s_step"), sem("s_xf"), sem("s_xfc")
        s_lnT, s_lnTs, s_lg = sem("s_lnT"), sem("s_lnTs"), sem("s_lg")
        s_xst = [sem("s_xst0"), sem("s_xst1")]
        s_scaled, s_cum, s_dif, s_exp, s_slot, s_scat = (sem("s_scaled"), sem("s_cum"), sem("s_dif"), sem("s_exp"),
                                                        sem("s_slot"), sem("s_scat"))
        s_places = sem("s_places")
        a_ready, scan_done, b_ready = sem("a_ready"), sem("scan_done"), sem("b_ready")
        ht_ready, stt_done, saved, bbc_in = sem("ht_ready"), sem("stt_done"), sem("saved"), sem("bbc_in")
        xnp_in, xi_mm, xi_sb, tap, halo = sem("xnp_in"), sem("xi_mm"), sem("xi_sb"), sem("tap"), sem("halo")
        halo0, th_done, u2_done, proj_mm = sem("halo0"), sem("th_done"), sem("u2_done"), sem("proj_mm")
        proj_sb, bT_out, v_mm, sp_step = sem("proj_sb"), sem("bT_out"), sem("v_mm"), sem("sp_step")
        d_done, du_done, yi_mm, yi_done = sem("d_done"), sem("du_done"), sem("yi_mm"), sem("yi_done")
        xne_in, z_mm, tz_done, sz_done = sem("xne_in"), sem("z_mm"), sem("tz_done"), sem("sz_done")
        yg_done, ygT_mm, ygT_sb, o_mm, o_sb, o_out = (sem("yg_done"), sem("ygT_mm"), sem("ygT_sb"), sem("o_mm"),
                                                      sem("o_sb"), sem("o_out"))
        w_in = [sem("w_in0"), sem("w_in1")]
        xb_in, xbT_mm, xbT_sb, g_mm, u_mm = sem("xb_in"), sem("xbT_mm"), sem("xbT_sb"), sem("g_mm"), sem("u_mm")
        tg_done, gs_done, tu_done, hm_done = sem("tg_done"), sem("gs_done"), sem("tu_done"), sem("hm_done")
        ybT_mm, ybT_sb, ybr_mm, ybr_sb, yb_out = (sem("ybT_mm"), sem("ybT_sb"), sem("ybr_mm"), sem("ybr_sb"),
                                                  sem("yb_out"))
        f_in = [sem("f_in0"), sem("f_in1")]
        f_ga = [sem("f_ga0"), sem("f_ga1")]
        f_dve = sem("f_dve")
        f_out = [sem("f_out0"), sem("f_out1")]
        gates = {"sp": sem("gate_sp"), "pool": sem("gate_pool"), "act": sem("gate_act"),
                 "dve": sem("gate_dve"), "pe": sem("gate_pe")}

        def holder(eng, name):
            def held(s, value):
                eng.wait_ge(s, value)
                eng.sem_inc(gates[name], 1)
            return held

        def run(eng, iteration):
            def around(b, uu, q):
                iteration(at(b, uu, q - 1), at(b, uu, q), at(b, uu, q + 1))

            def batch(b):
                for uu in range(UNITS):
                    if isinstance(b, int) and b == 0 and uu < 2:
                        for q in range(TT):
                            around(b, uu, q)
                    else:
                        around(b, uu, 0)
                        with eng.Fori(1, TT - 1) as q:
                            around(b, uu, q)
                        around(b, uu, TT - 1)

            iteration(None, None, at(0, 0, 0))
            batch(0)
            with eng.Fori(1, BATCH - 1) as b:
                batch(b)
            batch(BATCH - 1)
            iteration(at(BATCH - 1, UNITS - 1, TT - 1), None, None)

        def at(b, uu, q):
            g = first_g(b, uu) + q
            if isinstance(g, int) and not 0 <= g < ITERS:
                return None
            if isinstance(q, int):
                uu, q = uu + (q + TT) // TT - 1, q % TT
            b, uu = b + (uu + UNITS) // UNITS - 1, uu % UNITS
            first, last = (isinstance(b, int) and b == n for n in (0, BATCH - 1))
            return Iteration(b, uu, q, g, not (first and uu == 0), not (last and uu == UNITS - 1))

        def due(step, s, before, now, after):
            return (before, now, after)[1 - step // STEPS] if step % STEPS == s else None

        def first_g(b, uu):
            return b * (UNITS * TT) + uu * TT

        def order(d, q):
            return q if d == 0 else (TT - 1) - q

        def token_tile(b, uu, tt):
            return (b + uu // UNITS) * (L // P) + (HALF[uu % UNITS] * TT) + tt

        def pro_tt(uu, q):
            return order(DIR[uu % UNITS], q)

        def epi_tt(uu, q):
            return order(DIR[(uu + 2) % UNITS], q)

        block = ctx.enter_context(nc.Block())

        @block.sync
        def _(eng):
            held = holder(eng, "sp")
            eng.dma_start(cst[:, :], const[:, 0:P + EX]).then_inc(s_const, 16)
            eng.dma_start(below, const[:, P + EX:]).then_inc(s_const, 16)
            eng.dma_start(gam, ln_g.partition_broadcast(P)).then_inc(s_const, 16)
            eng.dma_start(bet, ln_b.partition_broadcast(P)).then_inc(s_const, 16)
            eng.dma_start(rt, routerT.rearrange("(k p) e -> p k e", p=P)).then_inc(s_const, 16)

            def load_x(group, i):
                eng.dma_start(xg[i], x[bass.ds(group * GT, GT)].rearrange("t p d -> p t d")).then_inc(s_x[i], 16)

            load_x(0, 0)
            load_x(1, 1)
            for d in range(2):
                m = mamba[d]
                eng.dma_start(in_w[d][:], m["in_w"].rearrange("(k p) n -> p k n", p=P)).then_inc(s_w, 16)
                eng.dma_start(xp_w[d][:], m["xproj"].rearrange("(k p) n -> p k n", p=P)).then_inc(s_w, 16)
                eng.dma_start(dt_w[d][:], m["dt_w"]).then_inc(s_w, 16)
                eng.dma_start(cv_w[d][:], m["conv_w"]).then_inc(s_w, 16)
                eng.dma_start(cv_b[d][:], m["conv_b"]).then_inc(s_w, 16)
                eng.dma_start(dp[d][:], m["Dp"]).then_inc(s_w, 16)
                eng.dma_start(negA[d][:], m["A_log"]).then_inc(s_w, 16)
                eng.dma_start(out_w[d][:], m["out_w"].rearrange("(k p) n -> p k n", p=P)).then_inc(s_w, 16)
            eng.wait_ge(s_zero, 1)
            zrows = xb_d.rearrange("(c p r) d -> c p (r d)", p=P, r=8)
            for c in range(SLOTS // (P * 8)):
                eng.dma_start(zrows[c], dT[0][:].rearrange("p e t -> p (e t)")).then_inc(s_zfill, 16)

            def load_expert_part(e, i, part):
                f = 2 * FF // FB
                eng.dma_start(w12[i][:, :, bass.ds(part * f, f)],
                              w12T[bass.ds(e, 1), :, bass.ds(part * f, f)].rearrange("a (k p) f -> p (a k) f", p=P))\
                   .then_inc(w_in[i], 16)
                eng.dma_start(w3[i][:, bass.ds(part, 1), :],
                              w3T[bass.ds(e, 1), bass.ds(part * P, P), :].rearrange("a p n -> p a n"))\
                   .then_inc(w_in[i], 16)

            for part in range(FB):
                load_expert_part(0, 0, part)

            def first_pair(k2, last):
                for i in range(2):
                    for t in range(GT):
                        k = k2 * (2 * GT) + (i * GT + t)
                        held(s_lnTs, k + 1)
                        eng.dma_start(xnT_d[bass.ds(k, 1)].rearrange("a p k t -> p (a k t)"),
                                      lnT[t % 2][:, 0:D]).then_inc(s_xst[t % 2], 16)
                    if not last:
                        load_x(k2 * 2 + (i + 2), i)

            with eng.Fori(0, TILES // (2 * GT) - 1) as k2:
                first_pair(k2, False)
            first_pair(TILES // (2 * GT) - 1, True)
            for i in range(2):
                eng.wait_ge(s_xst[i], 16 * (TILES // 2))

            def load_pro(b, uu, q, ps):
                held(xi_mm, ps)
                eng.dma_start(xnP[:], xnT_d[bass.ds(token_tile(b, uu, pro_tt(uu, q)), 1)]
                              .rearrange("a p k t -> p (a k) t")).then_inc(xnp_in, 16)

            def load_epi(b, uu, q, es):
                held(z_mm, es)
                eng.dma_start(xnE[:], xnT_d[bass.ds(token_tile(b, uu, epi_tt(uu, q)), 1)]
                              .rearrange("a p k t -> p (a k) t")).then_inc(xne_in, 16)

            def store_b(uu, q, ps):
                held(proj_sb, ps * 3 + 3)
                eng.dma_start(bT_d[uu % 2][:, bass.ds(pro_tt(uu, q) * P, P)], bs[BROW:BROW + NS, :])\
                   .then_inc(bT_out, 16)

            def load_bbc(uu, q, slices):
                held(bT_out, slices * 16)
                rows = bT_d[uu % 2][bass.ds(q * NPI, NPI), :].rearrange("(a n) t -> a (n t)", a=1)
                eng.dma_start(bbc[:, bass.ds(q % 2, 1)].rearrange("p a n t -> p (a n t)"),
                              rows.broadcast_to([P, NPI * H])).then_inc(bbc_in, 16)

            def load_slots(g, previous):
                held(xbT_mm, previous)
                eng.dma_start(xbr[:], xb_d[bass.ds(g * CH, CH)].rearrange("(j p) d -> p j d", p=CR))\
                   .then_inc(xb_in, 16)

            def store_epi(b, uu, q, es):
                held(o_sb, es + 1)
                eng.dma_start(yd_d[DIR[uu % UNITS]][bass.ds(token_tile(b, uu, epi_tt(uu, q)), 1)]
                              .rearrange("a p d -> p (a d)"), o_sbuf).then_inc(o_out, 16)

            load_pro(0, 0, 0, 0)
            for q in range(TT):
                store_b(0, q, q)
                load_pro(0, (q + 1) // TT, (q + 1) % TT, q + 1)
            load_bbc(0, 0, TT)
            eng.wait_ge(s_scat, 32 * TILES)
            load_slots(0, 0)

            def iteration(before, now, after):
                if now:
                    b, uu, q, g, _, _ = now
                    end = isinstance(q, int) and q == TT - 1
                    if not end:
                        held(b_ready, g * (2 * NPI)) if not (isinstance(g, int) and g == 0) else None
                        held(bbc_in, g * 16 + 16)
                        load_bbc(uu, q + 1, first_g(b, uu) + TT)
                if before and before.epi:
                    store_epi(before.b, before.uu - 1, before.q, before.g - TT)
                if now and after and after.pro:
                    load_pro(after.b, after.uu + 1, after.q, after.g + TT)
                if now:
                    if after:
                        load_slots(g + 1, g + 1)
                    if not (isinstance(b, int) and b == BATCH - 1 and uu >= 2):
                        expert0 = first_g(b, uu - uu % 2)
                        if not (isinstance(expert0, int) and expert0 == 0):
                            held(ybT_mm, expert0)
                        load_expert_part(b * 2 + (uu // 2 + 1), 1 - uu // 2, (uu % 2) * TT + q)
                    if after and after.epi:
                        load_epi(after.b, after.uu - 1, after.q, after.g - TT)
                    if not after:
                        load_epi(BATCH - 1, UNITS - 1, 0, ITERS - TT)
                if before:
                    held(ybr_sb, before.g + 1)
                    eng.dma_start(yb_d[bass.ds(before.g * CH, CH)].rearrange("(j p) d -> p j d", p=CR),
                                  ybr[:].rearrange("p (j d) -> p j d", j=2)).then_inc(yb_out, 16)
                if now and now.pro:
                    store_b(uu + 1, q, g + TT)
                if now and end and now.pro:
                    held(b_ready, g * (2 * NPI))
                    held(bbc_in, g * 16 + 16)
                    load_bbc(uu + 1, 0, g + 1 + TT)

            run(eng, iteration)

            for q in range(TT):
                es = ITERS - TT + q
                if q + 1 < TT:
                    load_epi(BATCH - 1, UNITS - 1, q + 1, es + 1)
                store_epi(BATCH - 1, UNITS - 1, q, es)

            eng.wait_ge(o_out, 16 * ITERS)
            eng.wait_ge(yb_out, 16 * ITERS)

            def last_pair(k2, first):
                for i in range(2):
                    t = k2 * 2 + i
                    if not first:
                        held(f_dve, t * 4 - 4)
                    eng.dma_start(fin[i][0], x[bass.ds(t, 1)].rearrange("a p d -> p (a d)")).then_inc(f_in[i], 16)
                    for d in range(2):
                        eng.dma_start(fin[i][1 + d], yd_d[d][bass.ds(t, 1)].rearrange("a p d -> p (a d)"))\
                           .then_inc(f_in[i], 16)

            last_pair(0, True)
            with eng.Fori(1, TILES // 2) as k2:
                last_pair(k2, False)
            for i in range(2):
                eng.wait_ge(f_out[i], 16 * (TILES // 2))

        @block.gpsimd
        def _(eng):
            held = holder(eng, "pool")
            eng.memset(dT[0][:], 0.0).then_inc(s_zero, 1)
            eng.memset(ones, 1.0).then_inc(s_mem, 1)
            eng.memset(dtT, 1.0).then_inc(s_mem, 1)

            eng.wait_ge(s_slot, 1)
            eng.wait_ge(s_xfc, TILES // GT)
            eng.wait_ge(s_zfill, 16 * (SLOTS // (P * 8)))
            for t in range(TILES):
                for k in range(2):
                    eng.indirect_dma_start(xb_d, bass.IndirectOffsetOnAxis(ap=slot_sc[:, k, t:t + 1], axis=0),
                                           xf_all[:, t, :], None, bounds_check=SLOTS - 1, oob_is_err=False)\
                       .then_inc(s_scat, 16)
            eng.wait_ge(s_w, 16 * 16)

            def zero_halo(d):
                eng.memset(xi[:, :, 0:HALO] if d == 0 else xi[:, :, P:P + HALO], 0.0).then_inc(halo0, 1)

            def move_halo(d, ps):
                held(tap, ps * TAPS + TAPS)
                tail, head = xi[:, :, P:P + HALO], xi[:, :, 0:HALO]
                src, dst = (tail, head) if d == 0 else (head, tail)
                eng.tensor_copy(dst, src).then_inc(halo, 1)

            def make_du(uu, q, ps, i):
                half = slice(2 * i, 2 * i + 2)
                held(d_done, ps + 1)
                held(u2_done, ps + 1)
                tt = pro_tt(uu, q)
                part = bass.ds(tt * P, P)
                eng.tensor_tensor(duT[uu % 2][:, half, part], dT[uu % 2][:, half, part], u2[:, half, :], ALU.mult)\
                   .then_inc(du_done, 1)

            def gate_y(uu, q, es, unit_end):
                held(sz_done, es + 1)
                held(stt_done, unit_end)
                tt = epi_tt(uu, q)
                eng.tensor_tensor(yg[:], y[uu % 2][:, bass.ds(tt, 1), :].rearrange("p a e -> p (a e)"), sz[:],
                                  ALU.mult).then_inc(yg_done, 1)

            def times_gate(g, i):
                held(tu_done, g * 4 + (i + 1))
                held(gs_done, g * 4 + (i + 1))
                if i == 0:
                    held(ybT_mm, g)
                eng.tensor_tensor(hm[:, 2 * i:2 * i + 2, :].rearrange("p f c -> p (f c)"), tu[i % 2][:], gs[i % 2][:],
                                  ALU.mult).then_inc(hm_done, 1)

            zero_halo(0)
            for ps in range(TT):
                move_halo(0, ps)
                for i in range(2):
                    make_du(0, ps, ps, i)

            def save(it, n):
                held(scan_done, it.g * 16 + (4 * n + 4 + SCAN0))
                col = H - 1 if DIR[it.uu] == 0 else 0
                eng.tensor_copy(state[:, bass.ds(it.q * NPI + n, 1), :],
                                h[n % 2][:, :, col:col + 1].rearrange("p e a -> p a e")).then_inc(saved, 1)

            def iteration(before, now, after):
                if now and isinstance(now.q, int) and now.q == 0:
                    held(du_done, 2 * now.g + 2 * TT)
                for j in range(2 * NPI):
                    if now:
                        b, uu, q, g, _, _ = now
                        n, half = j // 2, j % 2
                        if j == 0:
                            held(bbc_in, g * 16 + 16)
                        if j or not (isinstance(g, int) and g == 0):
                            held(scan_done, g * 16 + 2 * j)
                        eng.tensor_tensor(bm[j % 2][:], duT[uu % 2][:, 2 * half:2 * half + 2, :],
                                          bbc[:, bass.ds(q % 2, 1), n, :].broadcast_to([P, 2, H]),
                                          ALU.mult).then_inc(b_ready, 1)
                    if j == 0 and before:
                        save(before, NPI - 1)
                    if j in (3, 5, 7) and now:
                        save(now, (j - 3) // 2)
                    near = [2 * j, before, now, after]
                    for i, step in enumerate(POOL_AT["hidden"]):
                        it = due(2 * step, *near)
                        if it:
                            times_gate(it.g, i)
                    it = due(2 * POOL_AT["halo"], *near)
                    if it and it.pro:
                        d = DIR[(it.uu + 1) % UNITS]
                        move_halo(d, it.g + TT)
                        if it.uu % 2 == 0 and isinstance(it.q, int) and it.q == TT - 1:
                            held(halo, it.g + (TT + 1))
                            zero_halo(DIR[(it.uu + 2) % UNITS])
                    for i, step in enumerate(POOL_AT["du"]):
                        it = due(2 * step, *near)
                        if it and it.pro:
                            make_du((it.uu + 1) % UNITS, it.q, it.g + TT, i)
                    it = due(2 * POOL_AT["gated"], *near)
                    if it and it.epi:
                        gate_y((it.uu - 1) % UNITS, it.q, it.g - TT, first_g(it.b, it.uu) * NS + STT0)

            run(eng, iteration)

            for q in range(TT):
                gate_y(UNITS - 1, q, ITERS - TT + q, ITERS * NS + STT0)

            eng.wait_ge(yb_out, 16 * ITERS)
            for t in range(TILES):
                if t >= 2:
                    eng.wait_ge(f_dve, 4 * (t - 1))
                for k in range(2):
                    eng.indirect_dma_start(fga[t % 2][k], None, yb_d,
                                           bass.IndirectOffsetOnAxis(ap=slot_ga[:, k, t:t + 1], axis=0))\
                       .then_inc(f_ga[t % 2], 16)
            for i in range(2):
                eng.wait_ge(f_ga[i], 32 * (TILES // 2))

        @block.scalar
        def _(eng):
            held = holder(eng, "act")

            def first_pair(k2, first):
                for i in range(2):
                    grp = k2 * 2 + i
                    for r in range(2):
                        held(s_var, grp * 2 + (r + 1))
                        eng.activation(sd, ve, ACT.Sqrt).then_inc(s_sd, 1)
                    held(s_xf, grp + 1)
                    eng.activation(xf_all[:, bass.ds(grp * GT, GT), :], xfg[i], ACT.Copy).then_inc(s_xfc, 1)
                    for t in range(GT):
                        k = grp * GT + t
                        held(s_lnT, k + 1)
                        if not (first and i == 0 and t < 2):
                            held(s_xst[t % 2], grp * (8 * GT) + (t // 2) * 16)
                            held(s_lg, k - 1)
                        eng.activation(lnT[t % 2], ps_hT[t % 2][:, :], ACT.Copy).then_inc(s_lnTs, 1)

            first_pair(0, True)
            with eng.Fori(1, TILES // (2 * GT)) as k2:
                first_pair(k2, False)

            eng.wait_ge(s_dif, 1)
            eng.activation(ev[:, 0, :], ev[:, 1, :], ACT.Exp).then_inc(s_exp, 1)
            eng.wait_ge(s_w, 16 * 16)
            for d in range(2):
                eng.activation(negA[d][:], negA[d][:], ACT.Exp).then_inc(s_neg, 1)
            eng.wait_ge(s_neg, 2)
            for d in range(2):
                eng.activation(negA[d][:], negA[d][:], ACT.Copy, scale=-1.0).then_inc(s_neg, 1)
            eng.wait_ge(s_neg, 4)
            eng.wait_ge(s_scat, 32 * TILES)
            eng.wait_ge(s_zfill, 16 * (SLOTS // (P * 8)))

            def xi_out(d, ps):
                held(xi_mm, ps + 1)
                held(halo, ps)
                lo = HALO if d == 0 else 0
                eng.activation(xi[:, :, lo:lo + P], ps_x[:, :].rearrange("p (e t) -> p e t", e=ET), ACT.Copy)\
                   .then_inc(xi_sb, 1)

            def tanh_conv(ps):
                held(tap, ps * TAPS + TAPS)
                held(u2_done, ps)
                eng.activation(th[:], cv[:], ACT.Tanh, scale=0.5).then_inc(th_done, 1)

            def proj_out(uu, q, ps):
                held(proj_mm, ps + 1)
                held(v_mm, ps)
                eng.activation(dtT[0:RANK, :], ps_x[0:RANK, 0:P], ACT.Copy, scale=0.5).then_inc(proj_sb, 1)
                held(bT_out, ps * 16)
                eng.activation(bs[BROW:BROW + NS, :], ps_x[BROW:BROW + NS, 0:P], ACT.Copy, scale=0.25)\
                   .then_inc(proj_sb, 1)
                eng.activation(c_t[uu % 2][:, bass.ds(pro_tt(uu, q), 1), :].rearrange("p a n -> p (a n)"),
                               ps_x[:, P:P + NS], ACT.Copy, scale=0.5).then_inc(proj_sb, 1)

            def softplus_out(ps):
                flat = ps_p[:, :].rearrange("p (e t) -> p e t", e=ET)
                held(v_mm, ps + 1)
                held(d_done, ps)
                eng.activation(sp[:], flat, ACT.Abs).then_inc(sp_step, 1)
                held(sp_step, ps * 3 + 1)
                eng.activation(sp[:], sp[:], ACT.Exp, scale=-1.0).then_inc(sp_step, 1)

            def softplus_log(ps):
                held(sp_step, ps * 3 + 2)
                eng.activation(sp[:], sp[:], ACT.Ln, bias=1.0).then_inc(sp_step, 1)

            def y_init(uu, q, ps, es):
                held(yi_mm, ps + 1)
                if es is not None:
                    held(yg_done, es + 1)
                eng.activation(y[uu % 2][:, bass.ds(pro_tt(uu, q), 1), :].rearrange("p a e -> p (a e)"),
                               ps_p[:, :], ACT.Copy).then_inc(yi_done, 1)

            def tanh_z(es):
                held(z_mm, es + 1)
                held(ygT_mm, es)
                eng.activation(sz[:], ps_e[:, :], ACT.Tanh, scale=0.5).then_inc(tz_done, 1)

            def ygT_out(es):
                held(ygT_mm, es + 1)
                held(o_out, es * 16)
                eng.activation(ygT[:], ps_e[:, :], ACT.Copy, scale=0.5).then_inc(ygT_sb, 1)

            def o_out_sb(es):
                held(o_mm, es + 1)
                eng.activation(o_sbuf, ps_e[:, 0:D], ACT.Copy).then_inc(o_sb, 1)

            def xbT_out(g):
                held(xbT_mm, g + 1)
                held(u_mm, g * 4)
                eng.activation(xbT[:], ps_m[1][:, 0:KD * CH].rearrange("p (k c) -> p k c", k=KD), ACT.Copy)\
                   .then_inc(xbT_sb, 1)

            def tanh_g(g, i):
                held(g_mm, g * 4 + (i + 1))
                if i >= 2 or not (isinstance(g, int) and g == 0):
                    held(hm_done, g * 4 + (i - 1))
                eng.activation(tg[i % 2][:], ps_m[0][:, 0:2 * CH], ACT.Tanh, scale=0.5).then_inc(tg_done, 1)
                eng.activation(gs[i % 2][:], ps_m[0][:, 0:2 * CH], ACT.Copy, scale=0.5).then_inc(gs_done, 1)

            def ybT_out(g):
                held(ybT_mm, g + 1)
                held(ybr_mm, g)
                eng.activation(ybT[:], ps_m[0][:, 0:KD * CH].rearrange("p (k c) -> p k c", k=KD), ACT.Copy)\
                   .then_inc(ybT_sb, 1)

            def ybr_out(g):
                held(ybr_mm, g + 1)
                held(yb_out, g * 16)
                eng.activation(ybr[:], ps_m[1][0:CR, :], ACT.Copy).then_inc(ybr_sb, 1)

            for ps in range(TT):
                xi_out(0, ps)
                tanh_conv(ps)
                proj_out(0, ps, ps)
                softplus_out(ps)
                softplus_log(ps)
                y_init(0, ps, ps, None)

            def iteration(before, now, after):
                if now and isinstance(now.q, int) and now.q == 0:
                    held(d_done, now.g + TT)
                for s in range(STEPS):
                    if now:
                        b, uu, q, g, _, _ = now
                        n, e = s // ET, s % ET
                        if s > 1 or not (isinstance(g, int) and g == 0):
                            held(scan_done, g * 16 + (s - 1))
                        eng.activation(ex[s % 4][:, :], dT[uu % 2][:, e, :], ACT.Exp,
                                       scale=negA[DIR[uu]][:, bass.ds(q * NPI + n, 1), e]).then_inc(a_ready, 1)
                    near = [s, before, now, after]
                    it = due(ACT_AT["slots"], *near)
                    if it:
                        xbT_out(it.g)
                    it = due(ACT_AT["down"], *near)
                    if it:
                        ybT_out(it.g)
                    it = due(ACT_AT["rows"], *near)
                    if it:
                        ybr_out(it.g)
                    for i, step in enumerate(ACT_AT["gate"]):
                        it = due(step, *near)
                        if it:
                            tanh_g(it.g, i)
                    it = due(ACT_AT["y"], *near)
                    if it and it.pro:
                        y_init((it.uu + 1) % UNITS, it.q, it.g + TT, it.g - TT if it.epi else None)
                    it = due(ACT_AT["xi"], *near)
                    if it and it.pro:
                        xi_out(DIR[(it.uu + 1) % UNITS], it.g + TT)
                    it = due(ACT_AT["tanh"], *near)
                    if it and it.pro:
                        tanh_conv(it.g + TT)
                    it = due(ACT_AT["proj"], *near)
                    if it and it.pro:
                        held(stt_done, first_g(it.b, it.uu) * NS + STT0)
                        proj_out((it.uu + 1) % UNITS, it.q, it.g + TT)
                    it = due(ACT_AT["softplus"], *near)
                    if it and it.pro:
                        softplus_out(it.g + TT)
                    it = due(ACT_AT["log"], *near)
                    if it and it.pro:
                        softplus_log(it.g + TT)
                    it = due(ACT_AT["z"], *near)
                    if it and it.epi:
                        tanh_z(it.g - TT)
                    it = due(ACT_AT["turn"], *near)
                    if it and it.epi:
                        ygT_out(it.g - TT)
                    it = due(ACT_AT["out"], *near)
                    if it and it.epi:
                        o_out_sb(it.g - TT)

            run(eng, iteration)

            for q in range(TT):
                es = ITERS - TT + q
                tanh_z(es)
                ygT_out(es)
                o_out_sb(es)

            with eng.Fori(0, TILES // 2) as k2:
                for i in range(2):
                    t = k2 * 2 + i
                    held(f_dve, t * 4 + 4)
                    eng.dma_start(out[bass.ds(t, 1)].rearrange("a p d -> p (a d)"), fo[i]).then_inc(f_out[i], 16)

        @block.tensor
        def _(eng):
            held = holder(eng, "pe")
            eng.wait_ge(s_const, 16 * 5)

            def first_pair(k2, first):
                for i in range(2):
                    grp = k2 * 2 + i
                    eng.wait_ge(s_xf, grp + 1)
                    for t in range(GT):
                        k = grp * GT + t
                        if not (first and i == 0 and t < 2):
                            eng.wait_ge(s_lnTs, k - 1)
                        for j, src in enumerate((xg[i], xfg[i])):
                            for c in range(KD):
                                o = (j * KD + c) * P
                                ins = eng.transpose(ps_hT[t % 2][:, o:o + P], src[:, t, c * P:(c + 1) * P], ident)
                        ins.then_inc(s_lnT, 1)
                        if not (first and i == 0 and t == 0):
                            logits(grp * GT + (t - 1), (t + 1) % 2)

            def logits(k, par):
                eng.wait_ge(s_lnTs, k + 1)
                for c in range(KD):
                    ins = eng.matmul(ps_m[0][:, bass.ds(k * EX, EX)], lnT[par][:, D + c * P:D + (c + 1) * P],
                                     rt[:, c, :], start=(c == 0), stop=(c == KD - 1))
                ins.then_inc(s_lg, 1)

            first_pair(0, True)
            with eng.Fori(1, TILES // (2 * GT)) as k2:
                first_pair(k2, False)
            logits(TILES - 1, 1)

            eng.wait_ge(s_places, 1)
            eng.wait_ge(s_mem, 2)
            flat = both.rearrange("p t e -> p (t e)")
            eng.matmul(ps_m[1][:, 0:TILES * EX], below, flat, start=True, stop=True)
            eng.matmul(ps_p[:, 0:TILES * EX], ones, flat, start=True, stop=True).then_inc(s_cum, 1)
            eng.wait_ge(s_w, 16 * 16)
            eng.wait_ge(s_diag, 1)

            def xi_in(d, ps):
                eng.wait_ge(xnp_in, ps * 16 + 16)
                eng.wait_ge(proj_sb, ps * 3)
                for e in range(ET):
                    for k in range(KD):
                        ins = eng.matmul(ps_x[:, e * P:(e + 1) * P], in_w[d][:, k, e * P:(e + 1) * P],
                                         xnP[:, k, :], start=(k == 0), stop=(k == KD - 1))
                ins.then_inc(xi_mm, 1)

            def proj(d, ps):
                eng.wait_ge(u2_done, ps + 1)
                eng.wait_ge(xi_sb, ps + 1)
                for e in range(ET):
                    eng.matmul(ps_x[0:BROW + NS, 0:P], xp_w[d][:, e, 0:BROW + NS], u2[:, e, :],
                               start=(e == 0), stop=(e == ET - 1))
                for e in range(ET):
                    ins = eng.matmul(ps_x[:, P:P + NS], u2[:, e, :], xp_w[d][:, e, BROW + NS:],
                                     start=(e == 0), stop=(e == ET - 1))
                ins.then_inc(proj_mm, 1)

            def v_in(d, ps):
                eng.wait_ge(proj_sb, ps * 3 + 3)
                eng.wait_ge(yi_done, ps)
                for e in range(ET):
                    ins = eng.matmul(ps_p[:, e * P:(e + 1) * P], dt_w[d][:, e * P:(e + 1) * P],
                                     dtT[0:RANK + 1, :], start=True, stop=True)
                ins.then_inc(v_mm, 1)

            def y_start(d, ps):
                eng.wait_ge(d_done, ps + 1)
                for e in range(ET):
                    ins = eng.matmul(ps_p[:, e * P:(e + 1) * P], u2[:, e, :], diag[d][:, e, :],
                                     start=True, stop=True)
                ins.then_inc(yi_mm, 1)

            def z_in(d, es):
                eng.wait_ge(xne_in, es * 16 + 16)
                eng.wait_ge(o_sb, es)
                for k in range(KD):
                    ins = eng.matmul(ps_e[:, :], xnE[:, k, :], in_w[d][:, k, E:2 * E],
                                     start=(k == 0), stop=(k == KD - 1))
                ins.then_inc(z_mm, 1)

            def yg_turn(es):
                eng.wait_ge(sz_done, es + 1)
                eng.wait_ge(yg_done, es + 1)
                for e in range(ET):
                    ins = eng.transpose(ps_e[:, e * P:(e + 1) * P], yg[:, e * P:(e + 1) * P], ident)
                ins.then_inc(ygT_mm, 1)

            def out_proj(d, es, i):
                if i == 0:
                    eng.wait_ge(ygT_sb, es + 1)
                for e in (2 * i, 2 * i + 1):
                    ins = eng.matmul(ps_e[:, 0:D], ygT[:, e * P:(e + 1) * P], out_w[d][:, e, :],
                                     start=(e == 0), stop=(e == ET - 1))
                if i == 1:
                    ins.then_inc(o_mm, 1)

            def slots_turn(g):
                eng.wait_ge(xb_in, g * 16 + 16)
                eng.wait_ge(tu_done, g * 4)
                for k in range(KD):
                    for j in range(2):
                        o = k * CH + j * CR
                        ins = eng.transpose(ps_m[1][:, o:o + CR], xbr[:, j, k * P:(k + 1) * P], ident[0:CR, 0:CR])
                ins.then_inc(xbT_mm, 1)

            def gate_or_up(w, g, i, up):
                eng.wait_ge(xbT_sb, g + 1)
                if not up:
                    eng.wait_ge(gs_done, g * 4 + i)
                    if i == 0:
                        eng.wait_ge(ybT_sb, g)
                else:
                    eng.wait_ge(tu_done, g * 4 + i)
                    if i == 0:
                        eng.wait_ge(ybr_sb, g)
                for f in range(2):
                    c0 = up * FF + (2 * i + f) * P
                    for k in range(KD):
                        ins = eng.matmul(ps_m[up][:, f * CH:(f + 1) * CH], w12[w][:, k, c0:c0 + P],
                                         xbT[:, k, :], start=(k == 0), stop=(k == KD - 1))
                ins.then_inc(u_mm if up else g_mm, 1)

            def down(w, g, i):
                k = i // 2
                if i == 0:
                    eng.wait_ge(gs_done, g * 4 + 4)
                if i < 2:
                    eng.wait_ge(hm_done, g * 4 + (2 * i + 2))
                for f in range(i % 2 * (FB // 2), (i % 2 + 1) * (FB // 2)):
                    ins = eng.matmul(ps_m[0][:, k * CH:(k + 1) * CH], w3[w][:, f, k * P:(k + 1) * P],
                                     hm[:, f, :], start=(f == 0), stop=(f == FB - 1))
                if i == 3:
                    ins.then_inc(ybT_mm, 1)

            def rows_turn(g):
                eng.wait_ge(ybT_sb, g + 1)
                eng.wait_ge(xbT_sb, min(g + 2, ITERS) if isinstance(g, int) else g + 2)
                for j in range(2):
                    for k in range(KD):
                        o = j * D + k * P
                        ins = eng.transpose(ps_m[1][0:CR, o:o + P], ybT[:, k, j * CR:(j + 1) * CR], ident)
                ins.then_inc(ybr_mm, 1)

            for ps in range(TT):
                xi_in(0, ps)
                proj(0, ps)
                v_in(0, ps)
                y_start(0, ps)

            eng.sem_inc(ht_ready, HT0)

            def turn_states(g, n, tt):
                if tt == 0:
                    eng.wait_ge(scan_done, g * 16 + (4 * n + 4 + SCAN0))
                eng.wait_ge(stt_done, g * 16 + (4 * n + tt + STT0 - 1))
                for e in range(ET):
                    ins = eng.transpose(ps_hT[tt % 2][:, e * P:(e + 1) * P], h[n % 2][:, e, tt * P:(tt + 1) * P], ident)
                ins.then_inc(ht_ready, 1)

            def iteration(before, now, after):
                if now and now.uu % 2 == 0 and isinstance(now.q, int) and now.q == 0:
                    held(w_in[now.uu // 2], now.b * (32 * FB) + 32 * FB)
                for s in range(STEPS):
                    it = before if s < ET else now
                    if it:
                        turn_states(it.g, (s // ET - 1) % NPI, s % ET)
                    near = [s, before, now, after]
                    it = due(PE_AT["slots"], *near)
                    if it:
                        slots_turn(it.g)
                    for i, step in enumerate(PE_AT["down"]):
                        it = due(step, *near)
                        if it:
                            down(it.uu // 2, it.g, i)
                    it = due(PE_AT["rows"], *near)
                    if it:
                        rows_turn(it.g)
                    it = due(PE_AT["z"], *near)
                    if it and it.epi:
                        z_in(DIR[(it.uu - 1) % UNITS], it.g - TT)
                    it = due(PE_AT["turn"], *near)
                    if it and it.epi:
                        yg_turn(it.g - TT)
                    for i, step in enumerate(PE_AT["out"]):
                        it = due(step, *near)
                        if it and it.epi:
                            out_proj(DIR[(it.uu - 1) % UNITS], it.g - TT, i)
                    for up, name in enumerate(("gate", "up")):
                        for i, step in enumerate(PE_AT[name]):
                            it = due(step, *near)
                            if it:
                                gate_or_up(it.uu // 2, it.g, i, up)
                    it = due(PE_AT["proj"], *near)
                    if it and it.pro:
                        proj(DIR[(it.uu + 1) % UNITS], it.g + TT)
                    it = due(PE_AT["v"], *near)
                    if it and it.pro:
                        v_in(DIR[(it.uu + 1) % UNITS], it.g + TT)
                    it = due(PE_AT["y"], *near)
                    if it and it.pro:
                        y_start(DIR[(it.uu + 1) % UNITS], it.g + TT)
                    it = due(PE_AT["xi"], *near)
                    if it and it.pro:
                        xi_in(DIR[(it.uu + 1) % UNITS], it.g + TT)

            run(eng, iteration)

            for q in range(TT):
                es = ITERS - TT + q
                z_in(1, es)
                yg_turn(es)
                for i in range(2):
                    out_proj(1, es, i)

        @block.vector
        def _(eng):
            held = holder(eng, "dve")
            eng.wait_ge(s_const, 16 * 5)

            def stepper(base):
                count = [0]

                def step(ins):
                    ins.then_inc(s_step, 1)
                    count[0] += 1
                    eng.wait_ge(s_step, base + count[0])
                return step, count

            LN_STEPS = 15

            def inverse_root(src, r, grp, step):
                for t in range(GT):
                    ins = eng.bn_stats(st6[:, t, :], src[:, t, :])
                step(ins)
                eng.sem_inc(gates["dve"], 1)
                for t in range(GT):
                    ins = eng.bn_aggr(mv[:, t, :], st6[:, t, :])
                step(ins)
                eng.tensor_scalar(ve, mv[:, :, 1], EPS, None, ALU.add).then_inc(s_var, 1)
                eng.wait_ge(s_sd, grp * 2 + (r + 1))
                step(eng.reciprocal(rs, sd))
                step(eng.tensor_tensor(nt, rs, rs, ALU.mult))
                step(eng.tensor_tensor(nt, nt, ve, ALU.mult))
                step(eng.tensor_scalar(nt, nt, -0.5, 1.5, ALU.mult, ALU.add))
                step(eng.tensor_tensor(rs, rs, nt, ALU.mult))

            def first_pair(k2, first):
                for i in range(2):
                    grp = k2 * 2 + i
                    step, count = stepper(grp * LN_STEPS)
                    eng.wait_ge(s_x[i], k2 * 16 + 16)
                    inverse_root(xg[i], 0, grp, step)
                    for t in range(GT):
                        ins = eng.tensor_scalar(xg[i][:, t, :], xg[i][:, t, :], mv[:, t, 0:1], rs[:, t:t + 1],
                                                ALU.subtract, ALU.mult)
                    step(ins)
                    inverse_root(xg[i], 1, grp, step)
                    assert count[0] == LN_STEPS
                    if not first:
                        eng.wait_ge(s_xfc, grp - 1)
                    for t in range(GT):
                        ins = eng.scalar_tensor_tensor(out=xfg[i][:, t, :], in0=xg[i][:, t, :],
                                                       scalar=mv[:, t, 0:1], in1=gam, op0=ALU.subtract,
                                                       op1=ALU.mult)
                    ins.then_inc(s_scaled, 1)
                    eng.wait_ge(s_scaled, grp + 1)
                    for t in range(GT):
                        ins = eng.scalar_tensor_tensor(out=xfg[i][:, t, :], in0=xfg[i][:, t, :],
                                                       scalar=rs[:, t:t + 1], in1=bet, op0=ALU.mult,
                                                       op1=ALU.add)
                    ins.then_inc(s_xf, 1)

            GROUPS = TILES // GT
            first_pair(0, True)
            with eng.Fori(1, GROUPS // 2) as k2:
                first_pair(k2, False)

            step, _ = stepper(GROUPS * LN_STEPS)
            eng.wait_ge(s_lg, TILES)
            step(eng.tensor_scalar(lg.rearrange("p t e -> p (t e)"), ps_m[0][:, 0:TILES * EX], CLAMP, -CLAMP,
                                   ALU.min, ALU.max))
            for t in range(TILES):
                ins = eng.max(out=m8[:, t, :], in_=lg[:, t, :])
            step(ins)
            i8u = i8.bitcast(U32)
            for t in range(TILES):
                ins = eng.max_index(out=i8u[:, t, :], in_max=m8[:, t, :], in_values=lg[:, t, :])
            step(ins)
            for k in range(2):
                step(eng.tensor_copy(ixf[:, k, :], i8u[:, :, k]))
            iota = iota8.rearrange("p (a e) -> p a e", a=1).broadcast_to([P, TILES, EX])
            for k in range(2):
                one = ixf[:, k, :].rearrange("p (t a) -> p t a", a=1).broadcast_to([P, TILES, EX])
                step(eng.tensor_tensor(oh[k], iota, one, ALU.is_equal))
            eng.tensor_tensor(both, oh[0], oh[1], ALU.add).then_inc(s_places, 1)
            step(eng.tensor_tensor(ev[:, 1, :], m8[:, :, 1], m8[:, :, 0], ALU.subtract))
            eng.nop().then_inc(s_dif, 1)
            eng.wait_ge(s_cum, 1)
            step(eng.tensor_copy(tot.rearrange("p t e -> p (t e)"), ps_p[:, 0:TILES * EX]))
            for e in range(EX):
                ins = eng.tensor_tensor_scan(pos[:, :, e], ones[:, 0:TILES], tot[:, :, e], 0.0, ALU.mult, ALU.add)
            step(ins)
            step(eng.tensor_tensor(pos, pos, tot, ALU.subtract))
            step(eng.tensor_tensor(pos, pos, ps_m[1][:, 0:TILES * EX].rearrange("p (t e) -> p t e", t=TILES), ALU.add))
            for k in range(2):
                step(eng.tensor_tensor(prod, pos, oh[k], ALU.mult))
                step(eng.tensor_reduce(slf[:, k, :], prod, AX_X, ALU.add))
            step(eng.tensor_scalar(kp, slf, float(CAP), None, ALU.is_lt))
            step(eng.scalar_tensor_tensor(out=slf, in0=ixf, scalar=float(CAP), in1=slf, op0=ALU.mult, op1=ALU.add))
            step(eng.tensor_scalar(slot_ga[:], slf, float(SLOTS - 1), None, ALU.min))
            step(eng.tensor_scalar(ixf, kp, -2.0 * SLOTS, 2.0 * SLOTS, ALU.mult, ALU.add))
            eng.tensor_tensor(slot_sc[:], slf, ixf, ALU.add).then_inc(s_slot, 1)
            eng.wait_ge(s_exp, 1)
            step(eng.tensor_scalar(rsum, ev[:, 0, :], 1.0, 1e-12, ALU.add, ALU.add))
            step(eng.reciprocal(rsum, rsum))
            step(eng.tensor_tensor(ev[:, 1, :], ev[:, 0, :], rsum, ALU.mult))
            step(eng.tensor_tensor(gate_w[:, 0, :], rsum, kp[:, 0, :], ALU.mult))
            step(eng.tensor_tensor(gate_w[:, 1, :], ev[:, 1, :], kp[:, 1, :], ALU.mult))
            eng.wait_ge(s_w, 16 * 16)
            for d in range(2):
                for e in range(ET):
                    ins = eng.tensor_scalar(diag[d][:, e, :], ident, dp[d][:, e:e + 1], 0.5, ALU.mult, ALU.mult)
            ins.then_inc(s_diag, 1)

            def conv_tap(d, k, ps, starts):
                if k == 0:
                    eng.wait_ge(xi_sb, ps + 1)
                    eng.wait_ge(halo, ps)
                    eng.wait_ge(halo0, starts)
                    eng.wait_ge(yi_mm, ps)
                    eng.wait_ge(du_done, 2 * ps)
                else:
                    eng.wait_ge(tap, ps * TAPS + k)
                off = k if d == 0 else HALO - k
                for e in range(ET):
                    rest = cv_b[d][:, e:e + 1].broadcast_to([P, P]) if k == 0 else cv[:, e, :]
                    ins = eng.scalar_tensor_tensor(out=cv[:, e, :], in0=xi[:, e, off:off + P],
                                                   scalar=cv_w[d][:, e, k:k + 1], in1=rest,
                                                   op0=ALU.mult, op1=ALU.add)
                ins.then_inc(tap, 1)

            def make_u2(ps):
                eng.wait_ge(th_done, ps + 1)
                eng.scalar_tensor_tensor(out=u2[:], in0=th[:], scalar=1.0, in1=cv[:], op0=ALU.add,
                                         op1=ALU.mult).then_inc(u2_done, 1)

            def delta(uu, q, ps):
                held(sp_step, ps * 3 + 3)
                tt = pro_tt(uu, q)
                eng.scalar_tensor_tensor(out=dT[uu % 2][:, :, bass.ds(tt * P, P)],
                                         in0=ps_p[:, :].rearrange("p (e t) -> p e t", e=ET), scalar=0.0,
                                         in1=sp[:], op0=ALU.max, op1=ALU.add).then_inc(d_done, 1)

            def silu_z(es):
                eng.wait_ge(tz_done, es + 1)
                eng.scalar_tensor_tensor(out=sz[:], in0=sz[:], scalar=1.0, in1=ps_e[:, :], op0=ALU.add,
                                         op1=ALU.mult).then_inc(sz_done, 1)

            def times_up(g, i):
                eng.wait_ge(tg_done, g * 4 + (i + 1))
                eng.wait_ge(u_mm, g * 4 + (i + 1))
                eng.scalar_tensor_tensor(out=tu[i % 2][:], in0=tg[i % 2][:], scalar=1.0, in1=ps_m[1][:, 0:2 * CH],
                                         op0=ALU.add, op1=ALU.mult).then_inc(tu_done, 1)

            for ps in range(TT):
                for k in range(TAPS):
                    conv_tap(0, k, ps, 1)
                make_u2(ps)
                delta(0, ps, ps)
            eng.wait_ge(s_scat, 32 * TILES)
            eng.sem_inc(scan_done, SCAN0)
            eng.sem_inc(stt_done, STT0)

            def scan(it, n, e):
                s = n * ET + e
                flip = slice(None) if DIR[it.uu] == 0 else slice(None, None, -1)
                eng.wait_ge(a_ready, it.g * 16 + (s + 1))
                if s % 2 == 0:
                    eng.wait_ge(b_ready, it.g * 8 + (s // 2 + 1))
                if e == 0:
                    eng.wait_ge(ht_ready, it.g * 16 + 4 * n)
                    if n or not (isinstance(it.g, int) and it.g == 0):
                        eng.wait_ge(saved, it.g * 4 + (n - 1))
                init = state[:, bass.ds(it.q * NPI + n, 1), e] if it.uu % 2 == 1 else 0.0
                eng.tensor_tensor_scan(h[n % 2][:, e, flip], ex[s % 4][:, flip],
                                       bm[s // 2 % 2][:, e % 2, flip], init, ALU.mult, ALU.add)\
                   .then_inc(scan_done, 1)

            def add_state(it, n, tt):
                k = n * TT + tt
                par = it.uu % 2
                if k == 0 and isinstance(it.q, int) and it.q == 0:
                    eng.wait_ge(yi_done, it.g + TT)
                    held(proj_sb, it.g * 3 + 3 * TT)
                eng.wait_ge(ht_ready, it.g * 16 + (k + 1 + HT0))
                eng.wait_ge(stt_done, it.g * 16 + (k + 1))
                eng.scalar_tensor_tensor(out=y[par][:, tt, :], in0=ps_hT[tt % 2][:, :],
                                         scalar=c_t[par][:, tt, bass.ds(it.q * NPI + n, 1)],
                                         in1=y[par][:, tt, :], op0=ALU.mult, op1=ALU.add)\
                   .then_inc(stt_done, 1)

            def iteration(before, now, after):
                for s in range(STEPS):
                    if now:
                        scan(now, s // ET, s % ET)
                    it = before if s < ET else now
                    if it:
                        add_state(it, (s // ET - 1) % NPI, s % ET)
                    near = [s, before, now, after]
                    for tap_at, step in enumerate(DVE_AT["taps"]):
                        it = due(step, *near)
                        if it and it.pro:
                            starts = it.b * 2 + ((it.uu + 1) // 2 + 1)
                            conv_tap(DIR[(it.uu + 1) % UNITS], tap_at, it.g + TT, starts)
                    it = due(DVE_AT["u2"], *near)
                    if it and it.pro:
                        make_u2(it.g + TT)
                    it = due(DVE_AT["z"], *near)
                    if it and it.epi:
                        silu_z(it.g - TT)
                    for i, step in enumerate(DVE_AT["up"]):
                        it = due(step, *near)
                        if it:
                            times_up(it.g, i)
                    it = due(DVE_AT["delta"], *near)
                    if it and it.pro:
                        delta((it.uu + 1) % UNITS, it.q, it.g + TT)

            run(eng, iteration)

            for q in range(TT):
                silu_z(ITERS - TT + q)

            def last_pair(k2, first):
                for i in range(2):
                    t = k2 * 2 + i
                    eng.wait_ge(f_in[i], k2 * 48 + 48)
                    if not first:
                        eng.wait_ge(f_out[i], k2 * 16)
                    eng.tensor_tensor(fo[i], fin[i][1], fin[i][2], ALU.add).then_inc(f_dve, 1)
                    eng.wait_ge(f_dve, t * 4 + 1)
                    eng.tensor_tensor(fo[i], fo[i], fin[i][0], ALU.add).then_inc(f_dve, 1)
                    eng.wait_ge(f_ga[i], k2 * 32 + 32)
                    for k in range(2):
                        eng.wait_ge(f_dve, t * 4 + (k + 2))
                        eng.scalar_tensor_tensor(out=fo[i], in0=fga[i][k], scalar=gate_w[:, k, bass.ds(t, 1)],
                                                 in1=fo[i], op0=ALU.mult, op1=ALU.add).then_inc(f_dve, 1)

            last_pair(0, True)
            with eng.Fori(1, TILES // 2) as k2:
                last_pair(k2, False)


_MAMBA = ("in_w", "conv_w", "conv_b", "xproj", "dt_w", "A_log", "Dp", "out_w")


def _laid_out(inputs):
    def rows(a):
        return np.ascontiguousarray(a.reshape(ET, P, -1).transpose(1, 0, 2))

    pre = {k: np.asarray(v) for k, v in inputs.items()}
    got = {
        "x": pre["L0_attn_x"].reshape(TILES, P, D),
        "ln_g": pre["L0_ffn_ln_gamma"],
        "ln_b": pre["L0_ffn_ln_beta"],
        "routerT": pre["L0_ffn_router_w"].T,
        "w12T": pre["L0_ffn_w12"].transpose(0, 2, 1),
        "w3T": pre["L0_ffn_w3"].transpose(0, 2, 1),
        "const": np.concatenate([np.eye(P), np.tile(np.arange(EX), (P, 1)), np.triu(np.ones((P, P)), 1)], 1)
                   .astype(np.float32),
    }
    for side, name in enumerate(("fwd", "bwd")):
        w = {k: pre[f"L0_attn_{name}_{k}"] for k in
             ("in_w", "conv_w", "conv_b", "xproj_w", "dt_w", "dt_b", "A_log", "Dp", "out_w")}
        pad = np.zeros((E, BROW - RANK), np.float32)
        parts = {
            "in_w": w["in_w"],
            "conv_w": rows(w["conv_w"]),
            "conv_b": rows(w["conv_b"])[:, :, 0],
            "xproj": np.concatenate([w["xproj_w"][:, :RANK], pad, w["xproj_w"][:, RANK:]], 1),
            "dt_w": np.concatenate([w["dt_w"], w["dt_b"][None, :]], 0),
            "A_log": rows(w["A_log"]).transpose(0, 2, 1),
            "Dp": rows(w["Dp"])[:, :, 0],
            "out_w": w["out_w"],
        }
        for k in _MAMBA:
            got[f"{k}{side}"] = parts[k]
    return {k: np.ascontiguousarray(v) for k, v in got.items()}


def kernel(**inputs):
    import concourse.bacc as _bacc
    from concourse.bass_utils import run_bass_kernel_spmd as _run

    nc = _bacc.Bacc("TRN2", target_bir_lowering=False, num_devices=1)
    arrays, aps = {}, {}
    for name, a in _laid_out(inputs).items():
        arrays[f"in_{name}"] = a
        aps[name] = nc.dram_tensor(f"in_{name}", a.shape, mybir.dt.from_np(a.dtype), kind="ExternalInput").ap()
    out = nc.dram_tensor("out_0", (TILES, P, D), F32, kind="ExternalOutput").ap()
    mamba = [{k: aps[f"{k}{d}"] for k in _MAMBA} for d in range(2)]
    mixed_block(nc, aps["x"], aps["ln_g"], aps["ln_b"], aps["routerT"], aps["w12T"], aps["w3T"], mamba,
                aps["const"], out)
    r = _run(nc, [arrays], core_ids=[0])
    return r.results[0]["out_0"].reshape(BATCH, L, D)
```

```python
from collections import namedtuple
from contextlib import ExitStack

import numpy as np

import concourse.bass as bass
from concourse import mybir

F32 = mybir.dt.float32
I32 = mybir.dt.int32
U32 = mybir.dt.uint32
ALU = mybir.AluOpType
ACT = mybir.ActivationFunctionType
AX_X = mybir.AxisListType.X

P = 128
BATCH, L, D = 4, 1024, 256
E = 512
ET = E // P
KD = D // P
NS = 16
RANK = 16
TAPS = 4
HALO = TAPS - 1
H = 512
TT = H // P
TILES = BATCH * L // P
UNITS = 4
DIR = (0, 0, 1, 1)
HALF = (0, 1, 1, 0)
EX, CAP, FF = 8, 1280, 1024
FB = FF // P
CH = 160
CR = CH // 2
ITERS = BATCH * UNITS * TT
SLOTS = EX * CAP
NPI = NS // TT
CLAMP = 10000.0
EPS = 1e-5
BROW = RANK + NS
GT = 4
ZR = SLOTS // (2 * P * (TILES // GT))
RING = 4
SCATTERS = 4

SCAN0 = 2
STT0 = 4
HT0 = 4

STEPS = NPI * ET

Iteration = namedtuple("Iteration", "b uu q g epi pro")

PE_AT = dict(xi=-4, proj=7, v=10, c=10, y=14, z=5, turn=13, out=(16, 17), slots=2, gate=(8, 10, 13, 14),
             up=(9, 11, 13, 15), down=(17, 18, 19, 20), rows=23)
ACT_AT = dict(xi=1, conv=1, tanh=7, proj=11, c=14, softplus=14, log=14, y=19, z=10, turn=17, out=19,
              slots=3, gate=(11, 14, 16, 17), down=25, rows=27)
DVE_AT = dict(taps=(0, 1, 3), u2=5, delta=13, z=8, up=(10, 12, 14, 16))
POOL_AT = dict(halo=3, du=(7, 7), gated=5, hidden=(6, 7, 8, 9))


def mixed_block(nc, x, ln_g, ln_b, routerT, w12T, w3T, mamba, const, out):
    ctx = ExitStack()
    with ctx:
        def sb(name, shape, dt=F32):
            return ctx.enter_context(nc.sbuf_tensor(name, shape, dt))

        def sem(name):
            return ctx.enter_context(nc.semaphore(name))

        def dram(name, shape):
            return nc.dram_tensor(name, shape, F32).ap()

        xnT_d = dram("xnT_d", (TILES, P, KD, P))
        xb_d = dram("xb_d", (SLOTS, D))
        yb_d = dram("yb_d", (SLOTS, D))
        bT_d = dram("bT_d", (2, NS, H))
        yd_d = dram("yd_d", (2, TILES, P, D))

        def bank(name):
            return ctx.enter_context(nc.psum_tensor(name, [P, 512], F32))

        ps_a = bank("ps_a")
        ps_x = bank("ps_x")
        ps_hT = [bank("ps_hT0"), bank("ps_hT1")]
        ps_m = [bank("ps_m0"), bank("ps_m1")]
        ps_p = bank("ps_p")
        ps_e = bank("ps_e")

        cst = sb("cst", [P, P + EX])
        ident = cst[:, 0:P]
        iota8 = cst[:, P:P + EX]
        in_w = [sb(f"in_w{d}", [P, KD, 2 * E]) for d in range(2)]
        xp_w = [sb(f"xp_w{d}", [P, ET, BROW + NS]) for d in range(2)]
        dt_w = [sb(f"dt_w{d}", [RANK + 1, E]) for d in range(2)]
        cv_w = [sb(f"cv_w{d}", [P, ET, TAPS]) for d in range(2)]
        cv_b = [sb(f"cv_b{d}", [P, ET]) for d in range(2)]
        dp = [sb(f"dp{d}", [P, ET]) for d in range(2)]
        diag = [sb(f"diag{d}", [P, ET, P]) for d in range(2)]
        negA = [sb(f"negA{d}", [P, NS, ET]) for d in range(2)]
        out_w = [sb(f"out_w{d}", [P, ET, D]) for d in range(2)]
        wmoe = [sb(f"wmoe{i}", [P, KD * 2 * FF + FB * D]) for i in range(2)]
        w12 = [w[:, 0:KD * 2 * FF].rearrange("p (k f) -> p k f", k=KD) for w in wmoe]
        w3 = [w[:, KD * 2 * FF:].rearrange("p (j n) -> p j n", j=FB) for w in wmoe]
        gate_w = sb("gate_w", [P, 2, TILES])
        slot_sc = sb("slot_sc", [P, 2, TILES], I32)
        slot_ga = sb("slot_ga", [P, 2, TILES], I32)

        big = sb("big", [P, 2 * NPI * H + 2 * ET * H])
        bbc = big[:, 0:2 * NPI * H].rearrange("p (a n t) -> p a n t", a=2, n=NPI)
        odd = [big[:, o:o + ET * H].rearrange("p (e t) -> p e t", e=ET)
               for o in (2 * NPI * H, 2 * NPI * H + ET * H)]
        xf_all = big[:, 0:TILES * D].rearrange("p (t d) -> p t d", t=TILES)
        dT = [sb("dT0", [P, ET, H])[:, :, :], odd[0]]
        duT = [sb("duT0", [P, ET, H])[:, :, :], odd[1]]
        hy = sb("hy", [P, 2 * ET * H + 2 * TT * E])
        h = [hy[:, i * ET * H:(i + 1) * ET * H].rearrange("p (e t) -> p e t", e=ET) for i in range(2)]
        y = [hy[:, (2 + i) * ET * H:(3 + i) * ET * H].rearrange("p (t e) -> p t e", t=TT)
             for i in range(2)]
        bm = [sb(f"bm{i}", [P, 2, H]) for i in range(2)]
        ex = [ps_a] + [sb(f"ex{i}", [P, H]) for i in (1, 2, 3)]
        c_t = [sb(f"c_t{i}", [P, TT, NS]) for i in range(2)]
        state = sb("state", [P, NS, ET])

        xnP = sb("xnP", [P, KD, P])
        xi = sb("xi", [P, ET, P + HALO])
        cv = sb("cv", [P, ET, P])
        th = sb("th", [P, ET, P])
        u2 = cv
        dtb = sb("dtb", [BROW + NS, P])
        dtT, bs = dtb[0:BROW, :], dtb
        dcT = sb("dcT", [BROW, P])
        sp = th

        xnE = sb("xnE", [P, KD, P])
        sz = sb("sz", [P, E])
        yg = sz
        ygT = sb("ygT", [P, E])
        o_sbuf = ygT[:, 0:D]

        xbr = sb("xbr", [CR, 2, D])
        xbT = sb("xbT", [P, KD, CH])
        tg = [sb(f"tg{i}", [P, 2 * CH]) for i in range(2)]
        tu = tg
        gs = [sb(f"gs{i}", [P, 2 * CH]) for i in range(2)]
        hm = sb("hm", [P, FB, CH])
        ybT = sb("ybT", [P, KD, CH])
        ybr = sb("ybr", [CR, 2 * D])

        taken = {}

        def view(owner, n):
            at = taken.get(owner.name, 0)
            taken[owner.name] = at + n
            flat = owner[:, :, :].rearrange("p a b -> p (a b)") if len(owner.shape) == 3 else owner[:, :]
            assert at + n <= flat.shape[1]
            return flat[:, at:at + n]

        def tiles_of(ap, n):
            return ap.rearrange("p (t s) -> p t s", t=n)

        xg = [tiles_of(view(hy, GT * D), GT) for _ in range(2)]
        xfg = [tiles_of(view(hy, GT * D), GT) for _ in range(2)]
        spare = wmoe[1]
        lnT = [view(spare, 2 * D) for _ in range(2)]
        gam, bet = view(spare, D), view(spare, D)
        st6 = tiles_of(view(spare, 6 * GT), GT)
        mv = tiles_of(view(spare, 2 * GT), GT)
        ve, sd, rs, nt = [view(spare, GT) for _ in range(4)]
        lg, both, tot, pos = [tiles_of(view(spare, TILES * EX), TILES) for _ in range(4)]
        m8, i8, prod = [tiles_of(view(spare, TILES * EX), TILES) for _ in range(3)]
        oh = [tiles_of(view(spare, TILES * EX), TILES) for _ in range(2)]
        ones, below = view(spare, P), view(spare, P)
        rt = tiles_of(view(spare, KD * EX), KD)
        ixf, slf, kp = [tiles_of(view(spare, 2 * TILES), 2) for _ in range(3)]
        ev = tiles_of(view(spare, 2 * TILES), 2)
        rsum = view(spare, TILES)
        fin = [[view(wmoe[0], D) for _ in range(3)] for _ in range(RING)]
        fga = [[view(wmoe[0], D) for _ in range(2)] for _ in range(RING)]
        fo = [view(wmoe[0], D) for _ in range(RING)]
        end_bank = [ps_e, ps_p, ps_x, ps_a]
        end_xn = [big[:, q * D:(q + 1) * D].rearrange("p (k t) -> p k t", k=KD) for q in range(TT)]
        end_sz = [dT[0][:, q, :] for q in range(TT)]
        end_ygT = [duT[0][:, q, :] for q in range(TT)]
        end_o = [big[:, (TT + q) * D:(TT + q + 1) * D] for q in range(TT)]

        s_const, s_w = sem("s_const"), sem("s_w")
        s_zero, s_zfill, s_neg, s_diag, s_mem = sem("s_zero"), sem("s_zfill"), sem("s_neg"), sem("s_diag"), sem("s_mem")
        s_x = [sem("s_x0"), sem("s_x1")]
        s_var, s_sd, s_step, s_xf, s_xfc = sem("s_var"), sem("s_sd"), sem("s_step"), sem("s_xf"), sem("s_xfc")
        s_lnT, s_lnTs, s_lg = sem("s_lnT"), sem("s_lnTs"), sem("s_lg")
        s_xst = [sem("s_xst0"), sem("s_xst1")]
        s_scaled, s_cum, s_dif, s_exp, s_slot, s_scat = (sem("s_scaled"), sem("s_cum"), sem("s_dif"), sem("s_exp"),
                                                        sem("s_slot"),
                                                        [sem(f"s_scat{i}") for i in range(SCATTERS)])
        s_places = sem("s_places")
        SCATTERED = 16 * 2 * (TILES // SCATTERS)
        a_ready, scan_done, b_ready = sem("a_ready"), sem("scan_done"), sem("b_ready")
        ht_ready, stt_done, saved, bbc_in = sem("ht_ready"), sem("stt_done"), sem("saved"), sem("bbc_in")
        xnp_in, xi_mm, xi_sb, halo = sem("xnp_in"), sem("xi_mm"), sem("xi_sb"), sem("halo")
        tap_now, tap = sem("tap_now"), sem("tap")
        halo0, th_done, u2_done, proj_mm = sem("halo0"), sem("th_done"), sem("u2_done"), sem("proj_mm")
        c_mm, c_done = sem("c_mm"), sem("c_done")
        proj_sb, bT_out, v_mm, sp_step = sem("proj_sb"), sem("bT_out"), sem("v_mm"), sem("sp_step")
        d_done, du_done, yi_mm, yi_done = sem("d_done"), sem("du_done"), sem("yi_mm"), sem("yi_done")
        xne_in, z_mm, tz_done, sz_done = sem("xne_in"), sem("z_mm"), sem("tz_done"), sem("sz_done")
        yg_done, ygT_mm, ygT_sb, o_mm, o_sb, o_out = (sem("yg_done"), sem("ygT_mm"), sem("ygT_sb"), sem("o_mm"),
                                                      sem("o_sb"), sem("o_out"))
        w_in = [sem("w_in0"), sem("w_in1")]
        xb_in, xbT_mm, xbT_sb, g_mm, u_mm = sem("xb_in"), sem("xbT_mm"), sem("xbT_sb"), sem("g_mm"), sem("u_mm")
        tg_done, gs_done, tu_done, hm_done = sem("tg_done"), sem("gs_done"), sem("tu_done"), sem("hm_done")
        ybT_mm, ybT_sb, ybr_mm, ybr_sb, yb_out = (sem("ybT_mm"), sem("ybT_sb"), sem("ybr_mm"), sem("ybr_sb"),
                                                  sem("yb_out"))
        f_in = [sem(f"f_in{i}") for i in range(RING)]
        f_ga = [sem(f"f_ga{i}") for i in range(RING)]
        f_dve = sem("f_dve")
        f_out = [sem(f"f_out{i}") for i in range(RING)]
        gates = {"sp": sem("gate_sp"), "pool": sem("gate_pool"), "act": sem("gate_act"),
                 "dve": sem("gate_dve"), "pe": sem("gate_pe")}

        def holder(eng, name):
            def held(s, value):
                eng.wait_ge(s, value)
                eng.sem_inc(gates[name], 1)
            return held

        def run(eng, iteration):
            def around(b, uu, q):
                iteration(at(b, uu, q - 1), at(b, uu, q), at(b, uu, q + 1))

            def batch(b):
                for uu in range(UNITS):
                    if isinstance(b, int) and b == 0 and uu < 2:
                        for q in range(TT):
                            around(b, uu, q)
                    else:
                        around(b, uu, 0)
                        with eng.Fori(1, TT - 1) as q:
                            around(b, uu, q)
                        around(b, uu, TT - 1)

            iteration(None, None, at(0, 0, 0))
            batch(0)
            with eng.Fori(1, BATCH - 1) as b:
                batch(b)
            batch(BATCH - 1)
            iteration(at(BATCH - 1, UNITS - 1, TT - 1), None, None)

        def at(b, uu, q):
            g = first_g(b, uu) + q
            if isinstance(g, int) and not 0 <= g < ITERS:
                return None
            if isinstance(q, int):
                uu, q = uu + (q + TT) // TT - 1, q % TT
            b, uu = b + (uu + UNITS) // UNITS - 1, uu % UNITS
            first, last = (isinstance(b, int) and b == n for n in (0, BATCH - 1))
            return Iteration(b, uu, q, g, not (first and uu == 0), not (last and uu == UNITS - 1))

        def due(step, s, before, now, after):
            return (before, now, after)[1 - step // STEPS] if step % STEPS == s else None

        def first_g(b, uu):
            return b * (UNITS * TT) + uu * TT

        def order(d, q):
            return q if d == 0 else (TT - 1) - q

        def token_tile(b, uu, tt):
            return (b + uu // UNITS) * (L // P) + (HALF[uu % UNITS] * TT) + tt

        def pro_tt(uu, q):
            return order(DIR[uu % UNITS], q)

        def epi_tt(uu, q):
            return order(DIR[(uu + 2) % UNITS], q)

        block = ctx.enter_context(nc.Block())

        @block.sync
        def _(eng):
            held = holder(eng, "sp")
            eng.dma_start(cst[:, :], const[:, 0:P + EX]).then_inc(s_const, 16)
            eng.dma_start(below, const[:, P + EX:]).then_inc(s_const, 16)
            eng.dma_start(gam, ln_g.partition_broadcast(P)).then_inc(s_const, 16)
            eng.dma_start(bet, ln_b.partition_broadcast(P)).then_inc(s_const, 16)
            eng.dma_start(rt, routerT.rearrange("(k p) e -> p k e", p=P)).then_inc(s_const, 16)

            def load_x(group, i):
                eng.dma_start(xg[i], x[bass.ds(group * GT, GT)].rearrange("t p d -> p t d")).then_inc(s_x[i], 16)

            load_x(0, 0)
            load_x(1, 1)
            for d in range(2):
                m = mamba[d]
                eng.dma_start(in_w[d][:], m["in_w"].rearrange("(k p) n -> p k n", p=P)).then_inc(s_w, 16)
                eng.dma_start(xp_w[d][:], m["xproj"].rearrange("(k p) n -> p k n", p=P)).then_inc(s_w, 16)
                eng.dma_start(dt_w[d][:], m["dt_w"]).then_inc(s_w, 16)
                eng.dma_start(cv_w[d][:], m["conv_w"]).then_inc(s_w, 16)
                eng.dma_start(cv_b[d][:], m["conv_b"]).then_inc(s_w, 16)
                eng.dma_start(dp[d][:], m["Dp"]).then_inc(s_w, 16)
                eng.dma_start(negA[d][:], m["A_log"]).then_inc(s_w, 16)
                eng.dma_start(out_w[d][:], m["out_w"].rearrange("(k p) n -> p k n", p=P)).then_inc(s_w, 16)
            eng.wait_ge(s_zero, 1)
            zrows = xb_d.rearrange("(c p r) d -> c p (r d)", p=P, r=ZR)

            def fill_zeros(c):
                eng.dma_start(zrows[bass.ds(c, 1)].rearrange("a p n -> p (a n)"),
                              duT[0].rearrange("p e t -> p (e t)")[:, 0:ZR * D]).then_inc(s_zfill, 16)

            def load_expert_part(e, i, part):
                f = 2 * FF // FB
                eng.dma_start(w12[i][:, :, bass.ds(part * f, f)],
                              w12T[bass.ds(e, 1), :, bass.ds(part * f, f)].rearrange("a (k p) f -> p (a k) f", p=P))\
                   .then_inc(w_in[i], 16)
                eng.dma_start(w3[i][:, bass.ds(part, 1), :],
                              w3T[bass.ds(e, 1), bass.ds(part * P, P), :].rearrange("a p n -> p a n"))\
                   .then_inc(w_in[i], 16)

            def first_pair(k2, last):
                for i in range(2):
                    for t in range(GT):
                        k = k2 * (2 * GT) + (i * GT + t)
                        held(s_lnTs, k + 1)
                        eng.dma_start(xnT_d[bass.ds(k, 1)].rearrange("a p k t -> p (a k t)"),
                                      lnT[t % 2][:, 0:D]).then_inc(s_xst[t % 2], 16)
                    if not last:
                        load_x(k2 * 2 + (i + 2), i)
                    fill_zeros(k2 * 4 + 2 * i)
                    fill_zeros(k2 * 4 + (2 * i + 1))
                    load_expert_part(0, 0, k2 * 2 + i)

            first_pair(0, False)
            for i in range(2):
                eng.wait_ge(s_xst[i], 16 * GT)
            eng.dma_start(xnP[:], xnT_d[token_tile(0, 0, 0)]).then_inc(xnp_in, 16)
            with eng.Fori(1, TILES // (2 * GT) - 1) as k2:
                first_pair(k2, False)
            first_pair(TILES // (2 * GT) - 1, True)
            for i in range(2):
                eng.wait_ge(s_xst[i], 16 * (TILES // 2))

            def load_pro(b, uu, q, ps):
                held(xi_mm, ps)
                eng.dma_start(xnP[:], xnT_d[bass.ds(token_tile(b, uu, pro_tt(uu, q)), 1)]
                              .rearrange("a p k t -> p (a k) t")).then_inc(xnp_in, 16)

            def load_epi(b, uu, q, es):
                held(z_mm, es)
                eng.dma_start(xnE[:], xnT_d[bass.ds(token_tile(b, uu, epi_tt(uu, q)), 1)]
                              .rearrange("a p k t -> p (a k) t")).then_inc(xne_in, 16)

            def store_b(uu, q, ps):
                held(proj_sb, ps * 3 + 3)
                eng.dma_start(bT_d[uu % 2][:, bass.ds(pro_tt(uu, q) * P, P)], bs[BROW:BROW + NS, :])\
                   .then_inc(bT_out, 16)

            def load_bbc(uu, q, slices):
                held(bT_out, slices * 16)
                rows = bT_d[uu % 2][bass.ds(q * NPI, NPI), :].rearrange("(a n) t -> a (n t)", a=1)
                eng.dma_start(bbc[:, bass.ds(q % 2, 1)].rearrange("p a n t -> p (a n t)"),
                              rows.broadcast_to([P, NPI * H])).then_inc(bbc_in, 16)

            def load_slots(g, previous):
                held(xbT_mm, previous)
                eng.dma_start(xbr[:], xb_d[bass.ds(g * CH, CH)].rearrange("(j p) d -> p j d", p=CR))\
                   .then_inc(xb_in, 16)

            def store_epi(b, uu, q, es):
                held(o_sb, es + 1)
                eng.dma_start(yd_d[DIR[uu % UNITS]][bass.ds(token_tile(b, uu, epi_tt(uu, q)), 1)]
                              .rearrange("a p d -> p (a d)"), o_sbuf).then_inc(o_out, 16)

            for q in range(TT):
                load_pro(0, (q + 1) // TT, (q + 1) % TT, q + 1)
                store_b(0, q, q)
            eng.wait_ge(s_scat[0], SCATTERED)
            load_bbc(0, 0, TT)
            for i in range(1, SCATTERS):
                eng.wait_ge(s_scat[i], SCATTERED)
            load_slots(0, 0)

            def iteration(before, now, after):
                if now:
                    b, uu, q, g, _, _ = now
                    end = isinstance(q, int) and q == TT - 1
                    if not end:
                        if before:
                            held(b_ready, g * (2 * NPI))
                        held(bbc_in, g * 16 + 16)
                        load_bbc(uu, q + 1, first_g(b, uu) + TT)
                if before and before.epi:
                    store_epi(before.b, before.uu - 1, before.q, before.g - TT)
                if now and after and after.pro:
                    load_pro(after.b, after.uu + 1, after.q, after.g + TT)
                if now:
                    if after:
                        load_slots(g + 1, g + 1)
                    if not (isinstance(b, int) and b == BATCH - 1 and uu >= 2):
                        expert0 = first_g(b, uu - uu % 2)
                        if not (isinstance(expert0, int) and expert0 == 0):
                            held(ybT_mm, expert0)
                        load_expert_part(b * 2 + (uu // 2 + 1), 1 - uu // 2, (uu % 2) * TT + q)
                    if after and after.epi:
                        load_epi(after.b, after.uu - 1, after.q, after.g - TT)
                if before:
                    held(ybr_sb, before.g + 1)
                    eng.dma_start(yb_d[bass.ds(before.g * CH, CH)].rearrange("(j p) d -> p j d", p=CR),
                                  ybr[:].rearrange("p (j d) -> p j d", j=2)).then_inc(yb_out, 16)
                if now and now.pro:
                    store_b(uu + 1, q, g + TT)
                if now and end and now.pro:
                    held(b_ready, g * (2 * NPI))
                    held(bbc_in, g * 16 + 16)
                    load_bbc(uu + 1, 0, g + 1 + TT)
                if now and not after:
                    held(b_ready, ITERS * 2 * NPI)
                    for i in range(TT):
                        tile = token_tile(BATCH - 1, UNITS - 1, epi_tt(UNITS - 1, i))
                        eng.dma_start(end_xn[i], xnT_d[tile]).then_inc(xne_in, 16)

            run(eng, iteration)

            def store_result(t, i):
                held(f_dve, t * 4 + 4)
                eng.dma_start(out[bass.ds(t, 1)].rearrange("a p d -> p (a d)"), fo[i]).then_inc(f_out[i], 16)

            def last_tile(k, i, first):
                t = k * RING + i
                if not first:
                    store_result(t - RING, i)
                eng.dma_start(fin[i][0], x[bass.ds(t, 1)].rearrange("a p d -> p (a d)")).then_inc(f_in[i], 16)
                for d in range(2):
                    eng.dma_start(fin[i][1 + d], yd_d[d][bass.ds(t, 1)].rearrange("a p d -> p (a d)"))\
                       .then_inc(f_in[i], 16)

            eng.wait_ge(ybT_mm, first_g(BATCH - 1, 2))
            eng.wait_ge(o_out, 16 * (ITERS - TT))
            for i in range(RING):
                last_tile(0, i, True)
            early = (BATCH - 1) * (L // P) // RING
            with eng.Fori(1, early) as k:
                for i in range(RING):
                    last_tile(k, i, False)
            eng.wait_ge(o_out, 16 * ITERS)
            for k in range(early, TILES // RING):
                for i in range(RING):
                    last_tile(k, i, False)
            for i in range(RING):
                store_result(TILES - RING + i, i)
            for i in range(RING):
                eng.wait_ge(f_out[i], 16 * (TILES // RING))

        @block.gpsimd
        def _(eng):
            held = holder(eng, "pool")
            eng.memset(duT[0], 0.0).then_inc(s_zero, 1)
            eng.memset(ones, 1.0).then_inc(s_mem, 1)
            eng.memset(dtT, 1.0).then_inc(s_mem, 1)

            def zero_halo(d):
                eng.memset(xi[:, :, 0:HALO] if d == 0 else xi[:, :, P:P + HALO], 0.0).then_inc(halo0, 1)

            def move_halo(d, ps):
                held(tap, ps * HALO + HALO)
                tail, head = xi[:, :, P:P + HALO], xi[:, :, 0:HALO]
                src, dst = (tail, head) if d == 0 else (head, tail)
                eng.tensor_copy(dst, src).then_inc(halo, 1)

            def make_du(uu, q, ps, i):
                half = slice(2 * i, 2 * i + 2)
                if isinstance(ps, int) and ps == TT and i == 0:
                    for part in range(SCATTERS):
                        eng.wait_ge(s_scat[part], SCATTERED)
                held(d_done, ps + 1)
                held(u2_done, ps + 1)
                tt = pro_tt(uu, q)
                part = bass.ds(tt * P, P)
                eng.tensor_tensor(duT[uu % 2][:, half, part], dT[uu % 2][:, half, part], u2[:, half, :], ALU.mult)\
                   .then_inc(du_done, 1)

            def gate_y(uu, q, es, unit_end):
                held(sz_done, es + 1)
                held(stt_done, unit_end)
                tt = epi_tt(uu, q)
                eng.tensor_tensor(yg[:], y[uu % 2][:, bass.ds(tt, 1), :].rearrange("p a e -> p (a e)"), sz[:],
                                  ALU.mult).then_inc(yg_done, 1)

            def times_gate(g, i):
                held(tu_done, g * 4 + (i + 1))
                held(gs_done, g * 4 + (i + 1))
                if i == 0:
                    held(ybT_mm, g)
                eng.tensor_tensor(hm[:, 2 * i:2 * i + 2, :].rearrange("p f c -> p (f c)"), tu[i % 2][:], gs[i % 2][:],
                                  ALU.mult).then_inc(hm_done, 1)

            zero_halo(0)

            def first_pair(k2):
                for i in range(2):
                    grp = k2 * 2 + i
                    held(s_xf, grp + 1)
                    eng.tensor_copy(xf_all[:, bass.ds(grp * GT, GT), :], xfg[i]).then_inc(s_xfc, 1)

            with eng.Fori(0, TILES // (2 * GT)) as k2:
                first_pair(k2)

            eng.wait_ge(s_slot, 1)
            eng.wait_ge(s_xfc, TILES // GT)
            eng.wait_ge(s_zfill, 16 * (SLOTS // (P * ZR)))
            for part in range(SCATTERS):
                for t in range(part * TILES // SCATTERS, (part + 1) * TILES // SCATTERS):
                    for k in range(2):
                        eng.indirect_dma_start(xb_d, bass.IndirectOffsetOnAxis(ap=slot_sc[:, k, t:t + 1], axis=0),
                                               xf_all[:, t, :], None, bounds_check=SLOTS - 1, oob_is_err=False)\
                           .then_inc(s_scat[part], 16)

            def save(it, n):
                held(scan_done, it.g * 16 + (4 * n + 4 + SCAN0))
                col = H - 1 if DIR[it.uu] == 0 else 0
                eng.tensor_copy(state[:, bass.ds(it.q * NPI + n, 1), :],
                                h[n % 2][:, :, col:col + 1].rearrange("p e a -> p a e")).then_inc(saved, 1)

            def iteration(before, now, after):
                if now and isinstance(now.q, int) and now.q == 0:
                    held(du_done, 2 * now.g + 2 * TT)
                for j in range(2 * NPI):
                    if now:
                        b, uu, q, g, _, _ = now
                        n, half = j // 2, j % 2
                        if j == 0:
                            held(bbc_in, g * 16 + 16)
                        if j or not (isinstance(g, int) and g == 0):
                            held(scan_done, g * 16 + 2 * j)
                        eng.tensor_tensor(bm[j % 2][:], duT[uu % 2][:, 2 * half:2 * half + 2, :],
                                          bbc[:, bass.ds(q % 2, 1), n, :].broadcast_to([P, 2, H]),
                                          ALU.mult).then_inc(b_ready, 1)
                    if j == 0 and before:
                        save(before, NPI - 1)
                    if j in (3, 5, 7) and now:
                        save(now, (j - 3) // 2)
                    near = [2 * j, before, now, after]
                    for i, step in enumerate(POOL_AT["hidden"]):
                        it = due(2 * step, *near)
                        if it:
                            times_gate(it.g, i)
                    it = due(2 * POOL_AT["halo"], *near)
                    if it and it.pro:
                        d = DIR[(it.uu + 1) % UNITS]
                        move_halo(d, it.g + TT)
                        if it.uu % 2 == 0 and isinstance(it.q, int) and it.q == TT - 1:
                            held(halo, it.g + (TT + 1))
                            zero_halo(DIR[(it.uu + 2) % UNITS])
                    for i, step in enumerate(POOL_AT["du"]):
                        it = due(2 * step, *near)
                        if it and it.pro:
                            make_du((it.uu + 1) % UNITS, it.q, it.g + TT, i)
                    it = due(2 * POOL_AT["gated"], *near)
                    if it and it.epi:
                        gate_y((it.uu - 1) % UNITS, it.q, it.g - TT, first_g(it.b, it.uu) * NS + STT0)

            run(eng, iteration)

            eng.wait_ge(yb_out, 16 * ITERS)
            for t in range(TILES):
                if t == RING:
                    eng.wait_ge(stt_done, ITERS * NS + STT0)
                    for q in range(TT):
                        held(sz_done, ITERS - TT + q + 1)
                        eng.tensor_tensor(end_sz[q], y[(UNITS - 1) % 2][:, epi_tt(UNITS - 1, q), :], end_sz[q],
                                          ALU.mult).then_inc(yg_done, 1)
                if t >= RING:
                    eng.wait_ge(f_dve, 4 * (t - RING + 1))
                for k in range(2):
                    eng.indirect_dma_start(fga[t % RING][k], None, yb_d,
                                           bass.IndirectOffsetOnAxis(ap=slot_ga[:, k, t:t + 1], axis=0))\
                       .then_inc(f_ga[t % RING], 16)
            for i in range(RING):
                eng.wait_ge(f_ga[i], 32 * (TILES // RING))

        @block.scalar
        def _(eng):
            held = holder(eng, "act")

            def transposed(k, i, t, first):
                held(s_lnT, k + 1)
                if not first:
                    held(s_xst[t % 2], (k - t % 2) * 8)
                    held(s_lg, k - 1)
                eng.activation(lnT[t % 2], ps_hT[t % 2][:, :], ACT.Copy).then_inc(s_lnTs, 1)

            def first_pair(k2, first):
                for i in range(2):
                    grp = k2 * 2 + i
                    for r in range(2):
                        held(s_var, grp * 2 + (r + 1))
                        eng.activation(sd, ve, ACT.Sqrt).then_inc(s_sd, 1)
                        if not (first and i == 0):
                            for t in (2 * r, 2 * r + 1):
                                transposed((grp - 1) * GT + t, i, t, first and i == 1 and t < 2)

            first_pair(0, True)
            with eng.Fori(1, TILES // (2 * GT)) as k2:
                first_pair(k2, False)
            for t in range(GT):
                transposed(TILES - GT + t, 1, t, False)

            def xi_out(d, ps):
                held(xi_mm, ps + 1)
                held(halo, ps)
                lo = HALO if d == 0 else 0
                eng.activation(xi[:, :, lo:lo + P], ps_x[:, :].rearrange("p (e t) -> p e t", e=ET), ACT.Copy)\
                   .then_inc(xi_sb, 1)

            def conv_now(d, ps):
                held(xi_mm, ps + 1)
                held(yi_mm, ps)
                held(du_done, 2 * ps)
                for e in range(ET):
                    ins = eng.activation(cv[:, e, :], ps_x[:, e * P:(e + 1) * P], ACT.Identity,
                                         bias=cv_b[d][:, e:e + 1], scale=cv_w[d][:, e, HALO:HALO + 1])
                ins.then_inc(tap_now, 1)

            def tanh_conv(ps):
                held(tap, ps * HALO + HALO)
                held(u2_done, ps)
                eng.activation(th[:], cv[:], ACT.Tanh, scale=0.5).then_inc(th_done, 1)

            def proj_out(ps):
                held(proj_mm, ps + 1)
                held(v_mm, ps)
                eng.activation(dtT[0:RANK, :], ps_x[0:RANK, 0:P], ACT.Copy, scale=0.5).then_inc(proj_sb, 1)
                held(bT_out, ps * 16)
                eng.activation(bs[BROW:BROW + NS, :], ps_x[BROW:BROW + NS, 0:P], ACT.Copy, scale=0.25)\
                   .then_inc(proj_sb, 1)
                held(c_mm, ps)
                eng.activation(dcT[:, :], ps_x[0:BROW, 0:P], ACT.Copy, scale=0.5).then_inc(proj_sb, 1)

            def c_out(uu, q, ps, used=None):
                held(c_mm, ps + 1)
                if used is not None:
                    held(stt_done, used)
                eng.activation(c_t[uu % 2][:, bass.ds(pro_tt(uu, q), 1), :].rearrange("p a n -> p (a n)"),
                               ps_x[:, P + RANK:P + BROW], ACT.Copy).then_inc(c_done, 1)

            def softplus_out(ps):
                flat = ps_p[:, :].rearrange("p (e t) -> p e t", e=ET)
                held(v_mm, ps + 1)
                held(d_done, ps)
                eng.activation(sp[:], flat, ACT.Abs).then_inc(sp_step, 1)
                held(sp_step, ps * 3 + 1)
                eng.activation(sp[:], sp[:], ACT.Exp, scale=-1.0).then_inc(sp_step, 1)

            def softplus_log(ps):
                held(sp_step, ps * 3 + 2)
                eng.activation(sp[:], sp[:], ACT.Ln, bias=1.0).then_inc(sp_step, 1)

            def y_init(uu, q, ps, es):
                held(yi_mm, ps + 1)
                if es is not None:
                    held(yg_done, es + 1)
                eng.activation(y[uu % 2][:, bass.ds(pro_tt(uu, q), 1), :].rearrange("p a e -> p (a e)"),
                               ps_p[:, :], ACT.Copy).then_inc(yi_done, 1)

            def tanh_z(es):
                held(z_mm, es + 1)
                held(ygT_mm, es)
                eng.activation(sz[:], ps_e[:, :], ACT.Tanh, scale=0.5).then_inc(tz_done, 1)

            def ygT_out(es):
                held(ygT_mm, es + 1)
                held(o_out, es * 16)
                eng.activation(ygT[:], ps_e[:, :], ACT.Copy, scale=0.5).then_inc(ygT_sb, 1)

            def o_out_sb(es):
                held(o_mm, es + 1)
                eng.activation(o_sbuf, ps_e[:, 0:D], ACT.Copy).then_inc(o_sb, 1)

            def xbT_out(g):
                held(xbT_mm, g + 1)
                held(u_mm, g * 4)
                eng.activation(xbT[:], ps_m[1][:, 0:KD * CH].rearrange("p (k c) -> p k c", k=KD), ACT.Copy)\
                   .then_inc(xbT_sb, 1)

            def tanh_g(g, i):
                held(g_mm, g * 4 + (i + 1))
                if i >= 2 or not (isinstance(g, int) and g == 0):
                    held(hm_done, g * 4 + (i - 1))
                eng.activation(tg[i % 2][:], ps_m[0][:, 0:2 * CH], ACT.Tanh, scale=0.5).then_inc(tg_done, 1)
                eng.activation(gs[i % 2][:], ps_m[0][:, 0:2 * CH], ACT.Copy, scale=0.5).then_inc(gs_done, 1)

            def ybT_out(g):
                held(ybT_mm, g + 1)
                held(ybr_mm, g)
                eng.activation(ybT[:], ps_m[0][:, 0:KD * CH].rearrange("p (k c) -> p k c", k=KD), ACT.Copy)\
                   .then_inc(ybT_sb, 1)

            def ybr_out(g):
                held(ybr_mm, g + 1)
                held(yb_out, g * 16)
                eng.activation(ybr[:], ps_m[1][0:CR, :], ACT.Copy).then_inc(ybr_sb, 1)

            xi_out(0, 0)
            conv_now(0, 0)
            tanh_conv(0)

            eng.wait_ge(s_dif, 1)
            eng.activation(ev[:, 0, :], ev[:, 1, :], ACT.Exp).then_inc(s_exp, 1)
            eng.wait_ge(s_w, 16 * 16)
            for d in range(2):
                eng.activation(negA[d][:], negA[d][:], ACT.Exp).then_inc(s_neg, 1)
            eng.wait_ge(s_neg, 2)
            for d in range(2):
                eng.activation(negA[d][:], negA[d][:], ACT.Copy, scale=-1.0).then_inc(s_neg, 1)
            eng.wait_ge(s_neg, 4)

            for ps in range(TT):
                if ps:
                    conv_now(0, ps)
                    tanh_conv(ps)
                proj_out(ps)
                c_out(0, ps, ps)
                softplus_out(ps)
                softplus_log(ps)
                if ps + 1 < TT:
                    xi_out(0, ps + 1)
                y_init(0, ps, ps, None)

            def iteration(before, now, after):
                if now and isinstance(now.q, int) and now.q == 0:
                    held(d_done, now.g + TT)
                for s in range(STEPS):
                    if now:
                        b, uu, q, g, _, _ = now
                        n, e = s // ET, s % ET
                        if s > 1 or not (isinstance(g, int) and g == 0):
                            held(scan_done, g * 16 + (s - 1))
                        eng.activation(ex[s % 4][:, :], dT[uu % 2][:, e, :], ACT.Exp,
                                       scale=negA[DIR[uu]][:, bass.ds(q * NPI + n, 1), e]).then_inc(a_ready, 1)
                    near = [s, before, now, after]
                    it = due(ACT_AT["slots"], *near)
                    if it:
                        xbT_out(it.g)
                    it = due(ACT_AT["down"], *near)
                    if it:
                        ybT_out(it.g)
                    it = due(ACT_AT["rows"], *near)
                    if it:
                        ybr_out(it.g)
                    for i, step in enumerate(ACT_AT["gate"]):
                        it = due(step, *near)
                        if it:
                            tanh_g(it.g, i)
                    it = due(ACT_AT["y"], *near)
                    if it and it.pro:
                        y_init((it.uu + 1) % UNITS, it.q, it.g + TT, it.g - TT if it.epi else None)
                    it = due(ACT_AT["xi"], *near)
                    if it and it.pro:
                        xi_out(DIR[(it.uu + 1) % UNITS], it.g + TT)
                    it = due(ACT_AT["conv"], *near)
                    if it and it.pro:
                        conv_now(DIR[(it.uu + 1) % UNITS], it.g + TT)
                    it = due(ACT_AT["tanh"], *near)
                    if it and it.pro:
                        tanh_conv(it.g + TT)
                    it = due(ACT_AT["proj"], *near)
                    if it and it.pro:
                        proj_out(it.g + TT)
                    it = due(ACT_AT["c"], *near)
                    if it and it.pro:
                        c_out((it.uu + 1) % UNITS, it.q, it.g + TT, first_g(it.b, it.uu) * NS + STT0)
                    it = due(ACT_AT["softplus"], *near)
                    if it and it.pro:
                        softplus_out(it.g + TT)
                    it = due(ACT_AT["log"], *near)
                    if it and it.pro:
                        softplus_log(it.g + TT)
                    it = due(ACT_AT["z"], *near)
                    if it and it.epi:
                        tanh_z(it.g - TT)
                    it = due(ACT_AT["turn"], *near)
                    if it and it.epi:
                        ygT_out(it.g - TT)
                    it = due(ACT_AT["out"], *near)
                    if it and it.epi:
                        o_out_sb(it.g - TT)

            run(eng, iteration)

            for q in range(TT):
                held(z_mm, ITERS - TT + q + 1)
                eng.activation(end_sz[q], end_bank[q][:, :], ACT.Tanh, scale=0.5).then_inc(tz_done, 1)
            for q in range(TT):
                held(ygT_mm, ITERS - TT + q + 1)
                eng.activation(end_ygT[q], end_bank[q][:, :], ACT.Copy, scale=0.5).then_inc(ygT_sb, 1)
            for q in range(TT):
                held(o_mm, ITERS - TT + q + 1)
                if q == 0:
                    eng.wait_ge(xne_in, 16 * ITERS)
                eng.activation(end_o[q], end_bank[q][:, 0:D], ACT.Copy).then_inc(o_sb, 1)
                held(o_sb, ITERS - TT + q + 1)
                eng.dma_start(yd_d[DIR[UNITS - 1]][token_tile(BATCH - 1, UNITS - 1, epi_tt(UNITS - 1, q))],
                              end_o[q]).then_inc(o_out, 16)

        @block.tensor
        def _(eng):
            held = holder(eng, "pe")
            eng.wait_ge(s_const, 16 * 5)

            def first_pair(k2, first):
                for i in range(2):
                    grp = k2 * 2 + i
                    eng.wait_ge(s_xf, grp + 1)
                    for t in range(GT):
                        k = grp * GT + t
                        if not (first and i == 0 and t < 2):
                            eng.wait_ge(s_lnTs, k - 1)
                        for j, src in enumerate((xg[i], xfg[i])):
                            for c in range(KD):
                                o = (j * KD + c) * P
                                ins = eng.transpose(ps_hT[t % 2][:, o:o + P], src[:, t, c * P:(c + 1) * P], ident)
                        ins.then_inc(s_lnT, 1)
                        if not (first and i == 0 and t == 0):
                            logits(grp * GT + (t - 1), (t + 1) % 2)

            def logits(k, par):
                eng.wait_ge(s_lnTs, k + 1)
                for c in range(KD):
                    ins = eng.matmul(ps_m[0][:, bass.ds(k * EX, EX)], lnT[par][:, D + c * P:D + (c + 1) * P],
                                     rt[:, c, :], start=(c == 0), stop=(c == KD - 1))
                ins.then_inc(s_lg, 1)

            first_pair(0, True)
            with eng.Fori(1, TILES // (2 * GT)) as k2:
                first_pair(k2, False)
            def xi_in(d, ps):
                eng.wait_ge(xnp_in, ps * 16 + 16)
                eng.wait_ge(c_done, ps)
                for e in range(ET):
                    for k in range(KD):
                        ins = eng.matmul(ps_x[:, e * P:(e + 1) * P], in_w[d][:, k, e * P:(e + 1) * P],
                                         xnP[:, k, :], start=(k == 0), stop=(k == KD - 1))
                ins.then_inc(xi_mm, 1)

            def proj(d, ps):
                eng.wait_ge(u2_done, ps + 1)
                eng.wait_ge(xi_sb, ps + 1)
                for e in range(ET):
                    ins = eng.matmul(ps_x[0:BROW + NS, 0:P], xp_w[d][:, e, :], u2[:, e, :],
                                     start=(e == 0), stop=(e == ET - 1))
                ins.then_inc(proj_mm, 1)

            def v_in(d, ps):
                eng.wait_ge(proj_sb, ps * 3 + 3)
                eng.wait_ge(yi_done, ps)
                for e in range(ET):
                    ins = eng.matmul(ps_p[:, e * P:(e + 1) * P], dt_w[d][:, e * P:(e + 1) * P],
                                     dtT[0:RANK + 1, :], start=True, stop=True)
                ins.then_inc(v_mm, 1)

            def c_turn(ps):
                held(proj_sb, ps * 3 + 3)
                eng.transpose(ps_x[:, P:P + BROW], dcT[:, :], ident[0:BROW, 0:BROW]).then_inc(c_mm, 1)

            def y_start(d, ps):
                eng.wait_ge(d_done, ps + 1)
                for e in range(ET):
                    ins = eng.matmul(ps_p[:, e * P:(e + 1) * P], u2[:, e, :], diag[d][:, e, :],
                                     start=True, stop=True)
                ins.then_inc(yi_mm, 1)

            def z_in(d, es):
                eng.wait_ge(xne_in, es * 16 + 16)
                eng.wait_ge(o_sb, es)
                for k in range(KD):
                    ins = eng.matmul(ps_e[:, :], xnE[:, k, :], in_w[d][:, k, E:2 * E],
                                     start=(k == 0), stop=(k == KD - 1))
                ins.then_inc(z_mm, 1)

            def yg_turn(es):
                eng.wait_ge(sz_done, es + 1)
                eng.wait_ge(yg_done, es + 1)
                for e in range(ET):
                    ins = eng.transpose(ps_e[:, e * P:(e + 1) * P], yg[:, e * P:(e + 1) * P], ident)
                ins.then_inc(ygT_mm, 1)

            def out_proj(d, es, i):
                if i == 0:
                    eng.wait_ge(ygT_sb, es + 1)
                for e in (2 * i, 2 * i + 1):
                    ins = eng.matmul(ps_e[:, 0:D], ygT[:, e * P:(e + 1) * P], out_w[d][:, e, :],
                                     start=(e == 0), stop=(e == ET - 1))
                if i == 1:
                    ins.then_inc(o_mm, 1)

            def slots_turn(g):
                eng.wait_ge(xb_in, g * 16 + 16)
                eng.wait_ge(tu_done, g * 4)
                for k in range(KD):
                    for j in range(2):
                        o = k * CH + j * CR
                        ins = eng.transpose(ps_m[1][:, o:o + CR], xbr[:, j, k * P:(k + 1) * P], ident[0:CR, 0:CR])
                ins.then_inc(xbT_mm, 1)

            def gate_or_up(w, g, i, up):
                eng.wait_ge(xbT_sb, g + 1)
                if not up:
                    eng.wait_ge(gs_done, g * 4 + i)
                    if i == 0:
                        eng.wait_ge(ybT_sb, g)
                else:
                    eng.wait_ge(tu_done, g * 4 + i)
                    if i == 0:
                        eng.wait_ge(ybr_sb, g)
                for f in range(2):
                    c0 = up * FF + (2 * i + f) * P
                    for k in range(KD):
                        ins = eng.matmul(ps_m[up][:, f * CH:(f + 1) * CH], w12[w][:, k, c0:c0 + P],
                                         xbT[:, k, :], start=(k == 0), stop=(k == KD - 1))
                ins.then_inc(u_mm if up else g_mm, 1)

            def down(w, g, i):
                k = i // 2
                if i == 0:
                    eng.wait_ge(gs_done, g * 4 + 4)
                if i < 2:
                    eng.wait_ge(hm_done, g * 4 + (2 * i + 2))
                for f in range(i % 2 * (FB // 2), (i % 2 + 1) * (FB // 2)):
                    ins = eng.matmul(ps_m[0][:, k * CH:(k + 1) * CH], w3[w][:, f, k * P:(k + 1) * P],
                                     hm[:, f, :], start=(f == 0), stop=(f == FB - 1))
                if i == 3:
                    ins.then_inc(ybT_mm, 1)

            def rows_turn(g):
                eng.wait_ge(ybT_sb, g + 1)
                eng.wait_ge(xbT_sb, min(g + 2, ITERS) if isinstance(g, int) else g + 2)
                for j in range(2):
                    for k in range(KD):
                        o = j * D + k * P
                        ins = eng.transpose(ps_m[1][0:CR, o:o + P], ybT[:, k, j * CR:(j + 1) * CR], ident)
                ins.then_inc(ybr_mm, 1)

            logits(TILES - 1, 1)
            eng.wait_ge(s_w, 16 * 16)
            xi_in(0, 0)

            eng.wait_ge(s_places, 1)
            eng.wait_ge(s_mem, 2)
            flat = both.rearrange("p t e -> p (t e)")
            eng.matmul(ps_m[1][:, 0:TILES * EX], below, flat, start=True, stop=True)
            eng.matmul(ps_p[:, 0:TILES * EX], ones, flat, start=True, stop=True).then_inc(s_cum, 1)
            eng.wait_ge(s_diag, 1)

            for ps in range(TT):
                proj(0, ps)
                v_in(0, ps)
                c_turn(ps)
                if ps + 1 < TT:
                    xi_in(0, ps + 1)
                y_start(0, ps)

            eng.sem_inc(ht_ready, HT0)

            def turn_states(g, n, tt):
                if tt == 0:
                    eng.wait_ge(scan_done, g * 16 + (4 * n + 4 + SCAN0))
                eng.wait_ge(stt_done, g * 16 + (4 * n + tt + STT0 - 1))
                for e in range(ET):
                    ins = eng.transpose(ps_hT[tt % 2][:, e * P:(e + 1) * P], h[n % 2][:, e, tt * P:(tt + 1) * P], ident)
                ins.then_inc(ht_ready, 1)

            def iteration(before, now, after):
                if now and now.uu % 2 == 0 and isinstance(now.q, int) and now.q == 0:
                    held(w_in[now.uu // 2], now.b * (32 * FB) + 32 * FB)
                for s in range(STEPS):
                    it = before if s < ET else now
                    if it:
                        turn_states(it.g, (s // ET - 1) % NPI, s % ET)
                    near = [s, before, now, after]
                    it = due(PE_AT["slots"], *near)
                    if it:
                        slots_turn(it.g)
                    for i, step in enumerate(PE_AT["down"]):
                        it = due(step, *near)
                        if it:
                            down(it.uu // 2, it.g, i)
                    it = due(PE_AT["rows"], *near)
                    if it:
                        rows_turn(it.g)
                    it = due(PE_AT["z"], *near)
                    if it and it.epi:
                        z_in(DIR[(it.uu - 1) % UNITS], it.g - TT)
                    it = due(PE_AT["turn"], *near)
                    if it and it.epi:
                        yg_turn(it.g - TT)
                    for i, step in enumerate(PE_AT["out"]):
                        it = due(step, *near)
                        if it and it.epi:
                            out_proj(DIR[(it.uu - 1) % UNITS], it.g - TT, i)
                    for up, name in enumerate(("gate", "up")):
                        for i, step in enumerate(PE_AT[name]):
                            it = due(step, *near)
                            if it:
                                gate_or_up(it.uu // 2, it.g, i, up)
                    it = due(PE_AT["proj"], *near)
                    if it and it.pro:
                        proj(DIR[(it.uu + 1) % UNITS], it.g + TT)
                    it = due(PE_AT["v"], *near)
                    if it and it.pro:
                        v_in(DIR[(it.uu + 1) % UNITS], it.g + TT)
                    it = due(PE_AT["c"], *near)
                    if it and it.pro:
                        c_turn(it.g + TT)
                    it = due(PE_AT["y"], *near)
                    if it and it.pro:
                        y_start(DIR[(it.uu + 1) % UNITS], it.g + TT)
                    it = due(PE_AT["xi"], *near)
                    if it and it.pro:
                        xi_in(DIR[(it.uu + 1) % UNITS], it.g + TT)

            run(eng, iteration)

            d = DIR[UNITS - 1]
            eng.wait_ge(xne_in, 16 * ITERS)
            eng.wait_ge(o_sb, ITERS - TT)
            eng.wait_ge(yi_done, ITERS)
            eng.wait_ge(c_done, ITERS)
            eng.wait_ge(scan_done, ITERS * NPI * ET + SCAN0)
            for q in range(TT):
                for k in range(KD):
                    ins = eng.matmul(end_bank[q][:, :], end_xn[q][:, k, :], in_w[d][:, k, E:2 * E],
                                     start=(k == 0), stop=(k == KD - 1))
                ins.then_inc(z_mm, 1)
            for q in range(TT):
                eng.wait_ge(sz_done, ITERS - TT + q + 1)
                eng.wait_ge(yg_done, ITERS - TT + q + 1)
                for e in range(ET):
                    ins = eng.transpose(end_bank[q][:, e * P:(e + 1) * P], end_sz[q][:, e * P:(e + 1) * P], ident)
                ins.then_inc(ygT_mm, 1)
            for q in range(TT):
                eng.wait_ge(ygT_sb, ITERS - TT + q + 1)
                for e in range(ET):
                    ins = eng.matmul(end_bank[q][:, 0:D], end_ygT[q][:, e * P:(e + 1) * P], out_w[d][:, e, :],
                                     start=(e == 0), stop=(e == ET - 1))
                ins.then_inc(o_mm, 1)

        @block.vector
        def _(eng):
            held = holder(eng, "dve")
            eng.wait_ge(s_const, 16 * 5)

            def stepper(base):
                count = [0]

                def step(ins):
                    ins.then_inc(s_step, 1)
                    count[0] += 1
                    eng.wait_ge(s_step, base + count[0])
                return step, count

            LN_STEPS = 15

            def inverse_root(src, r, grp, step):
                for t in range(GT):
                    ins = eng.bn_stats(st6[:, t, :], src[:, t, :])
                step(ins)
                eng.sem_inc(gates["dve"], 1)
                for t in range(GT):
                    ins = eng.bn_aggr(mv[:, t, :], st6[:, t, :])
                step(ins)
                eng.tensor_scalar(ve, mv[:, :, 1], EPS, None, ALU.add).then_inc(s_var, 1)
                eng.wait_ge(s_sd, grp * 2 + (r + 1))
                step(eng.reciprocal(rs, sd))
                step(eng.tensor_tensor(nt, rs, rs, ALU.mult))
                step(eng.tensor_tensor(nt, nt, ve, ALU.mult))
                step(eng.tensor_scalar(nt, nt, -0.5, 1.5, ALU.mult, ALU.add))
                step(eng.tensor_tensor(rs, rs, nt, ALU.mult))

            def first_pair(k2, first):
                for i in range(2):
                    grp = k2 * 2 + i
                    step, count = stepper(grp * LN_STEPS)
                    eng.wait_ge(s_x[i], k2 * 16 + 16)
                    inverse_root(xg[i], 0, grp, step)
                    for t in range(GT):
                        ins = eng.tensor_scalar(xg[i][:, t, :], xg[i][:, t, :], mv[:, t, 0:1], rs[:, t:t + 1],
                                                ALU.subtract, ALU.mult)
                    step(ins)
                    inverse_root(xg[i], 1, grp, step)
                    assert count[0] == LN_STEPS
                    if not first:
                        eng.wait_ge(s_xfc, grp - 1)
                    for t in range(GT):
                        ins = eng.scalar_tensor_tensor(out=xfg[i][:, t, :], in0=xg[i][:, t, :],
                                                       scalar=mv[:, t, 0:1], in1=gam, op0=ALU.subtract,
                                                       op1=ALU.mult)
                    ins.then_inc(s_scaled, 1)
                    eng.wait_ge(s_scaled, grp + 1)
                    for t in range(GT):
                        ins = eng.scalar_tensor_tensor(out=xfg[i][:, t, :], in0=xfg[i][:, t, :],
                                                       scalar=rs[:, t:t + 1], in1=bet, op0=ALU.mult,
                                                       op1=ALU.add)
                    ins.then_inc(s_xf, 1)

            GROUPS = TILES // GT
            first_pair(0, True)
            with eng.Fori(1, GROUPS // 2) as k2:
                first_pair(k2, False)

            def conv_tap(d, k, ps, starts):
                if k == 0:
                    eng.wait_ge(tap_now, ps + 1)
                    eng.wait_ge(xi_sb, ps + 1)
                    eng.wait_ge(halo, ps)
                    eng.wait_ge(halo0, starts)
                else:
                    eng.wait_ge(tap, ps * HALO + k)
                off = k if d == 0 else HALO - k
                for e in range(ET):
                    ins = eng.scalar_tensor_tensor(out=cv[:, e, :], in0=xi[:, e, off:off + P],
                                                   scalar=cv_w[d][:, e, k:k + 1], in1=cv[:, e, :],
                                                   op0=ALU.mult, op1=ALU.add)
                ins.then_inc(tap, 1)

            def make_u2(ps):
                eng.wait_ge(th_done, ps + 1)
                eng.scalar_tensor_tensor(out=u2[:], in0=th[:], scalar=1.0, in1=cv[:], op0=ALU.add,
                                         op1=ALU.mult).then_inc(u2_done, 1)

            def delta(uu, q, ps):
                held(sp_step, ps * 3 + 3)
                if isinstance(ps, int) and ps == TT:
                    for part in range(SCATTERS):
                        eng.wait_ge(s_scat[part], SCATTERED)
                tt = pro_tt(uu, q)
                eng.scalar_tensor_tensor(out=dT[uu % 2][:, :, bass.ds(tt * P, P)],
                                         in0=ps_p[:, :].rearrange("p (e t) -> p e t", e=ET), scalar=0.0,
                                         in1=sp[:], op0=ALU.max, op1=ALU.add).then_inc(d_done, 1)

            def silu_z(es):
                eng.wait_ge(tz_done, es + 1)
                eng.scalar_tensor_tensor(out=sz[:], in0=sz[:], scalar=1.0, in1=ps_e[:, :], op0=ALU.add,
                                         op1=ALU.mult).then_inc(sz_done, 1)

            def times_up(g, i):
                eng.wait_ge(tg_done, g * 4 + (i + 1))
                eng.wait_ge(u_mm, g * 4 + (i + 1))
                eng.scalar_tensor_tensor(out=tu[i % 2][:], in0=tg[i % 2][:], scalar=1.0, in1=ps_m[1][:, 0:2 * CH],
                                         op0=ALU.add, op1=ALU.mult).then_inc(tu_done, 1)

            def convolve(ps):
                for k in range(HALO):
                    conv_tap(0, k, ps, 1)
                eng.wait_ge(tap, ps * HALO + HALO)
                eng.tensor_copy(xi[:, :, 0:HALO], xi[:, :, P:P + HALO]).then_inc(halo, 1)

            eng.wait_ge(s_w, 16 * 16)
            convolve(0)

            step, _ = stepper(GROUPS * LN_STEPS)
            eng.wait_ge(s_lg, TILES)
            step(eng.tensor_scalar(lg.rearrange("p t e -> p (t e)"), ps_m[0][:, 0:TILES * EX], CLAMP, -CLAMP,
                                   ALU.min, ALU.max))
            for t in range(TILES):
                ins = eng.max(out=m8[:, t, :], in_=lg[:, t, :])
            step(ins)
            i8u = i8.bitcast(U32)
            for t in range(TILES):
                ins = eng.max_index(out=i8u[:, t, :], in_max=m8[:, t, :], in_values=lg[:, t, :])
            step(ins)
            for k in range(2):
                step(eng.tensor_copy(ixf[:, k, :], i8u[:, :, k]))
            iota = iota8.rearrange("p (a e) -> p a e", a=1).broadcast_to([P, TILES, EX])
            for k in range(2):
                one = ixf[:, k, :].rearrange("p (t a) -> p t a", a=1).broadcast_to([P, TILES, EX])
                step(eng.tensor_tensor(oh[k], iota, one, ALU.is_equal))
            eng.tensor_tensor(both, oh[0], oh[1], ALU.add).then_inc(s_places, 1)
            step(eng.tensor_tensor(ev[:, 1, :], m8[:, :, 1], m8[:, :, 0], ALU.subtract))
            eng.nop().then_inc(s_dif, 1)
            make_u2(0)
            eng.wait_ge(s_cum, 1)
            step(eng.tensor_copy(tot.rearrange("p t e -> p (t e)"), ps_p[:, 0:TILES * EX]))
            for e in range(EX):
                ins = eng.tensor_tensor_scan(pos[:, :, e], ones[:, 0:TILES], tot[:, :, e], 0.0, ALU.mult, ALU.add)
            step(ins)
            step(eng.tensor_tensor(pos, pos, tot, ALU.subtract))
            step(eng.tensor_tensor(pos, pos, ps_m[1][:, 0:TILES * EX].rearrange("p (t e) -> p t e", t=TILES), ALU.add))
            for k in range(2):
                step(eng.tensor_tensor(prod, pos, oh[k], ALU.mult))
                step(eng.tensor_reduce(slf[:, k, :], prod, AX_X, ALU.add))
            step(eng.tensor_scalar(kp, slf, float(CAP), None, ALU.is_lt))
            step(eng.scalar_tensor_tensor(out=slf, in0=ixf, scalar=float(CAP), in1=slf, op0=ALU.mult, op1=ALU.add))
            step(eng.tensor_scalar(slot_ga[:], slf, float(SLOTS - 1), None, ALU.min))
            step(eng.tensor_scalar(ixf, kp, -2.0 * SLOTS, 2.0 * SLOTS, ALU.mult, ALU.add))
            eng.tensor_tensor(slot_sc[:], slf, ixf, ALU.add).then_inc(s_slot, 1)
            eng.wait_ge(s_exp, 1)
            step(eng.tensor_scalar(rsum, ev[:, 0, :], 1.0, 1e-12, ALU.add, ALU.add))
            step(eng.reciprocal(rsum, rsum))
            step(eng.tensor_tensor(ev[:, 1, :], ev[:, 0, :], rsum, ALU.mult))
            step(eng.tensor_tensor(gate_w[:, 0, :], rsum, kp[:, 0, :], ALU.mult))
            step(eng.tensor_tensor(gate_w[:, 1, :], ev[:, 1, :], kp[:, 1, :], ALU.mult))
            eng.wait_ge(s_w, 16 * 16)
            for d in range(2):
                for e in range(ET):
                    ins = eng.tensor_scalar(diag[d][:, e, :], ident, dp[d][:, e:e + 1], 0.5, ALU.mult, ALU.mult)
            ins.then_inc(s_diag, 1)

            for ps in range(TT):
                if ps:
                    convolve(ps)
                    make_u2(ps)
                delta(0, ps, ps)
                eng.wait_ge(d_done, ps + 1)
                eng.wait_ge(u2_done, ps + 1)
                eng.wait_ge(s_zfill, 16 * (SLOTS // (P * ZR)))
                eng.tensor_tensor(duT[0][:, :, ps * P:(ps + 1) * P], dT[0][:, :, ps * P:(ps + 1) * P], u2[:], ALU.mult)\
                   .then_inc(du_done, 2)
            eng.wait_ge(s_xfc, TILES // GT)
            eng.sem_inc(scan_done, SCAN0)
            eng.sem_inc(stt_done, STT0)

            def scan(it, n, e):
                s = n * ET + e
                flip = slice(None) if DIR[it.uu] == 0 else slice(None, None, -1)
                eng.wait_ge(a_ready, it.g * 16 + (s + 1))
                if s % 2 == 0:
                    eng.wait_ge(b_ready, it.g * 8 + (s // 2 + 1))
                if e == 0:
                    eng.wait_ge(ht_ready, it.g * 16 + 4 * n)
                    if n or not (isinstance(it.g, int) and it.g == 0):
                        eng.wait_ge(saved, it.g * 4 + (n - 1))
                init = state[:, bass.ds(it.q * NPI + n, 1), e] if it.uu % 2 == 1 else 0.0
                eng.tensor_tensor_scan(h[n % 2][:, e, flip], ex[s % 4][:, flip],
                                       bm[s // 2 % 2][:, e % 2, flip], init, ALU.mult, ALU.add)\
                   .then_inc(scan_done, 1)

            def add_state(it, n, tt):
                k = n * TT + tt
                par = it.uu % 2
                if k == 0 and isinstance(it.q, int) and it.q == 0:
                    eng.wait_ge(yi_done, it.g + TT)
                    held(c_done, it.g + TT)
                eng.wait_ge(ht_ready, it.g * 16 + (k + 1 + HT0))
                eng.wait_ge(stt_done, it.g * 16 + (k + 1))
                eng.scalar_tensor_tensor(out=y[par][:, tt, :], in0=ps_hT[tt % 2][:, :],
                                         scalar=c_t[par][:, tt, bass.ds(it.q * NPI + n, 1)],
                                         in1=y[par][:, tt, :], op0=ALU.mult, op1=ALU.add)\
                   .then_inc(stt_done, 1)

            def iteration(before, now, after):
                for s in range(STEPS):
                    if now:
                        scan(now, s // ET, s % ET)
                    it = before if s < ET else now
                    if it:
                        add_state(it, (s // ET - 1) % NPI, s % ET)
                    near = [s, before, now, after]
                    for tap_at, step in enumerate(DVE_AT["taps"]):
                        it = due(step, *near)
                        if it and it.pro:
                            starts = it.b * 2 + ((it.uu + 1) // 2 + 1)
                            conv_tap(DIR[(it.uu + 1) % UNITS], tap_at, it.g + TT, starts)
                    it = due(DVE_AT["u2"], *near)
                    if it and it.pro:
                        make_u2(it.g + TT)
                    it = due(DVE_AT["z"], *near)
                    if it and it.epi:
                        silu_z(it.g - TT)
                    for i, step in enumerate(DVE_AT["up"]):
                        it = due(step, *near)
                        if it:
                            times_up(it.g, i)
                    it = due(DVE_AT["delta"], *near)
                    if it and it.pro:
                        delta((it.uu + 1) % UNITS, it.q, it.g + TT)

            run(eng, iteration)

            for q in range(TT):
                eng.wait_ge(tz_done, ITERS - TT + q + 1)
                eng.scalar_tensor_tensor(out=end_sz[q], in0=end_sz[q], scalar=1.0, in1=end_bank[q][:, :], op0=ALU.add,
                                         op1=ALU.mult).then_inc(sz_done, 1)

            def last_ring(k, first):
                for i in range(RING):
                    t = k * RING + i
                    eng.wait_ge(f_in[i], k * 48 + 48)
                    if not first:
                        eng.wait_ge(f_out[i], k * 16)
                    eng.tensor_tensor(fo[i], fin[i][1], fin[i][2], ALU.add).then_inc(f_dve, 1)
                    eng.wait_ge(f_dve, t * 4 + 1)
                    eng.tensor_tensor(fo[i], fo[i], fin[i][0], ALU.add).then_inc(f_dve, 1)
                    eng.wait_ge(f_ga[i], k * 32 + 32)
                    for j in range(2):
                        eng.wait_ge(f_dve, t * 4 + (j + 2))
                        eng.scalar_tensor_tensor(out=fo[i], in0=fga[i][j], scalar=gate_w[:, j, bass.ds(t, 1)],
                                                 in1=fo[i], op0=ALU.mult, op1=ALU.add).then_inc(f_dve, 1)

            last_ring(0, True)
            with eng.Fori(1, TILES // RING) as k:
                last_ring(k, False)


_MAMBA = ("in_w", "conv_w", "conv_b", "xproj", "dt_w", "A_log", "Dp", "out_w")


def _laid_out(inputs):
    def rows(a):
        return np.ascontiguousarray(a.reshape(ET, P, -1).transpose(1, 0, 2))

    pre = {k: np.asarray(v) for k, v in inputs.items()}
    got = {
        "x": pre["L0_attn_x"].reshape(TILES, P, D),
        "ln_g": pre["L0_ffn_ln_gamma"],
        "ln_b": pre["L0_ffn_ln_beta"],
        "routerT": pre["L0_ffn_router_w"].T,
        "w12T": pre["L0_ffn_w12"].transpose(0, 2, 1),
        "w3T": pre["L0_ffn_w3"].transpose(0, 2, 1),
        "const": np.concatenate([np.eye(P), np.tile(np.arange(EX), (P, 1)), np.triu(np.ones((P, P)), 1)], 1)
                   .astype(np.float32),
    }
    for side, name in enumerate(("fwd", "bwd")):
        w = {k: pre[f"L0_attn_{name}_{k}"] for k in
             ("in_w", "conv_w", "conv_b", "xproj_w", "dt_w", "dt_b", "A_log", "Dp", "out_w")}
        parts = {
            "in_w": w["in_w"],
            "conv_w": rows(w["conv_w"]),
            "conv_b": rows(w["conv_b"])[:, :, 0],
            "xproj": np.concatenate([w["xproj_w"][:, :RANK], w["xproj_w"][:, RANK + NS:],
                                     w["xproj_w"][:, RANK:RANK + NS]], 1),
            "dt_w": np.concatenate([w["dt_w"], w["dt_b"][None, :]], 0),
            "A_log": rows(w["A_log"]).transpose(0, 2, 1),
            "Dp": rows(w["Dp"])[:, :, 0],
            "out_w": w["out_w"],
        }
        for k in _MAMBA:
            got[f"{k}{side}"] = parts[k]
    return {k: np.ascontiguousarray(v) for k, v in got.items()}


def kernel(**inputs):
    import concourse.bacc as _bacc
    from concourse.bass_utils import run_bass_kernel_spmd as _run

    nc = _bacc.Bacc("TRN2", target_bir_lowering=False, num_devices=1)
    arrays, aps = {}, {}
    for name, a in _laid_out(inputs).items():
        arrays[f"in_{name}"] = a
        aps[name] = nc.dram_tensor(f"in_{name}", a.shape, mybir.dt.from_np(a.dtype), kind="ExternalInput").ap()
    out = nc.dram_tensor("out_0", (TILES, P, D), F32, kind="ExternalOutput").ap()
    mamba = [{k: aps[f"{k}{d}"] for k in _MAMBA} for d in range(2)]
    mixed_block(nc, aps["x"], aps["ln_g"], aps["ln_b"], aps["routerT"], aps["w12T"], aps["w3T"], mamba,
                aps["const"], out)
    r = _run(nc, [arrays], core_ids=[0])
    return r.results[0]["out_0"].reshape(BATCH, L, D)
```
